# Optimizing a Trainium2 kernel written in Bass

```python
import numpy as np
import jax
import jax.numpy as jnp

def _softmax(x, axis=-1):
    return jax.nn.softmax(x, axis=axis)

def _gelu(x):
    return jax.nn.gelu(x, approximate=True)

def _silu(x):
    return jax.nn.silu(x)

def _sigmoid(x):
    return jax.nn.sigmoid(x)

def _layernorm(x, axis=-1, eps=1e-05):
    m = jnp.mean(x, axis=axis, keepdims=True)
    v = jnp.var(x, axis=axis, keepdims=True)
    return (x - m) / jnp.sqrt(v + eps)

def _scatter_add(tgt, idx, src, axis=0):
    return tgt.at[idx].add(src)

def _segment_sum(src, seg, n):
    return jax.ops.segment_sum(src, seg, n)
kernel_name = 'mk_xattn_seq_d1_seqx_r8_fe7c05'

def setup_inputs(seed: int=0):
    np.random.seed(seed)
    _w = jnp.asarray

    def _rec_inputs():
        import jax
        import jax.numpy as jnp
        _rk = jax.random.key(seed)
        x = -0.0002928 + 1 * jax.random.normal(jax.random.fold_in(_rk, 1), (16, 128, 128), jnp.float32)
        _lenS = 128 - jax.random.randint(jax.random.fold_in(_rk, 7), (16,), 0, max(1, 128 // 4) + 1, jnp.int32)
        _lenS2 = 77 - jax.random.randint(jax.random.fold_in(_rk, 8), (16,), 0, max(1, 77 // 4) + 1, jnp.int32)
        _ctx_1024P = jax.random.normal(jax.random.fold_in(_rk, 11), (16, 16, 128), jnp.float32)
        _ctx_1024c = jax.random.dirichlet(jax.random.fold_in(_rk, 511), 0.3 * jnp.ones((16,), jnp.float32), (16, 77))
        _ctx_1024t = jnp.einsum('bsk,bkd->bsd', _ctx_1024c, _ctx_1024P)
        _ctx_1024t = _ctx_1024t * jax.lax.rsqrt(jnp.mean(jnp.square(_ctx_1024t)) + 1e-12) * 0.953939
        ctx_1024 = -1.39393e-06 + 0.999914 * (_ctx_1024t + 0.3 * jax.random.normal(jax.random.fold_in(_rk, 611), (16, 77, 128), jnp.float32))
        return (x, ctx_1024)
    x, ctx_1024 = _rec_inputs()

    def _L0_xattn_setup():
        import jax, jax.numpy as jnp
        import numpy as np
        B, S, SE, D, H, FF, E, K = (2, 256, 256, 128, 16, 512, 8, 2)
        HD = D // H

        def _layernorm(x, g, b):
            m = x.mean(-1, keepdims=True)
            v = ((x - m) ** 2).mean(-1, keepdims=True)
            return (x - m) / jnp.sqrt(v + 1e-05) * g + b

        def _attn(q_in, k_in, v_in, wq, bq, wk, bk, wv, bv, wo, bo, causal):
            Bq, Sq, Dm = q_in.shape
            Sk = k_in.shape[1]
            Q = (q_in @ wq + bq).reshape(Bq, Sq, H, HD)
            Kp = (k_in @ wk + bk).reshape(Bq, Sk, H, HD)
            V = (v_in @ wv + bv).reshape(Bq, Sk, H, HD)
            scores = jnp.einsum('bqhd,bkhd->bhqk', Q, Kp) / jnp.sqrt(jnp.float32(HD))
            if causal:
                mask = jnp.tril(jnp.ones((Sq, Sk), bool))
                scores = jnp.where(mask, scores, -jnp.inf)
            a = jax.nn.softmax(scores, axis=-1)
            o = jnp.einsum('bhqk,bkhd->bqhd', a, V).reshape(Bq, Sq, Dm)
            return o @ wo + bo

        def _moe(x, rw, rb, w1, b1, w2, b2):
            T = x.shape[0] * x.shape[1]
            xf = x.reshape(T, D)
            router_weights = jax.nn.softmax(xf @ rw + rb, axis=-1)
            topw, topi = jax.lax.top_k(router_weights, K)
            topw = jax.nn.softmax(topw, axis=-1)
            combine = jnp.zeros((T, E), xf.dtype).at[jnp.arange(T)[:, None], topi].add(topw)
            h = jax.nn.gelu(jnp.einsum('td,edf->etf', xf, w1) + b1[:, None, :], approximate=False)
            eo = jnp.einsum('etf,efd->etd', h, w2) + b2[:, None, :]
            out = jnp.einsum('etd,te->td', eo, combine)
            return out.reshape(x.shape)
        key = jax.random.key(seed)
        ks = jax.random.split(key, 32)
        w = lambda k, shape: jax.random.normal(k, shape, jnp.float32) * 0.02
        inp = {'x': jax.random.normal(ks[0], (B, S, D), jnp.float32), 'encoder_output': jax.random.normal(ks[1], (B, SE, D), jnp.float32), 'sa_wq': w(ks[2], (D, D)), 'sa_bq': jnp.zeros((D,), jnp.float32), 'sa_wk': w(ks[3], (D, D)), 'sa_bk': jnp.zeros((D,), jnp.float32), 'sa_wv': w(ks[4], (D, D)), 'sa_bv': jnp.zeros((D,), jnp.float32), 'sa_wo': w(ks[5], (D, D)), 'sa_bo': jnp.zeros((D,), jnp.float32), 'ca_wq': w(ks[6], (D, D)), 'ca_bq': jnp.zeros((D,), jnp.float32), 'ca_wk': w(ks[7], (D, D)), 'ca_bk': jnp.zeros((D,), jnp.float32), 'ca_wv': w(ks[8], (D, D)), 'ca_bv': jnp.zeros((D,), jnp.float32), 'ca_wo': w(ks[9], (D, D)), 'ca_bo': jnp.zeros((D,), jnp.float32), 'ln1_g': jnp.ones((D,), jnp.float32), 'ln1_b': jnp.zeros((D,), jnp.float32), 'ln2_g': jnp.ones((D,), jnp.float32), 'ln2_b': jnp.zeros((D,), jnp.float32), 'ln3_g': jnp.ones((D,), jnp.float32), 'ln3_b': jnp.zeros((D,), jnp.float32), 'router_w': w(ks[10], (D, E)), 'router_b': jnp.zeros((E,), jnp.float32), 'e_w1': w(ks[11], (E, D, FF)), 'e_b1': jnp.zeros((E, FF), jnp.float32), 'e_w2': w(ks[12], (E, FF, D)), 'e_b2': jnp.zeros((E, D), jnp.float32)}
        return inp
    _L0_xattn_all = _L0_xattn_setup()
    _L0_xattn_in = {k: v for k, v in _L0_xattn_all.items() if k in ('sa_wq', 'sa_bq', 'sa_wk', 'sa_bk', 'sa_wv', 'sa_bv', 'sa_wo', 'sa_bo', 'ca_wq', 'ca_bq', 'ca_wk', 'ca_bk', 'ca_wv', 'ca_bv', 'ca_wo', 'ca_bo', 'ln1_g', 'ln1_b', 'ln2_g', 'ln2_b', 'ln3_g', 'ln3_b', 'router_w', 'router_b', 'e_w1', 'e_b1', 'e_w2', 'e_b2')}
    del _L0_xattn_all
    return {'x': x, 'ctx_1024': ctx_1024, 'L0_xattn_sa_wq': _L0_xattn_in['sa_wq'], 'L0_xattn_sa_bq': _L0_xattn_in['sa_bq'], 'L0_xattn_sa_wk': _L0_xattn_in['sa_wk'], 'L0_xattn_sa_bk': _L0_xattn_in['sa_bk'], 'L0_xattn_sa_wv': _L0_xattn_in['sa_wv'], 'L0_xattn_sa_bv': _L0_xattn_in['sa_bv'], 'L0_xattn_sa_wo': _L0_xattn_in['sa_wo'], 'L0_xattn_sa_bo': _L0_xattn_in['sa_bo'], 'L0_xattn_ca_wq': _L0_xattn_in['ca_wq'], 'L0_xattn_ca_bq': _L0_xattn_in['ca_bq'], 'L0_xattn_ca_wk': _L0_xattn_in['ca_wk'], 'L0_xattn_ca_bk': _L0_xattn_in['ca_bk'], 'L0_xattn_ca_wv': _L0_xattn_in['ca_wv'], 'L0_xattn_ca_bv': _L0_xattn_in['ca_bv'], 'L0_xattn_ca_wo': _L0_xattn_in['ca_wo'], 'L0_xattn_ca_bo': _L0_xattn_in['ca_bo'], 'L0_xattn_ln1_g': _L0_xattn_in['ln1_g'], 'L0_xattn_ln1_b': _L0_xattn_in['ln1_b'], 'L0_xattn_ln2_g': _L0_xattn_in['ln2_g'], 'L0_xattn_ln2_b': _L0_xattn_in['ln2_b'], 'L0_xattn_ln3_g': _L0_xattn_in['ln3_g'], 'L0_xattn_ln3_b': _L0_xattn_in['ln3_b'], 'L0_xattn_router_w': _L0_xattn_in['router_w'], 'L0_xattn_router_b': _L0_xattn_in['router_b'], 'L0_xattn_e_w1': _L0_xattn_in['e_w1'], 'L0_xattn_e_b1': _L0_xattn_in['e_b1'], 'L0_xattn_e_w2': _L0_xattn_in['e_w2'], 'L0_xattn_e_b2': _L0_xattn_in['e_b2']}

def reference(x, ctx_1024, L0_xattn_sa_wq, L0_xattn_sa_bq, L0_xattn_sa_wk, L0_xattn_sa_bk, L0_xattn_sa_wv, L0_xattn_sa_bv, L0_xattn_sa_wo, L0_xattn_sa_bo, L0_xattn_ca_wq, L0_xattn_ca_bq, L0_xattn_ca_wk, L0_xattn_ca_bk, L0_xattn_ca_wv, L0_xattn_ca_bv, L0_xattn_ca_wo, L0_xattn_ca_bo, L0_xattn_ln1_g, L0_xattn_ln1_b, L0_xattn_ln2_g, L0_xattn_ln2_b, L0_xattn_ln3_g, L0_xattn_ln3_b, L0_xattn_router_w, L0_xattn_router_b, L0_xattn_e_w1, L0_xattn_e_b1, L0_xattn_e_w2, L0_xattn_e_b2):
    import jax
    import jax.numpy as jnp

    def _L0_xattn_ref(x, encoder_output, sa_wq, sa_bq, sa_wk, sa_bk, sa_wv, sa_bv, sa_wo, sa_bo, ca_wq, ca_bq, ca_wk, ca_bk, ca_wv, ca_bv, ca_wo, ca_bo, ln1_g, ln1_b, ln2_g, ln2_b, ln3_g, ln3_b, router_w, router_b, e_w1, e_b1, e_w2, e_b2):
        import jax, jax.numpy as jnp
        import numpy as np
        B, S, SE, D, H, FF, E, K = (2, 256, 256, 128, 16, 512, 8, 2)
        HD = D // H

        def _layernorm(x, g, b):
            m = x.mean(-1, keepdims=True)
            v = ((x - m) ** 2).mean(-1, keepdims=True)
            return (x - m) / jnp.sqrt(v + 1e-05) * g + b

        def _attn(q_in, k_in, v_in, wq, bq, wk, bk, wv, bv, wo, bo, causal):
            Bq, Sq, Dm = q_in.shape
            Sk = k_in.shape[1]
            Q = (q_in @ wq + bq).reshape(Bq, Sq, H, HD)
            Kp = (k_in @ wk + bk).reshape(Bq, Sk, H, HD)
            V = (v_in @ wv + bv).reshape(Bq, Sk, H, HD)
            scores = jnp.einsum('bqhd,bkhd->bhqk', Q, Kp) / jnp.sqrt(jnp.float32(HD))
            if causal:
                mask = jnp.tril(jnp.ones((Sq, Sk), bool))
                scores = jnp.where(mask, scores, -jnp.inf)
            a = jax.nn.softmax(scores, axis=-1)
            o = jnp.einsum('bhqk,bkhd->bqhd', a, V).reshape(Bq, Sq, Dm)
            return o @ wo + bo

        def _moe(x, rw, rb, w1, b1, w2, b2):
            T = x.shape[0] * x.shape[1]
            xf = x.reshape(T, D)
            router_weights = jax.nn.softmax(xf @ rw + rb, axis=-1)
            topw, topi = jax.lax.top_k(router_weights, K)
            topw = jax.nn.softmax(topw, axis=-1)
            combine = jnp.zeros((T, E), xf.dtype).at[jnp.arange(T)[:, None], topi].add(topw)
            h = jax.nn.gelu(jnp.einsum('td,edf->etf', xf, w1) + b1[:, None, :], approximate=False)
            eo = jnp.einsum('etf,efd->etd', h, w2) + b2[:, None, :]
            out = jnp.einsum('etd,te->td', eo, combine)
            return out.reshape(x.shape)
        x = _layernorm(x + _attn(x, x, x, sa_wq, sa_bq, sa_wk, sa_bk, sa_wv, sa_bv, sa_wo, sa_bo, True), ln1_g, ln1_b)
        x = _layernorm(x + _attn(x, encoder_output, encoder_output, ca_wq, ca_bq, ca_wk, ca_bk, ca_wv, ca_bv, ca_wo, ca_bo, False), ln2_g, ln2_b)
        x = _layernorm(x + _moe(x, router_w, router_b, e_w1, e_b1, e_w2, e_b2), ln3_g, ln3_b)
        return x
    x = _L0_xattn_ref(x, ctx_1024, L0_xattn_sa_wq, L0_xattn_sa_bq, L0_xattn_sa_wk, L0_xattn_sa_bk, L0_xattn_sa_wv, L0_xattn_sa_bv, L0_xattn_sa_wo, L0_xattn_sa_bo, L0_xattn_ca_wq, L0_xattn_ca_bq, L0_xattn_ca_wk, L0_xattn_ca_bk, L0_xattn_ca_wv, L0_xattn_ca_bv, L0_xattn_ca_wo, L0_xattn_ca_bo, L0_xattn_ln1_g, L0_xattn_ln1_b, L0_xattn_ln2_g, L0_xattn_ln2_b, L0_xattn_ln3_g, L0_xattn_ln3_b, L0_xattn_router_w, L0_xattn_router_b, L0_xattn_e_w1, L0_xattn_e_b1, L0_xattn_e_w2, L0_xattn_e_b2)
    return x

_drawn_inputs = setup_inputs


def setup_inputs(seed=0):
    import zlib

    import numpy as np

    out = dict(_drawn_inputs(seed))
    spreads = {'L0_xattn_sa_bq': (0.0, 0.8),
     'L0_xattn_sa_bk': (0.0, 2.0),
     'L0_xattn_sa_bv': (0.0, 0.272),
     'L0_xattn_sa_bo': (0.0, 0.1),
     'L0_xattn_ca_bq': (0.0, 2.0),
     'L0_xattn_ca_bk': (0.0, 2.0),
     'L0_xattn_ca_bv': (0.0, 0.31),
     'L0_xattn_ca_bo': (0.0, 0.1),
     'L0_xattn_ln1_g': (1.0, 0.2),
     'L0_xattn_ln1_b': (0.0, 0.1),
     'L0_xattn_ln2_g': (1.0, 0.2),
     'L0_xattn_ln2_b': (0.0, 0.1),
     'L0_xattn_ln3_g': (1.0, 0.2),
     'L0_xattn_ln3_b': (0.0, 0.1),
     'L0_xattn_router_b': (0.0, 0.1),
     'L0_xattn_e_b1': (0.0, 0.516),
     'L0_xattn_e_b2': (0.0, 0.1)}
    factors = {'L0_xattn_sa_wq': 8.0,
     'L0_xattn_sa_wk': 8.0,
     'L0_xattn_sa_wv': 4.454,
     'L0_xattn_ca_wq': 8.0,
     'L0_xattn_ca_wk': 8.0}
    for name, (base, spread) in spreads.items():
        noise = np.random.default_rng([zlib.crc32(name.encode()), seed]).standard_normal(out[name].shape)
        drawn = base * np.exp(spread * noise) if base else spread * noise
        out[name] = jnp.asarray(drawn.astype(out[name].dtype))
    for name, factor in factors.items():
        out[name] = (out[name] * factor).astype(out[name].dtype)
    return out
```

```python
from contextlib import ExitStack

import numpy as np
import concourse.bass as bass
from concourse import mybir

F32, F32R, BF16, I32 = mybir.dt.float32, mybir.dt.float32r, mybir.dt.bfloat16, mybir.dt.int32
ALU, ACT, AX = mybir.AluOpType, mybir.ActivationFunctionType, mybir.AxisListType

P = 128
HEADS, HD = 16, 8
GROUPS, J = 4, 4
EPS = 1e-5
EXPERTS, TOPK = 8, 2
CONSTS = 3 * P + GROUPS
ROW = P + 2


class Attention:

    def __init__(self, name, keys, w):
        self.name, self.keys, self.w = name, keys, w
        self.kpad = keys + keys % 2
        self.causal = name == "sa"


class Router:
    pass


class SlotTable:
    pass


def shape_constants():
    row = np.arange(P)
    c = np.zeros((P, CONSTS), np.float32)
    c[:, 0:P] = np.eye(P)
    c[:, P:2 * P] = np.where(row[None, :] > row[:, None], -1e30, 0.0)
    c[:, 2 * P:3 * P] = row[:, None] < row[None, :]
    for g in range(GROUPS):
        c[:, 3 * P + g] = (row % 32 < 8) & (row % GROUPS == g)
    return c


def expert_constants(tokens, slots):
    e, e9, m, s = np.arange(EXPERTS), np.arange(EXPERTS + 1), np.arange(tokens // P), np.arange(slots)
    parts = [EXPERTS - e, e * tokens, m * P, (e[None, :] < e9[:, None]).ravel(), s, e9, e9 * tokens, s * P]
    return np.tile(np.concatenate(parts).astype(np.float32)[None, :], (P, 1))


def result_rows(batch):
    p, b, c = np.ogrid[:P, :batch, :TOPK]
    return (c * batch * P + b * P + p).astype(np.int32)


def slot_count(tokens):
    n = (TOPK * tokens + EXPERTS * (P - 1)) // P
    return -(-n // 4) * 4


def build(nc, x, ctx_1024, sa, ca, moe, ln3, out, consts, expert_consts, rows_of_results):
    B, S, D = x.shape
    T_ALL = B * S
    F = moe["w1"].shape[2]
    FC = F // P
    SLOTS = slot_count(T_ALL)
    SC = ctx_1024.shape[1]
    PAIRS = B // 2
    SCALE = float(HD) ** -0.5

    stack = ExitStack()
    with stack:
        def sb(name, shape, dt=F32):
            return stack.enter_context(nc.sbuf_tensor(name, shape, dt))

        def sem(name):
            return stack.enter_context(nc.semaphore(name))

        bank = [stack.enter_context(nc.psum_tensor(f"bank{n}", [P, 512], F32)) for n in range(8)]
        SCORE, SHIFTED, WEIGHED, ACT_BANK, DVE_BANK = (0, 1), (2, 3), (4, 5), 6, 7

        cst = sb("cst", [P, CONSTS])
        ident, kones = cst[:, 0:P], cst[:, 3 * P:3 * P + GROUPS]
        ident_bf = sb("ident_bf", [P, P], BF16)
        causal_bf = sb("causal_bf", [P, P], BF16)
        half = sb("half", [P, 1])
        spread = {n: sb(f"spread_{n}", [P, GROUPS, J, 4, HD], F32R) for n in ("hq", "lq", "hk", "lk")}
        ones = sb("ones", [P, P])
        ecst = sb("ecst", [P, expert_consts.shape[1]])
        cut = np.cumsum([0, EXPERTS, EXPERTS, T_ALL // P, (EXPERTS + 1) * EXPERTS, SLOTS, EXPERTS + 1, EXPERTS + 1, SLOTS])
        falling, region, tile_starts, below, slot_no, expert_no, region9, slot_rows = (
            ecst[:, int(a):int(b)] for a, b in zip(cut[:-1], cut[1:]))
        xe = sb("xe", [P, B, TOPK, ROW])
        residual = xe[:, :, 0, 0:D]
        rw, rb = sb("router_w", [D, EXPERTS]), sb("router_b", [P, EXPERTS])
        b1_rows, b1 = sb("b1_rows", [EXPERTS * FC, P]), sb("expert_b1", [P, EXPERTS * FC])
        b2 = sb("expert_b2", [P, EXPERTS, D])
        g3, beta3 = sb("gamma3", [P, D]), sb("beta3", [P, D])
        dispatched = nc.dram_tensor("dispatched", [(EXPERTS + 1) * T_ALL, ROW], F32).ap()
        results = nc.dram_tensor("results", [TOPK * T_ALL, D], F32).ap()
        r = RT = Router()
        r.xT = sb("r_xT", [D, 2 * P])
        r.lg, r.ls, r.exl, r.p, r.eq, r.key, r.oh1, r.pm, r.eq2, r.key2, r.oh2, r.sel, r.base, r.t1, r.t2 = (
            sb(f"r_by_expert{n}", [P, 2, EXPERTS]) for n in range(15))
        r.nmx, r.sm, r.rsm, r.p1, r.km, r.p2, r.km2, r.d, r.ed, r.den, r.w1 = (
            sb(f"r_by_token{n}", [P, 2]) for n in range(11))
        r.pos = sb("r_pos", [P, TOPK, 2])
        r.row = sb("r_row", [P, B, TOPK], I32)
        r.acc = sb("r_acc", [P, EXPERTS])
        r.s_xt_ps = sem("r_xt_ps")
        r.s_xT = sem("r_xT")
        r.s_xe1 = sem("r_xe1")
        r.s_lg_ps = sem("r_lg_ps")
        r.s_rt = sem("r_rt")
        r.s_exp = sem("r_exp")
        r.s_rank_ps = sem("r_rank_ps")
        r.s_disp = sem("r_disp")
        s_fill, s_filled, s_late = sem("fill"), sem("filled"), sem("late")
        s_rows = sem("rows_of_results")
        s_const, s_zero = sem("s_const"), sem("s_zero")
        s_setup, s_pool_setup = sem("s_setup"), sem("s_pool_setup")

        def kind(name, keys, w, g, b, bo_next):
            k = Attention(name, keys, w)
            t = lambda n, shape, dt=F32: sb(f"{name}_{n}", shape, dt)
            k.wq, k.wk, k.wv, k.wo = (t(n, [D, D]) for n in ("wq", "wk", "wv", "wo"))
            k.bq, k.bk = t("bq", [P, 1]), t("bk", [P, 1])
            k.bv, k.bo, k.g, k.b = (t(n, [P, D]) for n in ("bv", "bo", "gamma", "beta"))
            k.xin = t("xin", [P, 2, D])
            k.xT = t("xT", [D, 2 * P])
            if not k.causal:
                k.cin, k.cT = t("cin", [keys, 2, D]), t("cT", [D, 2 * keys])
            k.hq, k.lq, k.hk, k.lk = (t(n, [P, 2 * P], F32R) for n in ("hq", "lq", "hk", "lk"))
            k.qu = t("qu", [P, GROUPS, 2 * P], F32R)
            k.ku = t("ku", [P, GROUPS, 2 * keys], F32R)
            k.qm = t("qm", [P, GROUPS, J, 2 * P], F32R)
            k.km = t("km", [P, GROUPS, J, 2 * k.kpad], F32R)
            k.vo = t("vo", [keys, 2, GROUPS, 64])
            k.nm = t("nm", [P, 2, GROUPS, J])
            k.mm = t("mm", [P, 2, J, 32], F32R)
            k.pt_all = t("pt", [P, 2 * GROUPS * 512])
            k.pt = [k.pt_all[0:keys, u * GROUPS * 512:(u + 1) * GROUPS * 512] for u in range(2)]
            k.us = [t(f"us{u}", [P, 2, 512]) for u in range(2)]
            k.rd = t("rd", [P, 2, 2, 2, J])
            k.on, k.oT, k.y, k.xn, k.xg = (t(n, [P, 2, D]) for n in ("on", "oT", "y", "xn", "xg"))
            k.bs, k.ba, k.ve, k.rs = t("bs", [P, 2, 6]), t("ba", [P, 2, 2]), t("ve", [P, 2]), t("rs", [P, 2])
            k.x1 = t("x1", [P, 2, D])
            k.s_ld = sem(f"{name}_ld")
            k.s_xt_ps = sem(f"{name}_xt_ps")
            k.s_xt = sem(f"{name}_xt")
            k.s_ct_ps = sem(f"{name}_ct_ps")
            k.s_ct = sem(f"{name}_ct")
            k.s_c_ps = sem(f"{name}_c_ps")
            k.s_hi = sem(f"{name}_hi")
            k.s_lo = sem(f"{name}_lo")
            k.s_rq_ps = sem(f"{name}_rq_ps")
            k.s_rk_ps = sem(f"{name}_rk_ps")
            k.s_qu = sem(f"{name}_qu")
            k.s_ku = sem(f"{name}_ku")
            k.s_v_ps = sem(f"{name}_v_ps")
            k.s_vo = sem(f"{name}_vo")
            k.s_bdq = sem(f"{name}_bdq")
            k.s_bdk = sem(f"{name}_bdk")
            k.s_s1_ps = sem(f"{name}_s1_ps")
            k.s_nm = sem(f"{name}_nm")
            k.s_mmh = sem(f"{name}_mmh")
            k.s_mm = sem(f"{name}_mm")
            k.s_mt_ps = sem(f"{name}_mt_ps")
            k.s_sha = sem(f"{name}_sha")
            k.s_shv = sem(f"{name}_shv")
            k.s_s2_ps = sem(f"{name}_s2_ps")
            k.s_ex = sem(f"{name}_ex")
            k.s_pm = sem(f"{name}_pm")
            k.s_u_ps = sem(f"{name}_u_ps")
            k.s_us = sem(f"{name}_us")
            k.s_t_ps = sem(f"{name}_t_ps")
            k.s_rd = sem(f"{name}_rd")
            k.s_on = sem(f"{name}_on")
            k.s_ot_ps = sem(f"{name}_ot_ps")
            k.s_ot = sem(f"{name}_ot")
            k.s_w_ps = sem(f"{name}_w_ps")
            k.s_y = sem(f"{name}_y")
            k.s_bs = sem(f"{name}_bs")
            k.s_ba = sem(f"{name}_ba")
            k.s_ve = sem(f"{name}_ve")
            k.s_rs = sem(f"{name}_rs")
            k.s_xn = sem(f"{name}_xn")
            k.s_xg = sem(f"{name}_xg")
            k.s_x1 = sem(f"{name}_x1")
            k.s_xr = sem(f"{name}_xr")
            return k

        SA = kind("sa", S, sa, None, None, None)
        CA = kind("ca", SC, ca, None, None, None)
        KINDS = (SA, CA)
        fill = CA.pt_all[:, 0:T_ALL // P * ROW]
        w2 = SA.pt_all[:, :].rearrange("p (e c d) -> p e c d", e=EXPERTS, c=FC)
        ROUTER_OPS = 31
        SELECTED = 18
        tb = SlotTable()
        TABLE_OPS = 13
        E9 = EXPERTS + 1
        tb.count, tb.tiles, tb.first, tb.shift, tb.expert, tb.start = (
            sb(f"tb_row{n}", [1, size]) for n, size in enumerate((EXPERTS, EXPERTS, E9, E9, SLOTS, SLOTS)))
        tb.full, tb.before, tb.past, tb.one, tb.prod = (
            sb(f"tb_square{n}", [1, a, b]) for n, (a, b) in enumerate(((EXPERTS, T_ALL // P), (E9, EXPERTS), (SLOTS, EXPERTS), (SLOTS, E9), (SLOTS, E9))))
        s_table, s_weights, s_counts, s_b1 = sem("table"), sem("expert_weights"), sem("counts"), sem("b1")
        slot_expert_i, slot_row_i = sb("slot_expert", [1, SLOTS], I32), sb("slot_row", [1, SLOTS], I32)
        rows_sb = sb("rows_sb", [P, B, TOPK], I32)
        AHEAD = 4
        xs = [sb(f"xs{v}", [P, ROW]) for v in range(AHEAD)]
        w1 = [CA.pt_all[:, v * F:(v + 1) * F] for v in range(AHEAD)]
        xsT = [sb(f"xsT{v}", [D, P]) for v in range(2)]
        hid = [SA.us[v][:, 0, :].rearrange("p (c n) -> p c n", c=FC) for v in range(2)]
        yb = [sb(f"yb{v}", [P, D]) for v in range(2)]
        ys = [CA.pt_all[:, AHEAD * F + v * D:AHEAD * F + (v + 1) * D] for v in range(AHEAD)]
        s_xs, s_w1, s_scatter = ([sem(f"{n}{v}") for v in range(AHEAD)] for n in ("xs", "w1", "scatter"))
        s_xst_ps, s_xst, s_h_ps, s_gelu, s_o_ps, s_yb, s_ys = (sem("m_" + n) for n in "xst_ps xst h_ps gelu o_ps yb ys".split())
        TN = 4
        TAIL = B // TN
        yy = [CA.pt_all[:, c * B * D:(c + 1) * B * D].rearrange("p (b d) -> p b d", b=B) for c in range(2)]
        y3, o3 = yy
        bs3, ba3, ve3, rs3 = sb("bs3", [P, B, 6]), sb("ba3", [P, B, 2]), sb("ve3", [P, B]), sb("rs3", [P, B])
        s_yy = [sem(f"yy{q}") for q in range(TAIL)]
        s_y3a, s_y3, s_bs3, s_ba3, s_ve3, s_rs3, s_xn3, s_g3, s_o3 = (sem("t_" + n) for n in "y3a y3 bs3 ba3 ve3 rs3 xn3 g3 o3".split())
        s_out, s_spread0, s_pool_ones = sem("s_out"), sem("s_spread0"), sem("pool_ones")
        SETUP = 14

        block = stack.enter_context(nc.Block())

        def after_pair(p):
            return not isinstance(p, int) or p > 0

        ORDER = [
            (SA, "scores", 0, 0), (RT, "route", 0, -2), (RT, "gate", 0, -2), (CA, "turn", 0, -1), (SA, "scores", 1, 0),
            (SA, "shift", 0, 0), (SA, "shift_rows", 0, 0), (CA, "project", 0, -1), (SA, "shift", 1, 0), (SA, "shift_rows", 1, 0), (CA, "spread_terms", 0, -1),
            (CA, "spread_terms", 1, -1), (SA, "weights", 0, 0), (CA, "values", 0, -1), (RT, "choose", 0, -2), (SA, "mix", 0, 0),
            (SA, "weights", 1, 0), (SA, "restore", 0, 0), (SA, "mix", 1, 0), (RT, "place", 0, -2), (CA, "scores", 0, -1),
            (SA, "turn_heads", 0, 0), (CA, "scores", 1, -1), (SA, "norm", 0, 0), (SA, "restore", 1, 0), (CA, "shift", 0, -1), (CA, "shift_rows", 0, -1),
            (SA, "turn", 0, 1), (CA, "shift", 1, -1), (CA, "shift_rows", 1, -1), (SA, "project", 0, 1), (SA, "turn_heads", 1, 0), (CA, "weights", 0, -1),
            (SA, "spread_terms", 0, 1), (SA, "norm", 1, 0), (CA, "mix", 0, -1), (CA, "weights", 1, -1), (SA, "spread_terms", 1, 1),
            (SA, "values", 0, 1), (CA, "restore", 0, -1), (CA, "mix", 1, -1), (CA, "turn_heads", 0, -1), (CA, "restore", 1, -1),
            (CA, "norm", 0, -1), (CA, "turn_heads", 1, -1), (CA, "norm", 1, -1)]

        def iteration(i, steps):
            for k, step, u, ahead in ORDER:
                if not isinstance(i, int) or 0 <= i + ahead < PAIRS:
                    if step in steps:
                        steps[step](k, i + ahead, u)

        FIRST_ITERATION, LAST_ITERATION = -max(o[3] for o in ORDER), PAIRS - 1 - min(o[3] for o in ORDER)

        def iterations(steps, end_iteration=lambda i: None):
            for i in range(FIRST_ITERATION, LAST_ITERATION + 1):
                iteration(i, steps)
                end_iteration(i)

        def slots(engine):
            for i in range(SLOTS // AHEAD):
                for v in range(AHEAD):
                    yield i, v

        @block.sync
        def _(sp):
            sp.dma_start(cst[:, :], consts).then_inc(s_const, 16)
            sp.dma_start(residual, x.rearrange("b p d -> p b d")).then_inc(s_const, 16)
            for k in KINDS:
                for tile, n in ((k.wq, "wq"), (k.wk, "wk"), (k.wv, "wv"), (k.wo, "wo")):
                    sp.dma_start(tile[:, :], k.w[n]).then_inc(s_const, 16)
                for tile, n in ((k.bq, "bq"), (k.bk, "bk")):
                    sp.dma_start(tile[:, :], k.w[n].rearrange("(p o) -> p o", o=1)).then_inc(s_const, 16)
                for tile, n in ((k.bv, "bv"), (k.bo, "bo"), (k.g, "g"), (k.b, "b")):
                    sp.dma_start(tile[:, :], k.w[n].rearrange("(o d) -> o d", o=1).to_broadcast([P, D])).then_inc(s_const, 16)

            def turn(k, p, u):
                if after_pair(p):
                    sp.wait_ge(k.s_xt_ps if k.causal else k.s_ct_ps, p)
                if k.causal:
                    sp.dma_start(k.xin[:, :, :], x[bass.ds(p * 2, 2)].rearrange("b p d -> p b d")).then_inc(k.s_ld, 16)
                else:
                    sp.dma_start(k.cin[:, :, :], ctx_1024[bass.ds(p * 2, 2)].rearrange("b p d -> p b d")).then_inc(k.s_ld, 16)

            def spread_terms(k, p, u):
                if u == 0:
                    return
                sp.wait_ge(k.s_ku, p * 2 + 2)
                if after_pair(p):
                    sp.wait_ge(k.s_s1_ps, p * 8)
                for j in range(J):
                    rows = slice(32 * j + 8, 32 * j + 32)
                    sp.dma_start(k.km[rows, :, j, 0:2 * k.keys].bitcast(F32), k.ku[rows, :, :].bitcast(F32)).then_inc(k.s_bdk, 16)
                sp.wait_ge(k.s_qu, p * 2 + 2)
                if after_pair(p):
                    sp.wait_ge(k.s_s2_ps, p * 8)
                for j in range(J):
                    rows = slice(32 * j + 8, 32 * j + 32)
                    sp.dma_start(k.qm[rows, :, j, :].bitcast(F32), k.qu[rows, :, :].bitcast(F32)).then_inc(k.s_bdq, 16)

            sp.dma_start(rw[:, :], moe["rw"]).then_inc(s_late, 16)
            sp.dma_start(rb[:, :], moe["rb"].rearrange("(o d) -> o d", o=1).to_broadcast([P, EXPERTS])).then_inc(s_late, 16)
            sp.dma_start(ecst[:, :], expert_consts).then_inc(s_late, 16)
            sp.dma_start(rows_sb[:, :, :], rows_of_results).then_inc(s_rows, 16)
            sp.wait_ge(s_fill, 1)
            for e in range(EXPERTS + 1):
                sp.dma_start(dispatched[e * T_ALL:(e + 1) * T_ALL, :].rearrange("(p n) w -> p (n w)", p=P), fill[:, :]).then_inc(s_filled, 16)
            sp.dma_start(b1_rows[:, :], moe["b1"].rearrange("e (c f) -> (e c) f", c=FC)).then_inc(s_weights, 16)
            sp.dma_start(b2[:, :, :], moe["b2"].rearrange("(o e) d -> o e d", o=1).to_broadcast([P, EXPERTS, D])).then_inc(s_weights, 16)
            for tile, w in ((g3, ln3["g"]), (beta3, ln3["b"])):
                sp.dma_start(tile[:, :], w.rearrange("(o d) -> o d", o=1).to_broadcast([P, D])).then_inc(s_weights, 16)
            sp.wait_ge(s_zero, 4)
            def end(i):
                if i == PAIRS:
                    sp.wait_ge(SA.s_u_ps, PAIRS * 4)
                    for e in range(EXPERTS):
                        sp.dma_start(w2[:, e], moe["w2"][e].rearrange("(c f) d -> f c d", c=FC)).then_inc(s_weights, 16)

            iterations({"turn": turn, "spread_terms": spread_terms}, end)
            sp.wait_ge(SA.s_t_ps, PAIRS * 4)

            sp.wait_ge(s_table, TABLE_OPS)
            sp.wait_ge(r.s_disp, PAIRS * 4 * 16)
            sp.wait_ge(CA.s_u_ps, PAIRS * 4)
            for i, v in slots(sp):
                n = i * AHEAD + v
                row = sp.value_load(slot_row_i[0:1, bass.ds(n, 1)], min_val=0, max_val=(EXPERTS + 1) * T_ALL - P)
                expert = sp.value_load(slot_expert_i[0:1, bass.ds(n, 1)], min_val=0, max_val=EXPERTS - 1)
                if after_pair(i):
                    sp.wait_ge(s_scatter[v], i * 16)
                    sp.wait_ge(s_h_ps, (i - 1) * 2 * AHEAD + 2 * v + 2)
                sp.dma_start(xs[v][:, :], dispatched[bass.ds(row, P), :]).then_inc(s_xs[v], 16)
                sp.dma_start(w1[v], moe["w1"][bass.ds(expert, 1)].rearrange("o d f -> d (o f)")).then_inc(s_w1[v], 16)

            for v in range(AHEAD):
                sp.wait_ge(s_scatter[v], 16 * (SLOTS // AHEAD))
            for q in range(TAIL):
                for c in range(TOPK):
                    src = results[c * T_ALL + q * TN * P:c * T_ALL + (q + 1) * TN * P, :]
                    sp.dma_start(yy[c][:, TN * q:TN * q + TN, :], src.rearrange("(b p) d -> p b d", p=P)).then_inc(s_yy[q], 16)
            for q in range(TAIL):
                sp.wait_ge(s_o3, TN * (q + 1))
                sp.dma_start(out[TN * q:TN * q + TN].rearrange("b p d -> p b d"), o3[:, TN * q:TN * q + TN, :]).then_inc(s_out, 16)
            sp.wait_ge(s_out, 16 * TAIL)

        @block.tensor
        def _(pe):
            held = {}
            now = [0]

            def take(b):
                for s, n, c in held.get(b, ()):
                    pe.wait_ge(s, now[0] * n + c)

            def give(b, s, n, value_at_zero, *others):
                held[b] = ((s, n, value_at_zero),) + others

            off = [0]

            def turn(k, p, u):
                if k.causal:
                    pe.wait_ge(k.s_ld, p * 16 + 16)
                else:
                    pe.wait_ge(SA.s_x1, p * 2 + 2)
                src = k.xin if k.causal else SA.x1
                take(ACT_BANK)
                for v in range(2):
                    ins = pe.transpose(bank[ACT_BANK][:, P * v:P * v + P], src[:, v, :], ident)
                ins.then_inc(k.s_xt_ps, 1)
                give(ACT_BANK, k.s_xt, 1, 1 + off[0])
                if not k.causal:
                    pe.wait_ge(k.s_ld, p * 16 + 16)
                    take(DVE_BANK)
                    for v in range(2):
                        ins = pe.transpose(bank[DVE_BANK][:, SC * v:SC * v + SC], k.cin[:, v, :], ident[0:SC, 0:SC])
                    ins.then_inc(k.s_ct_ps, 1)
                    give(DVE_BANK, k.s_ct, 1, 1 + off[0])

            def project(k, p, u):
                pe.wait_ge(k.s_xt, p + 1)
                take(ACT_BANK)
                pe.matmul(bank[ACT_BANK][:, 0:2 * P], k.wq[:, :], k.xT[:, :], start=True, stop=True).then_inc(k.s_c_ps, 1)
                give(ACT_BANK, k.s_lo, 2, 1 + 2 * off[0])
                if not k.causal:
                    pe.wait_ge(k.s_ct, p + 1)
                take(DVE_BANK)
                src = k.xT if k.causal else k.cT
                pe.matmul(bank[DVE_BANK][:, 0:2 * k.keys], k.wk[:, :], src[:, :], start=True, stop=True).then_inc(k.s_c_ps, 1)
                give(DVE_BANK, k.s_lo, 2, 2 + 2 * off[0])

            def spread_terms(k, p, u):
                for b, hi, lo, h, l, s, done, n in (
                        (ACT_BANK, "hq", "lq", k.hq, k.lq, k.s_rq_ps, k.s_qu, 1),
                        (DVE_BANK, "hk", "lk", k.hk, k.lk, k.s_rk_ps, k.s_ku, 2)):
                    pe.wait_ge(k.s_lo, p * 2 + n)
                    take(b)
                    for g in (2 * u, 2 * u + 1):
                        dst = bank[b][:, 2 * P * (g % 2):2 * P * (g % 2) + 2 * P]
                        pe.matmul(dst, spread[hi][:, g].rearrange("c j t d -> c (j t d)"), h[:, :], start=True, stop=False)
                        ins = pe.matmul(dst, spread[lo][:, g].rearrange("c j t d -> c (j t d)"), l[:, :], start=False, stop=True)
                    ins.then_inc(s, 1)
                    give(b, done, 2, u + 1 + 2 * off[0])

            def values(k, p, u):
                src = k.xT if k.causal else k.cT
                take(DVE_BANK)
                for v in range(2):
                    ins = pe.matmul(bank[DVE_BANK][0:k.keys, P * v:P * v + P], src[:, k.keys * v:k.keys * v + k.keys], k.wv[:, :], start=True, stop=True)
                ins.then_inc(k.s_v_ps, 1)
                give(DVE_BANK, k.s_vo, 1, 1 + off[0])

            def scores(k, p, u):
                if u == 0:
                    pe.wait_ge(k.s_bdk, p * 64 + 64)
                    pe.wait_ge(k.s_qu, p * 2 + 2)
                for g in range(GROUPS):
                    b = SCORE[g % 2]
                    take(b)
                    dst = bank[b][:, :].rearrange("q (j n) -> q j n", j=J)[:, :, 0:k.kpad]
                    if k.causal:
                        pe.matmul(dst, ident_bf[:, :], causal_bf[:, :].rearrange("q (o n) -> q o n", o=1).to_broadcast([P, J, P]), start=True, stop=False)
                    pe.matmul(dst, k.qu[:, g, P * u:P * u + P], k.km[:, g, :, k.keys * u:k.keys * u + k.kpad],
                              start=not k.causal, stop=True).then_inc(k.s_s1_ps, 1)
                    give(b, k.s_nm, 8, 4 * u + g + 1 + 8 * off[0])

            def shift(k, p, u):
                pe.wait_ge(k.s_mm, p * 2 + u + 1)
                take(ACT_BANK)
                pe.transpose(bank[ACT_BANK][:, 0:P], k.mm[:, u].rearrange("q j r -> q (j r)").bitcast(F32), ident).then_inc(k.s_mt_ps, 1)
                give(ACT_BANK, k.s_sha, 4, 2 * u + 2 + 4 * off[0], (k.s_shv, 4, 2 * u + 2 + 4 * off[0]))

            def weights(k, p, u):
                pe.wait_ge(k.s_sha, p * 4 + 2 * u + 2)
                pe.wait_ge(k.s_shv, p * 4 + 2 * u + 2)
                if u == 0:
                    pe.wait_ge(k.s_bdq, p * 64 + 64)
                    pe.wait_ge(k.s_ku, p * 2 + 2)
                for g in range(GROUPS):
                    b = SHIFTED[g % 2]
                    take(b)
                    pe.matmul(bank[b][0:k.keys, :], k.ku[:, g, k.keys * u:k.keys * u + k.keys], k.qm[:, g, :, P * u:P * u + P],
                              start=True, stop=True).then_inc(k.s_s2_ps, 1)
                    give(b, k.s_ex, 8, 4 * u + g + 1 + 8 * off[0])

            def mix(k, p, u):
                if u == 0:
                    pe.wait_ge(k.s_vo, p + 1)
                for g in range(GROUPS):
                    b = WEIGHED[g // 2]
                    pe.wait_ge(k.s_pm if k.causal else k.s_ex, p * 8 + 4 * u + g + 1)
                    if g % 2 == 0:
                        take(b)
                    ins = pe.matmul(bank[b][64 * (g % 2):64 * (g % 2) + 64, :], k.vo[:, u, g, :], k.pt[u][:, 512 * g:512 * g + 512], start=True, stop=True)
                    if g % 2:
                        ins.then_inc(k.s_u_ps, 1)
                        give(b, k.s_us, 4, 2 * u + g // 2 + 1 + 4 * off[0])

            def restore(k, p, u):
                for h in range(2):
                    b = WEIGHED[h]
                    take(b)
                    pe.wait_ge(k.s_us, p * 4 + 2 * u + h + 1)
                    for j in range(J):
                        ins = pe.transpose(bank[b][:, P * j:P * j + P], k.us[u][:, h, P * j:P * j + P], ident)
                    ins.then_inc(k.s_t_ps, 1)
                    give(b, k.s_on, 4, 2 * u + h + 1 + 4 * off[0])

            def turn_heads(k, p, u):
                pe.wait_ge(k.s_on, p * 4 + 2 * u + 2)
                take(ACT_BANK)
                pe.transpose(bank[ACT_BANK][:, 0:P], k.on[:, u, :], ident).then_inc(k.s_ot_ps, 1)
                give(ACT_BANK, k.s_ot, 2, u + 1 + 2 * off[0])

            def norm(k, p, u):
                pe.wait_ge(k.s_ot, p * 2 + u + 1)
                take(DVE_BANK)
                pe.matmul(bank[DVE_BANK][:, 0:D], k.oT[:, u, :], k.wo[:, :], start=True, stop=True).then_inc(k.s_w_ps, 1)
                give(DVE_BANK, k.s_y, 2, u + 1 + 2 * off[0])

            def route(k, p, u):
                pe.wait_ge(CA.s_x1, p * 2 + 2)
                take(ACT_BANK)
                for v in range(2):
                    ins = pe.transpose(bank[ACT_BANK][:, P * v:P * v + P], CA.x1[:, v, :], ident)
                ins.then_inc(r.s_xt_ps, 1)
                give(ACT_BANK, r.s_xT, 1, 1 + off[0])
                pe.wait_ge(r.s_xT, p + 1)
                take(DVE_BANK)
                for v in range(2):
                    ins = pe.matmul(bank[DVE_BANK][:, EXPERTS * v:EXPERTS * v + EXPERTS], r.xT[:, P * v:P * v + P], rw[:, :], start=True, stop=True)
                ins.then_inc(r.s_lg_ps, 1)
                give(DVE_BANK, r.s_rt, ROUTER_OPS, 1 + ROUTER_OPS * off[0])

            def place(k, p, u):
                pe.wait_ge(r.s_rt, p * ROUTER_OPS + SELECTED)
                take(DVE_BANK)
                for v in range(2):
                    dst = bank[DVE_BANK][:, EXPERTS * v:EXPERTS * v + EXPERTS]
                    pe.matmul(dst, cst[:, 2 * P:3 * P], r.sel[:, v, :], start=True, stop=False)
                    ins = pe.matmul(dst, ones[:, :], r.acc[:, :], start=False, stop=(v == 0))
                    if v == 1:
                        ins = pe.matmul(dst, ones[:, :], r.sel[:, 0, :], start=False, stop=True)
                ins.then_inc(r.s_rank_ps, 1)
                give(DVE_BANK, r.s_rt, ROUTER_OPS, SELECTED + 6 + ROUTER_OPS * off[0])

            pe.wait_ge(s_const, 16 * 22)
            pe.wait_ge(s_setup, SETUP)
            pe.wait_ge(s_late, 48)
            raw = {"route": route, "place": place, "turn": turn, "project": project, "spread_terms": spread_terms, "values": values, "scores": scores, "shift": shift, "weights": weights, "mix": mix, "restore": restore, "turn_heads": turn_heads, "norm": norm}

            def at(f):
                def g(k, p, u):
                    off[0] = p - now[0]
                    f(k, p, u)
                return g

            def end(i):
                now[0] += 1
                for b in held:
                    held[b] = tuple((s, n, c - n) for s, n, c in held[b])

            now[0] = FIRST_ITERATION
            iterations({n: at(f) for n, f in raw.items()}, end)

            pe.wait_ge(r.s_rt, PAIRS * ROUTER_OPS)
            take(DVE_BANK)
            pe.matmul(bank[DVE_BANK][:, 0:EXPERTS], ones[:, :], r.acc[:, :], start=True, stop=True).then_inc(s_counts, 1)

            pe.wait_ge(s_weights, 16 * (EXPERTS + 4))
            take(ACT_BANK)
            pe.transpose(bank[ACT_BANK][:, 0:EXPERTS * FC], b1_rows[:, :], ident[0:EXPERTS * FC, 0:EXPERTS * FC]).then_inc(s_b1, 1)
            pe.wait_ge(s_b1, 2)
            pe.wait_ge(s_table, TABLE_OPS)

            def hidden(i, v):
                n, b = i * AHEAD + v, v % 2
                pe.wait_ge(s_xs[v], i * 16 + 16)
                pe.wait_ge(s_xst, n - 1) if after_pair(i) or v >= 2 else None
                pe.transpose(bank[6 + b][:, 0:P], xs[v][:, 0:P], ident).then_inc(s_xst_ps, 1)
                pe.wait_ge(s_xst, n + 1)
                pe.wait_ge(s_w1[v], i * 16 + 16)
                for c in range(FC):
                    if (after_pair(i) or v >= 2) and c % 2 == 0:
                        pe.wait_ge(s_gelu, (n - 2) * 4 + c + 2)
                    ins = pe.matmul(bank[2 * b + c // 2][:, P * (c % 2):P * (c % 2) + P], w1[v][:, P * c:P * c + P], xsT[b][:, :], start=True, stop=True)
                    if c % 2:
                        ins.then_inc(s_h_ps, 1)

            def output(i, v):
                n, b = i * AHEAD + v, v % 2
                expert = pe.value_load(slot_expert_i[0:1, bass.ds(n, 1)], min_val=0, max_val=EXPERTS - 1)
                if after_pair(i) or v >= 2:
                    pe.wait_ge(s_yb, n - 1)
                for c in range(FC):
                    pe.wait_ge(s_gelu, n * 4 + c + 1)
                    ins = pe.matmul(bank[4 + b][:, 0:D], hid[b][:, c, :], w2[:, bass.ds(expert, 1), c, :].rearrange("f o d -> f (o d)"), start=(c == 0), stop=(c == FC - 1))
                ins.then_inc(s_o_ps, 1)

            hidden(0, 0)
            for i, v in slots(pe):
                if v < AHEAD - 1:
                    hidden(i, v + 1)
                elif i < SLOTS // AHEAD - 1:
                    hidden(i + 1, 0)
                output(i, v)

        @block.scalar
        def _(act):
            act.wait_ge(s_const, 16 * 22)
            act.wait_ge(s_zero, 4)

            def turn(k, p, u):
                act.wait_ge(k.s_xt_ps, p + 1)
                if after_pair(p):
                    act.wait_ge(k.s_v_ps, p) if k.causal else act.wait_ge(k.s_c_ps, p * 2)
                act.copy(k.xT[:, :], bank[ACT_BANK][:, 0:2 * P]).then_inc(k.s_xt, 1)

            def project(k, p, u):
                act.wait_ge(k.s_c_ps, p * 2 + 1)
                if after_pair(p):
                    act.wait_ge(k.s_rq_ps, p * 2)
                act.activation(k.hq[:, :], bank[ACT_BANK][:, 0:2 * P], ACT.Identity, bias=k.bq[:, :]).then_inc(k.s_hi, 1)
                act.wait_ge(k.s_c_ps, p * 2 + 2)
                if after_pair(p):
                    act.wait_ge(k.s_rk_ps, p * 2)
                n = 2 * k.keys
                act.activation(k.hk[:, 0:n], bank[DVE_BANK][:, 0:n], ACT.Identity, bias=k.bk[:, :]).then_inc(k.s_hi, 1)

            def spread_terms(k, p, u):
                act.wait_ge(k.s_rq_ps, p * 2 + u + 1)
                if after_pair(p):
                    act.wait_ge(k.s_s1_ps, p * 8)
                    act.wait_ge(k.s_bdq, p * 64)
                act.copy(k.qu[:, 2 * u:2 * u + 2, :].rearrange("r g n -> r (g n)"), bank[ACT_BANK][:, :]).then_inc(k.s_qu, 1)

            def shift(k, p, u):
                act.wait_ge(k.s_mt_ps, p * 2 + u + 1)
                if after_pair(p):
                    act.wait_ge(k.s_s2_ps, (p - 1) * 8 + 4 * u + 4)
                for j in (0, 1):
                    rows = slice(32 * j, 32 * j + 8)
                    src = bank[ACT_BANK][rows, 0:P].rearrange("r (o n) -> r o n", o=1).to_broadcast([8, GROUPS, P])
                    act.copy(k.qm[rows, :, j, P * u:P * u + P], src).then_inc(k.s_sha, 1)

            def weights(k, p, u):
                if not k.causal and not after_pair(p):
                    act.wait_ge(s_filled, 16 * (EXPERTS + 1))
                for g in range(GROUPS):
                    act.wait_ge(k.s_s2_ps, p * 8 + 4 * u + g + 1)
                    if after_pair(p) and g % 2 == 0:
                        act.wait_ge(k.s_u_ps, (p - 1) * 4 + 2 * u + g // 2 + 1)
                    act.activation(k.pt[u][:, 512 * g:512 * g + 512], bank[SHIFTED[g % 2]][0:k.keys, :], ACT.Exp, scale=SCALE).then_inc(k.s_ex, 1)

            def mix(k, p, u):
                for h in range(2):
                    act.wait_ge(k.s_u_ps, p * 4 + 2 * u + h + 1)
                    if after_pair(p):
                        act.wait_ge(k.s_t_ps, (p - 1) * 4 + 2 * u + h + 1)
                    act.copy(k.us[u][:, h, :], bank[WEIGHED[h]][:, :]).then_inc(k.s_us, 1)

            def turn_heads(k, p, u):
                act.wait_ge(k.s_ot_ps, p * 2 + u + 1)
                if after_pair(p):
                    act.wait_ge(k.s_w_ps, (p - 1) * 2 + u + 1)
                act.copy(k.oT[:, u, :], bank[ACT_BANK][:, 0:P]).then_inc(k.s_ot, 1)

            def route(k, p, u):
                act.wait_ge(r.s_xt_ps, p + 1)
                if after_pair(p):
                    act.wait_ge(r.s_lg_ps, p)
                act.copy(r.xT[:, :], bank[ACT_BANK][:, 0:2 * P]).then_inc(r.s_xT, 1)
                act.wait_ge(CA.s_x1, p * 2 + 2)
                act.copy(xe[:, bass.ds(p * 2, 2), 1, 0:D], CA.x1[:, :, :]).then_inc(r.s_xe1, 1)

            def gate(k, p, u):
                act.wait_ge(r.s_rt, p * ROUTER_OPS + 3)
                act.activation(r.exl[:, :, :], r.ls[:, :, :], ACT.Exp).then_inc(r.s_exp, 1)

            def choose(k, p, u):
                act.wait_ge(r.s_rt, p * ROUTER_OPS + SELECTED + 1)
                act.activation(r.ed[:, :], r.d[:, :], ACT.Exp).then_inc(r.s_exp, 1)

            iterations({"route": route, "gate": gate, "choose": choose, "turn": turn, "project": project, "spread_terms": spread_terms, "shift": shift, "weights": weights, "mix": mix, "turn_heads": turn_heads})

            act.wait_ge(s_b1, 1)
            act.copy(b1[:, :], bank[ACT_BANK][:, 0:EXPERTS * FC]).then_inc(s_b1, 1)
            act.wait_ge(s_b1, 2)
            act.wait_ge(s_table, TABLE_OPS)
            for i, v in slots(act):
                n, b = i * AHEAD + v, v % 2
                expert = act.value_load(slot_expert_i[0:1, bass.ds(n, 1)], min_val=0, max_val=EXPERTS - 1)
                for c in range(FC):
                    if c % 2 == 0:
                        act.wait_ge(s_h_ps, n * 2 + c // 2 + 1)
                    if (after_pair(i) or v >= 2) and c == 0:
                        act.wait_ge(s_o_ps, n - 1)
                    act.activation(hid[b][:, c, :], bank[2 * b + c // 2][:, P * (c % 2):P * (c % 2) + P], ACT.Gelu,
                                   bias=b1[:, bass.ds(expert * FC + c, 1)]).then_inc(s_gelu, 1)

        @block.vector
        def _(dve):
            dve.memset(ones[:, :], 1.0).then_inc(s_pool_ones, 1)
            dve.memset(fill[:, :], 1.0).then_inc(s_fill, 1)
            dve.memset(r.acc[:, :], 0.0).then_inc(s_pool_ones, 1)
            n_setup = [0]

            def setup(ins):
                n_setup[0] += 1
                ins.then_inc(s_setup, 1)

            for k in KINDS:
                setup(dve.memset(k.vo[:, :, :, 32:64], 1.0))
                setup(dve.memset(k.mm[:, :, :, :].bitcast(F32), 0.0))
            setup(dve.memset(CA.hk[:, 2 * SC:].bitcast(F32), 0.0))
            setup(dve.memset(CA.lk[:, 2 * SC:].bitcast(F32), 0.0))
            zeroed = n_setup[0]
            for n in spread:
                dve.memset(spread[n][:, :, :, :, :].bitcast(F32), 0.0).then_inc(s_spread0, 1)
            dve.wait_ge(s_spread0, 4)
            dve.wait_ge(s_const, 16 * 22)
            for n, terms in (("hq", (1, 2)), ("lq", (3,)), ("hk", (1, 3)), ("lk", (2,))):
                for t in terms:
                    setup(dve.tensor_copy(spread[n][:, :, :, t, :], ident.rearrange("c (g j d) -> c g j d", g=GROUPS, j=J)))
            setup(dve.tensor_copy(ident_bf[:, :], ident))
            setup(dve.tensor_copy(causal_bf[:, :], cst[:, P:2 * P]))
            assert n_setup[0] == SETUP, n_setup[0]

            def turn(k, p, u):
                if k.causal:
                    return
                dve.wait_ge(k.s_ct_ps, p + 1)
                if after_pair(p):
                    dve.wait_ge(k.s_v_ps, p)
                dve.tensor_copy(k.cT[:, :], bank[DVE_BANK][:, 0:2 * SC]).then_inc(k.s_ct, 1)

            def project(k, p, u):
                for n, (b, bias, h, l, w, s) in enumerate(((ACT_BANK, k.bq, k.hq, k.lq, 2 * P, k.s_rq_ps), (DVE_BANK, k.bk, k.hk, k.lk, 2 * k.keys, k.s_rk_ps))):
                    dve.wait_ge(k.s_hi, p * 2 + n + 1)
                    if after_pair(p):
                        dve.wait_ge(s, p * 2)
                    dve.scalar_tensor_tensor(out=l[:, 0:w], in0=bank[b][:, 0:w], scalar=bias[:, :], in1=h[:, 0:w].bitcast(F32),
                                             op0=ALU.add, op1=ALU.subtract).then_inc(k.s_lo, 1)

            def spread_terms(k, p, u):
                dve.wait_ge(k.s_rk_ps, p * 2 + u + 1)
                if after_pair(p):
                    dve.wait_ge(k.s_s2_ps, p * 8)
                    dve.wait_ge(k.s_bdk, p * 64)
                n = 2 * k.keys
                dve.tensor_tensor(k.ku[:, 2 * u:2 * u + 2, :], bank[DVE_BANK][:, :].rearrange("r (g n) -> r g n", g=2)[:, :, 0:n],
                                  kones[:, 2 * u:2 * u + 2].rearrange("r (g o) -> r g o", o=1).to_broadcast([P, 2, n]), ALU.add).then_inc(k.s_ku, 1)

            def values(k, p, u):
                dve.wait_ge(k.s_v_ps, p + 1)
                if after_pair(p):
                    dve.wait_ge(k.s_u_ps, p * 4)
                for_all = k.bv[0:k.keys, :].rearrange("n (o g c) -> n o g c", o=1, g=GROUPS).to_broadcast([k.keys, 2, GROUPS, 32])
                dve.tensor_tensor(k.vo[:, :, :, 0:32], bank[DVE_BANK][0:k.keys, 0:2 * P].rearrange("n (b g c) -> n b g c", b=2, g=GROUPS),
                                  for_all, ALU.add).then_inc(k.s_vo, 1)

            def scores(k, p, u):
                if after_pair(p):
                    dve.wait_ge(k.s_mm, (p - 1) * 2 + u + 1)
                for g in range(GROUPS):
                    dve.wait_ge(k.s_s1_ps, p * 8 + 4 * u + g + 1)
                    dve.tensor_reduce(k.nm[:, u, g, :], bank[SCORE[g % 2]][:, :].rearrange("q (j n) -> q j n", j=J)[:, :, 0:k.keys],
                                      AX.X, ALU.max, negate=True).then_inc(k.s_nm, 1)

            def shift(k, p, u):
                if after_pair(p):
                    dve.wait_ge(k.s_mt_ps, (p - 1) * 2 + u + 1)
                dve.wait_ge(k.s_nm, p * 8 + 4 * u + 4)
                nm = k.nm[:, u].rearrange("q g j -> q j g")
                dve.tensor_copy(k.mm[:, u, :, 0:4], nm).then_inc(k.s_mmh, 1)
                dve.wait_ge(k.s_mmh, p * 2 + u + 1)
                dve.tensor_tensor(k.mm[:, u, :, 4:8], nm, k.mm[:, u, :, 0:4].bitcast(F32), ALU.subtract).then_inc(k.s_mm, 1)

            def shift_rows(k, p, u):
                dve.wait_ge(k.s_mt_ps, p * 2 + u + 1)
                if after_pair(p):
                    dve.wait_ge(k.s_s2_ps, (p - 1) * 8 + 4 * u + 4)
                for j in (2, 3):
                    rows = slice(32 * j, 32 * j + 8)
                    src = bank[ACT_BANK][rows, 0:P].rearrange("r (o n) -> r o n", o=1).to_broadcast([8, GROUPS, P])
                    dve.tensor_copy(k.qm[rows, :, j, P * u:P * u + P], src).then_inc(k.s_shv, 1)

            def restore(k, p, u):
                if after_pair(p):
                    dve.wait_ge(k.s_on, (p - 1) * 4 + 2 * u + 2)
                    dve.wait_ge(k.s_ot_ps, (p - 1) * 2 + u + 1)
                for h in range(2):
                    dve.wait_ge(k.s_t_ps, p * 4 + 2 * u + h + 1)
                    t = bank[WEIGHED[h]][:, :]
                    sums = t.rearrange("q (j s r) -> q s j r", j=J, s=2)[:, :, :, 32]
                    dve.reciprocal(k.rd[:, u, h], sums).then_inc(k.s_rd, 1)
                    dve.wait_ge(k.s_rd, p * 4 + 2 * u + h + 1)
                    vals = bass.AP(t.tensor, t.offset, [list(t.ap[0]), [64, 2], [P + HD, J], [1, HD]])
                    dve.tensor_tensor(k.on[:, u, 64 * h:64 * h + 64].rearrange("q (s j d) -> q s j d", s=2, j=J), vals,
                                      k.rd[:, u, h].rearrange("q s (j o) -> q s j o", o=1).to_broadcast([P, 2, J, HD]), ALU.mult).then_inc(k.s_on, 1)

            def norm(k, p, u):
                n = p * 2 + u + 1
                dve.wait_ge(k.s_w_ps, n)
                dve.wait_ge(s_pool_setup, 4) if k.causal else dve.wait_ge(SA.s_xr, n)
                if after_pair(p):
                    dve.wait_ge(k.s_xn, n - 2)
                dve.tensor_tensor(k.y[:, u, :], bank[DVE_BANK][:, 0:D], residual[:, bass.ds(p * 2 + u, 1), :].rearrange("q o d -> q (o d)"), ALU.add).then_inc(k.s_y, 1)
                dve.wait_ge(k.s_y, n)
                dve.bn_stats(k.bs[:, u, :], k.y[:, u, :]).then_inc(k.s_bs, 1)
                dve.wait_ge(k.s_bs, n)
                if after_pair(p):
                    dve.wait_ge(k.s_ve, n - 2)
                dve.bn_aggr(k.ba[:, u, :], k.bs[:, u, :]).then_inc(k.s_ba, 1)
                dve.wait_ge(k.s_rs, n)
                dve.wait_ge(k.s_ba, n)
                if after_pair(p):
                    dve.wait_ge(k.s_xg, n - 2)
                dve.tensor_scalar(k.xn[:, u, :], k.y[:, u, :], k.ba[:, u, 0:1], k.rs[:, u:u + 1], ALU.subtract, ALU.mult).then_inc(k.s_xn, 1)

            done = [0]

            def routed(p, ins):
                done[0] = done[0] % ROUTER_OPS + 1
                ins.then_inc(r.s_rt, 1)
                dve.wait_ge(r.s_rt, p * ROUTER_OPS + done[0])

            def wide(t):
                return t[:, :].rearrange("q (v o) -> q v o", o=1).to_broadcast([P, 2, EXPERTS])

            def each(t):
                return t.rearrange("q (o e) -> q o e", o=1).to_broadcast([P, 2, EXPERTS])

            def gate(k, p, u):
                dve.wait_ge(r.s_lg_ps, p + 1)
                if after_pair(p):
                    dve.wait_ge(r.s_disp, p * 64)
                    dve.wait_ge(r.s_rank_ps, p)
                routed(p, dve.tensor_tensor(r.lg[:, :, :], bank[DVE_BANK][:, 0:2 * EXPERTS].rearrange("q (v e) -> q v e", v=2), each(rb), ALU.add))
                routed(p, dve.tensor_reduce(r.nmx[:, :], r.lg[:, :, :], AX.X, ALU.max, negate=True))
                routed(p, dve.tensor_tensor(r.ls[:, :, :], r.lg[:, :, :], wide(r.nmx), ALU.add))

            def choose(k, p, u):
                dve.wait_ge(r.s_exp, p * 2 + 1)
                routed(p, dve.tensor_reduce(r.sm[:, :], r.exl[:, :, :], AX.X, ALU.add))
                routed(p, dve.reciprocal(r.rsm[:, :], r.sm[:, :]))
                routed(p, dve.tensor_tensor(r.p[:, :, :], r.exl[:, :, :], wide(r.rsm), ALU.mult))
                for prob, best, eq, key, km, oh in ((r.p, r.p1, r.eq, r.key, r.km, r.oh1), (r.pm, r.p2, r.eq2, r.key2, r.km2, r.oh2)):
                    if oh is r.oh2:
                        routed(p, dve.scalar_tensor_tensor(out=r.pm[:, :, :], in0=r.oh1[:, :, :], scalar=-2.0, in1=r.p[:, :, :], op0=ALU.mult, op1=ALU.add))
                    routed(p, dve.tensor_reduce(best[:, :], prob[:, :, :], AX.X, ALU.max))
                    routed(p, dve.tensor_tensor(eq[:, :, :], prob[:, :, :], wide(best), ALU.is_equal))
                    routed(p, dve.tensor_tensor(key[:, :, :], eq[:, :, :], each(falling), ALU.mult))
                    routed(p, dve.tensor_reduce(km[:, :], key[:, :, :], AX.X, ALU.max))
                    routed(p, dve.tensor_tensor(oh[:, :, :], each(falling), wide(km), ALU.is_equal))
                routed(p, dve.tensor_tensor(r.sel[:, :, :], r.oh1[:, :, :], r.oh2[:, :, :], ALU.add))
                assert done[0] == SELECTED, done[0]
                routed(p, dve.tensor_tensor(r.d[:, :], r.p2[:, :], r.p1[:, :], ALU.subtract))

            def place(k, p, u):
                dve.wait_ge(r.s_exp, p * 2 + 2)
                routed(p, dve.tensor_scalar(r.den[:, :], r.ed[:, :], 1.0, None, ALU.add))
                routed(p, dve.reciprocal(r.w1[:, :], r.den[:, :]))
                tile = lambda c, col: xe[:, bass.ds(p * 2, 2), c, col].rearrange("q v -> q v")
                routed(p, dve.tensor_tensor(tile(1, ROW - 1), r.ed[:, :], r.w1[:, :], ALU.mult))
                routed(p, dve.tensor_copy(tile(0, ROW - 1), r.w1[:, :]))
                dve.wait_ge(r.s_rank_ps, p + 1)
                routed(p, dve.tensor_tensor(r.base[:, :, :], bank[DVE_BANK][:, 0:2 * EXPERTS].rearrange("q (v e) -> q v e", v=2), each(region), ALU.add))
                assert done[0] == SELECTED + 6, done[0]
                routed(p, dve.tensor_tensor(r.t1[:, :, :], r.base[:, :, :], r.oh1[:, :, :], ALU.mult))
                routed(p, dve.tensor_tensor(r.t2[:, :, :], r.base[:, :, :], r.oh2[:, :, :], ALU.mult))
                routed(p, dve.tensor_reduce(r.pos[:, 0, :], r.t1[:, :, :], AX.X, ALU.add))
                routed(p, dve.tensor_reduce(r.pos[:, 1, :], r.t2[:, :, :], AX.X, ALU.add))
                routed(p, dve.tensor_tensor(r.acc[:, :], r.acc[:, :], r.sel[:, 0, :], ALU.add))
                routed(p, dve.tensor_tensor(r.acc[:, :], r.acc[:, :], r.sel[:, 1, :], ALU.add))
                routed(p, dve.tensor_copy(r.row[:, bass.ds(p * 2, 2), :], r.pos[:, :, :].rearrange("q c v -> q v c")))
                assert done[0] == ROUTER_OPS, done[0]

            dve.wait_ge(s_late, 48)
            dve.wait_ge(s_zero, 4)
            dve.wait_ge(s_rows, 16)
            dve.tensor_copy(xe[:, :, :, P:P + 1].rearrange("q b c o -> q b (c o)").bitcast(I32), rows_sb[:, :, :]).then_inc(s_rows, 1)
            dve.wait_ge(s_pool_ones, 2)
            dve.wait_ge(s_setup, SETUP)
            iterations({"gate": gate, "choose": choose, "place": place, "turn": turn, "project": project, "spread_terms": spread_terms, "values": values, "scores": scores, "shift": shift, "shift_rows": shift_rows, "restore": restore, "norm": norm})

            tables = [0]

            def listed(ins):
                tables[0] += 1
                ins.then_inc(s_table, 1)
                dve.wait_ge(s_table, tables[0])

            row0 = lambda t, a, b, inner=True: (t.rearrange("q (o n) -> q o n", o=1) if inner else t.rearrange("q (n o) -> q n o", o=1)).to_broadcast([1, a, b])
            dve.wait_ge(s_counts, 1)
            listed(dve.tensor_copy(tb.count[:, :], bank[DVE_BANK][0:1, 0:EXPERTS]))
            listed(dve.tensor_tensor(tb.full[:, :, :], row0(tb.count[:, :], EXPERTS, T_ALL // P, False), row0(tile_starts[0:1], EXPERTS, T_ALL // P), ALU.is_gt))
            listed(dve.tensor_reduce(tb.tiles[:, :], tb.full[:, :, :], AX.X, ALU.add))
            listed(dve.tensor_tensor(tb.before[:, :, :], row0(tb.tiles[:, :], E9, EXPERTS), below[0:1].rearrange("q (a b) -> q a b", a=E9), ALU.mult))
            listed(dve.tensor_reduce(tb.first[:, :], tb.before[:, :, :], AX.X, ALU.add))
            listed(dve.tensor_tensor(tb.past[:, :, :], row0(slot_no[0:1], SLOTS, EXPERTS, False), row0(tb.first[:, 1:E9], SLOTS, EXPERTS), ALU.is_ge))
            listed(dve.tensor_reduce(tb.expert[:, :], tb.past[:, :, :], AX.X, ALU.add))
            listed(dve.tensor_scalar(slot_expert_i[:, :], tb.expert[:, :], float(EXPERTS - 1), None, ALU.min))
            listed(dve.scalar_tensor_tensor(out=tb.shift[:, :], in0=tb.first[:, :], scalar=-float(P), in1=region9[0:1], op0=ALU.mult, op1=ALU.add))
            listed(dve.tensor_tensor(tb.one[:, :, :], row0(tb.expert[:, :], SLOTS, E9, False), row0(expert_no[0:1], SLOTS, E9), ALU.is_equal))
            listed(dve.tensor_tensor(tb.prod[:, :, :], tb.one[:, :, :], row0(tb.shift[:, :], SLOTS, E9), ALU.mult))
            listed(dve.tensor_reduce(tb.start[:, :], tb.prod[:, :, :], AX.X, ALU.add))
            listed(dve.tensor_tensor(slot_row_i[:, :], tb.start[:, :], slot_rows[0:1], ALU.add))
            assert tables[0] == TABLE_OPS

            dve.wait_ge(s_weights, 16 * (EXPERTS + 4))

            def turned(i, v):
                n, b = i * AHEAD + v, v % 2
                dve.wait_ge(s_xst_ps, n + 1)
                if after_pair(i) or v >= 2:
                    dve.wait_ge(s_h_ps, (n - 2) * 2 + 2)
                dve.tensor_copy(xsT[b][:, :], bank[6 + b][:, 0:P]).then_inc(s_xst, 1)

            def gated(i, v):
                n, b = i * AHEAD + v, v % 2
                expert = dve.value_load(slot_expert_i[0:1, bass.ds(n, 1)], min_val=0, max_val=EXPERTS - 1)
                dve.wait_ge(s_o_ps, n + 1)
                if after_pair(i) or v >= 2:
                    dve.wait_ge(s_ys, n - 1)
                if after_pair(i):
                    dve.wait_ge(s_scatter[v], i * 16)
                dve.tensor_tensor(yb[b][:, :], bank[4 + b][:, 0:D], b2[:, bass.ds(expert, 1), :].rearrange("q o d -> q (o d)"), ALU.add).then_inc(s_yb, 1)
                dve.wait_ge(s_yb, n + 1)
                dve.tensor_scalar(ys[v], yb[b][:, :], xs[v][:, ROW - 1:ROW], None, ALU.mult).then_inc(s_ys, 1)

            turned(0, 0)
            for i, v in slots(dve):
                if v < AHEAD - 1:
                    turned(i, v + 1)
                elif i < SLOTS // AHEAD - 1:
                    turned(i + 1, 0)
                gated(i, v)

            for q in range(TAIL):
                t = slice(TN * q, TN * q + TN)
                dve.wait_ge(s_yy[q], 32)
                dve.tensor_tensor(y3[:, t, :], yy[0][:, t, :], xe[:, t, 0, 0:D], ALU.add).then_inc(s_y3a, 1)
                dve.wait_ge(s_y3a, q + 1)
                dve.tensor_tensor(y3[:, t, :], y3[:, t, :], yy[1][:, t, :], ALU.add).then_inc(s_y3, 1)
                dve.wait_ge(s_y3, q + 1)
                for b in range(TN * q, TN * q + TN):
                    dve.bn_stats(bs3[:, b, :], y3[:, b, :]).then_inc(s_bs3, 1)
                for b in range(TN * q, TN * q + TN):
                    dve.wait_ge(s_bs3, b + 1)
                    dve.bn_aggr(ba3[:, b, :], bs3[:, b, :]).then_inc(s_ba3, 1)
                dve.wait_ge(s_rs3, q + 1)
                for b in range(TN * q, TN * q + TN):
                    dve.wait_ge(s_ba3, b + 1)
                    dve.tensor_scalar(y3[:, b, :], y3[:, b, :], ba3[:, b, 0:1], rs3[:, b:b + 1], ALU.subtract, ALU.mult).then_inc(s_xn3, 1)
                dve.wait_ge(s_xn3, TN * (q + 1))
                dve.tensor_tensor(y3[:, t, :], y3[:, t, :], g3[:, :].rearrange("q (o d) -> q o d", o=1).to_broadcast([P, TN, D]), ALU.mult).then_inc(s_g3, 1)
                dve.wait_ge(s_g3, q + 1)
                dve.tensor_tensor(o3[:, t, :], y3[:, t, :], beta3[:, :].rearrange("q (o d) -> q o d", o=1).to_broadcast([P, TN, D]), ALU.add).then_inc(s_o3, TN)

        @block.gpsimd
        def _(pool):
            for k in KINDS:
                pool.memset(k.qm[:, :, :, :].bitcast(F32), 0.0).then_inc(s_zero, 1)
                pool.memset(k.km[:, :, :, :].bitcast(F32), 0.0).then_inc(s_zero, 1)
            pool.memset(half[:, :], -0.5).then_inc(s_pool_setup, 1)
            pool.wait_ge(s_const, 16 * 22)
            pool.tensor_tensor(residual, residual, SA.bo[:, :].rearrange("p (o d) -> p o d", o=1).to_broadcast([P, B, D]), ALU.add).then_inc(s_pool_setup, 3)

            def weights(k, p, u):
                if not k.causal:
                    return
                for g in range(GROUPS):
                    n = p * 8 + 4 * u + g + 1
                    pool.wait_ge(k.s_ex, n)
                    blockg = k.pt[u][:, 512 * g:512 * g + 512]
                    pool.affine_select(out=blockg, in_=blockg, compare_op=ALU.is_ge, fill=0.0, base=0,
                                       pattern=[[0, J], [1, P]], channel_multiplier=-1).then_inc(k.s_pm, 1)

            def norm(k, p, u):
                n = p * 2 + u + 1
                pool.wait_ge(k.s_ba, n)
                if after_pair(p):
                    pool.wait_ge(k.s_xn, n - 2)
                pool.tensor_scalar(k.ve[:, u:u + 1], k.ba[:, u, 1:2], EPS, None, ALU.add).then_inc(k.s_ve, 1)
                pool.wait_ge(k.s_ve, n)
                pool.tensor_tensor(k.rs[:, u:u + 1], k.ve[:, u:u + 1], half[:, :], ALU.pow).then_inc(k.s_rs, 1)
                pool.wait_ge(k.s_xn, n)
                if after_pair(p):
                    pool.wait_ge(k.s_x1, n - 2)
                pool.tensor_tensor(k.xg[:, u, :], k.xn[:, u, :], k.g[:, :], ALU.mult).then_inc(k.s_xg, 1)
                pool.wait_ge(k.s_xg, n)
                if after_pair(p):
                    pool.wait_ge(CA.s_xt_ps, p) if k.causal else pool.wait_ge(r.s_xt_ps, p)
                    if not k.causal:
                        pool.wait_ge(r.s_xe1, p)
                    pool.wait_ge(k.s_xr, n - 2)
                pool.tensor_tensor(k.x1[:, u, :], k.xg[:, u, :], k.b[:, :], ALU.add).then_inc(k.s_x1, 1)
                pool.wait_ge(k.s_x1, n)
                if k.causal:
                    pool.tensor_tensor(residual[:, bass.ds(p * 2 + u, 1), :].rearrange("q o d -> q (o d)"), k.x1[:, u, :], CA.bo[:, :], ALU.add).then_inc(k.s_xr, 1)
                else:
                    pool.tensor_copy(xe[:, bass.ds(p * 2 + u, 1), 0, 0:D].rearrange("q o d -> q (o d)"), k.x1[:, u, :]).then_inc(k.s_xr, 1)

            def place(k, p, u):
                pool.wait_ge(r.s_rt, p * ROUTER_OPS + ROUTER_OPS)
                pool.wait_ge(r.s_xe1, p + 1)
                pool.wait_ge(CA.s_xr, p * 2 + 2)
                for v in range(2):
                    for c in range(TOPK):
                        pool.indirect_dma_start(out=dispatched, out_offset=bass.IndirectOffsetOnAxis(ap=r.row[:, 2 * p + v, c:c + 1], axis=0),
                                                in_=xe[:, 2 * p + v, c, :], in_offset=None).then_inc(r.s_disp, 16)

            pool.wait_ge(s_filled, 16 * (EXPERTS + 1))
            pool.wait_ge(s_rows, 17)
            iterations({"place": place, "weights": weights, "norm": norm})

            for i, v in slots(pool):
                pool.wait_ge(s_ys, i * AHEAD + v + 1)
                pool.indirect_dma_start(out=results, out_offset=bass.IndirectOffsetOnAxis(ap=xs[v][:, P:P + 1].bitcast(I32), axis=0),
                                        in_=ys[v], in_offset=None, bounds_check=TOPK * T_ALL - 1, oob_is_err=False).then_inc(s_scatter[v], 16)
            for q in range(TAIL):
                pool.wait_ge(s_ba3, TN * (q + 1))
                t = slice(TN * q, TN * q + TN)
                pool.tensor_scalar(ve3[:, t], ba3[:, t, 1], EPS, None, ALU.add).then_inc(s_ve3, 1)
                pool.wait_ge(s_ve3, q + 1)
                pool.tensor_tensor(rs3[:, t], ve3[:, t], half[:, :].to_broadcast([P, TN]), ALU.pow).then_inc(s_rs3, 1)


NAMES = ("wq", "wk", "wv", "wo", "bq", "bk", "bv", "bo")


def kernel(**inputs):
    import concourse.bacc as bacc
    from concourse.bass_utils import run_bass_kernel_spmd

    nc = bacc.Bacc("TRN2", target_bir_lowering=False, num_devices=1)
    arrays = {}

    def given(name, a):
        a = np.ascontiguousarray(a)
        arrays[f"in_{name}"] = a
        return nc.dram_tensor(f"in_{name}", a.shape, mybir.dt.from_np(a.dtype), kind="ExternalInput").ap()

    x, ctx = given("x", inputs["x"]), given("ctx", inputs["ctx_1024"])
    layer = lambda name: given(name, inputs["L0_xattn_" + name])
    sa, ca = ({n: layer(f"{a}_{n}") for n in NAMES} | {"g": layer(f"{l}_g"), "b": layer(f"{l}_b")} for a, l in (("sa", "ln1"), ("ca", "ln2")))
    moe = dict(rw=layer("router_w"), rb=layer("router_b"), w1=layer("e_w1"), b1=layer("e_b1"), w2=layer("e_w2"), b2=layer("e_b2"))
    ln3 = dict(g=layer("ln3_g"), b=layer("ln3_b"))
    tokens = x.shape[0] * x.shape[1]
    consts = given("shape_constants", shape_constants())
    expert_consts = given("expert_constants", expert_constants(tokens, slot_count(tokens)))
    rows = given("result_rows", result_rows(x.shape[0]))
    out = nc.dram_tensor("out", x.shape, F32, kind="ExternalOutput").ap()
    build(nc, x, ctx, sa, ca, moe, ln3, out, consts, expert_consts, rows)
    return run_bass_kernel_spmd(nc, [arrays], core_ids=[0]).results[0]["out"]
```

```python
from contextlib import ExitStack

import numpy as np
import concourse.bass as bass
from concourse import mybir

F32, F32R, BF16, I32 = mybir.dt.float32, mybir.dt.float32r, mybir.dt.bfloat16, mybir.dt.int32
ALU, ACT, AX = mybir.AluOpType, mybir.ActivationFunctionType, mybir.AxisListType

P = 128
HEADS, HD = 16, 8
GROUPS, J = 4, 4
EPS = 1e-5
EXPERTS, TOPK = 8, 2
CONSTS = 3 * P + GROUPS
SLOTS_A_ROUND = 8
ROW = P + 2


class Attention:

    def __init__(self, name, keys, w):
        self.name, self.keys, self.w = name, keys, w
        self.kpad = keys + keys % 2
        self.causal = name == "sa"


class Router:
    pass


class SlotTable:
    pass


def shape_constants():
    row = np.arange(P)
    c = np.zeros((P, CONSTS), np.float32)
    c[:, 0:P] = np.eye(P)
    c[:, P:2 * P] = np.where(row[None, :] > row[:, None], -1e30, 0.0)
    c[:, 2 * P:3 * P] = row[:, None] < row[None, :]
    for g in range(GROUPS):
        c[:, 3 * P + g] = (row % 32 < 8) & (row % GROUPS == g)
    return c


def expert_constants(tokens, slots):
    e, e9, m, s = np.arange(EXPERTS), np.arange(EXPERTS + 1), np.arange(tokens // P), np.arange(slots)
    parts = [EXPERTS - e, e * tokens, m * P, (e[None, :] < e9[:, None]).ravel(), s, e9, e9 * tokens, s * P]
    return np.tile(np.concatenate(parts).astype(np.float32)[None, :], (P, 1))


def result_rows(batch):
    p, b, c = np.ogrid[:P, :batch, :TOPK]
    return (c * batch * P + b * P + p).astype(np.int32)


def slot_count(tokens):
    n = (TOPK * tokens + EXPERTS * (P - 1)) // P
    return -(-n // SLOTS_A_ROUND) * SLOTS_A_ROUND


def build(nc, x, ctx_1024, sa, ca, moe, out, consts, expert_consts, rows_of_results):
    B, S, D = x.shape
    T_ALL = B * S
    F = moe["w1"].shape[2]
    FC = F // P
    SLOTS = slot_count(T_ALL)
    SC = ctx_1024.shape[1]
    PAIRS = B // 2
    SCALE = float(HD) ** -0.5

    stack = ExitStack()
    with stack:
        def sb(name, shape, dt=F32):
            return stack.enter_context(nc.sbuf_tensor(name, shape, dt))

        def sem(name):
            return stack.enter_context(nc.semaphore(name))

        bank = [stack.enter_context(nc.psum_tensor(f"bank{n}", [P, 512], F32)) for n in range(8)]
        SCORE, SHIFTED, WEIGHED, ACT_BANK, DVE_BANK = (0, 1), (2, 3), (4, 5), 6, 7

        cst = sb("cst", [P, CONSTS])
        ident, kones = cst[:, 0:P], cst[:, 3 * P:3 * P + GROUPS]
        ident_bf = sb("ident_bf", [P, P], BF16)
        causal_bf = sb("causal_bf", [P, P], BF16)
        half = sb("half", [P, 1])
        spread = {n: sb(f"spread_{n}", [P, GROUPS, J, 4, HD], F32R) for n in ("hq", "lq", "hk", "lk")}
        ones = sb("ones", [P, P])
        ecst = sb("ecst", [P, expert_consts.shape[1]])
        cut = np.cumsum([0, EXPERTS, EXPERTS, T_ALL // P, (EXPERTS + 1) * EXPERTS, SLOTS, EXPERTS + 1, EXPERTS + 1, SLOTS])
        falling, region, tile_starts, below, slot_no, expert_no, region9, slot_rows = (
            ecst[:, int(a):int(b)] for a, b in zip(cut[:-1], cut[1:]))
        residual = sb("residual", [P, B, D])
        rw = sb("router_w", [D, EXPERTS])
        late_rows = sb("late_rows", [P, EXPERTS + EXPERTS * D + 2 * D])
        rb, g3, beta3 = late_rows[:, 0:EXPERTS], late_rows[:, EXPERTS * (D + 1):EXPERTS * (D + 1) + D], late_rows[:, EXPERTS * (D + 1) + D:]
        b2 = late_rows[:, EXPERTS:EXPERTS * (D + 1)].rearrange("p (e d) -> p e d", e=EXPERTS)
        b1_rows, b1 = sb("b1_rows", [EXPERTS * FC, P]), sb("expert_b1", [P, EXPERTS * FC])
        dispatched = nc.dram_tensor("dispatched", [(EXPERTS + 1) * T_ALL, ROW], F32).ap()
        results = nc.dram_tensor("results", [TOPK * T_ALL, D], F32).ap()
        r = RT = Router()
        r.xT = sb("r_xT", [D, 2 * P])
        r.lg, r.ls, r.exl, r.p, r.eq, r.key, r.oh1, r.pm, r.eq2, r.key2, r.oh2, r.sel, r.base, r.t1, r.t2 = (
            sb(f"r_by_expert{n}", [P, 2, EXPERTS]) for n in range(15))
        r.nmx, r.sm, r.rsm, r.p1, r.km, r.p2, r.km2, r.d, r.ed, r.den, r.w1 = (
            sb(f"r_by_token{n}", [P, 2]) for n in range(11))
        r.pos = sb("r_pos", [P, TOPK, 2])
        r.sent = sb("r_sent", [P, 2, TOPK, ROW])
        r.row = sb("r_row", [P, 2, TOPK], I32)
        r.acc = sb("r_acc", [P, EXPERTS])
        r.s_xt_ps = sem("r_xt_ps")
        r.s_xT = sem("r_xT")
        r.s_xe1 = sem("r_xe1")
        r.s_lg_ps = sem("r_lg_ps")
        r.s_rt = sem("r_rt")
        r.s_exp = sem("r_exp")
        r.s_rank_ps = sem("r_rank_ps")
        r.s_disp = sem("r_disp")
        s_fill, s_filled, s_late = sem("fill"), sem("filled"), sem("late")
        s_spare, s_residual = sem("spare"), sem("residual_loaded")
        s_const = sem("s_const")
        s_setup, s_pool_setup = sem("s_setup"), sem("s_pool_setup")

        def kind(name, keys, w, g, b, bo_next):
            k = Attention(name, keys, w)
            t = lambda n, shape, dt=F32: sb(f"{name}_{n}", shape, dt)
            k.square = t("square", [D, 4 * D + 2])
            k.wq, k.wk, k.wv, k.wo = (k.square[:, n * D:(n + 1) * D] for n in range(4))
            k.bq, k.bk = (k.square[:, 4 * D + n:4 * D + n + 1] for n in range(2))
            k.rows = t("rows", [P, 4 * D])
            k.bv, k.bo, k.g, k.b = (k.rows[:, n * D:(n + 1) * D] for n in range(4))
            k.s_const, k.s_zero = sem(f"{name}_const"), sem(f"{name}_zero")
            k.xin = t("xin", [P, 2, D])
            k.xT = t("xT", [D, 2 * P])
            if not k.causal:
                k.cin, k.cT = t("cin", [keys, 2, D]), t("cT", [D, 2 * keys])
            k.hq, k.lq, k.hk, k.lk = (t(n, [P, 2 * P], F32R) for n in ("hq", "lq", "hk", "lk"))
            k.qu = t("qu", [P, GROUPS, 2 * P], F32R)
            k.ku = t("ku", [P, GROUPS, 2 * keys], F32R)
            k.qm = t("qm", [P, GROUPS, J, 2 * P], F32R)
            k.km = t("km", [P, GROUPS, J, 2 * k.kpad], F32R)
            k.vo = t("vo", [keys, 2, GROUPS, 64])
            k.nm = t("nm", [P, 2, GROUPS, J])
            k.mm = t("mm", [P, 2, J, 32], F32R)
            k.pt_all = t("pt", [P, 2 * GROUPS * 512])
            k.pt = [k.pt_all[0:keys, u * GROUPS * 512:(u + 1) * GROUPS * 512] for u in range(2)]
            k.us = [t(f"us{u}", [P, 2, 512]) for u in range(2)]
            k.rd = t("rd", [P, 2, 2, 2, J])
            k.on, k.oT, k.y, k.xn, k.xg = (t(n, [P, 2, D]) for n in ("on", "oT", "y", "xn", "xg"))
            k.bs, k.ba, k.ve, k.rs = t("bs", [P, 2, 6]), t("ba", [P, 2, 2]), t("ve", [P, 2]), t("rs", [P, 2])
            k.x1 = t("x1", [P, 2, D])
            k.s_ld = sem(f"{name}_ld")
            k.s_xt_ps = sem(f"{name}_xt_ps")
            k.s_xt = sem(f"{name}_xt")
            k.s_ct_ps = sem(f"{name}_ct_ps")
            k.s_ct = sem(f"{name}_ct")
            k.s_c_ps = sem(f"{name}_c_ps")
            k.s_hi = sem(f"{name}_hi")
            k.s_lo = sem(f"{name}_lo")
            k.s_rq_ps = sem(f"{name}_rq_ps")
            k.s_rk_ps = sem(f"{name}_rk_ps")
            k.s_qu = sem(f"{name}_qu")
            k.s_ku = sem(f"{name}_ku")
            k.s_v_ps = sem(f"{name}_v_ps")
            k.s_vo = sem(f"{name}_vo")
            k.s_bdq = sem(f"{name}_bdq")
            k.s_bdk = sem(f"{name}_bdk")
            k.s_s1_ps = sem(f"{name}_s1_ps")
            k.s_nm = sem(f"{name}_nm")
            k.s_mmh = sem(f"{name}_mmh")
            k.s_mm = sem(f"{name}_mm")
            k.s_mt_ps = sem(f"{name}_mt_ps")
            k.s_sha = sem(f"{name}_sha")
            k.s_shv = sem(f"{name}_shv")
            k.s_s2_ps = sem(f"{name}_s2_ps")
            k.s_ex = sem(f"{name}_ex")
            k.s_pm = sem(f"{name}_pm")
            k.s_u_ps = sem(f"{name}_u_ps")
            k.s_us = sem(f"{name}_us")
            k.s_t_ps = sem(f"{name}_t_ps")
            k.s_rd = sem(f"{name}_rd")
            k.s_on = sem(f"{name}_on")
            k.s_ot_ps = sem(f"{name}_ot_ps")
            k.s_ot = sem(f"{name}_ot")
            k.s_w_ps = sem(f"{name}_w_ps")
            k.s_y = sem(f"{name}_y")
            k.s_bs = sem(f"{name}_bs")
            k.s_ba = sem(f"{name}_ba")
            k.s_ve = sem(f"{name}_ve")
            k.s_rs = sem(f"{name}_rs")
            k.s_xn = sem(f"{name}_xn")
            k.s_xg = sem(f"{name}_xg")
            k.s_x1 = sem(f"{name}_x1")
            k.s_xr = sem(f"{name}_xr")
            return k

        SA = kind("sa", S, sa, None, None, None)
        CA = kind("ca", SC, ca, None, None, None)
        KINDS = (SA, CA)
        filler = sb("filler", [P, 2, ROW])
        w2 = SA.pt_all[:, :].rearrange("p (e c d) -> p e c d", e=EXPERTS, c=FC)
        ROUTER_OPS = 32
        SELECTED = 18
        tb = SlotTable()
        TABLE_OPS = 13
        E9 = EXPERTS + 1
        tb.count, tb.tiles, tb.first, tb.shift, tb.expert, tb.start = (
            sb(f"tb_row{n}", [1, size]) for n, size in enumerate((EXPERTS, EXPERTS, E9, E9, SLOTS, SLOTS)))
        tb.full, tb.before, tb.past, tb.one, tb.prod = (
            sb(f"tb_square{n}", [1, a, b]) for n, (a, b) in enumerate(((EXPERTS, T_ALL // P), (E9, EXPERTS), (SLOTS, EXPERTS), (SLOTS, E9), (SLOTS, E9))))
        s_table, s_weights, s_counts, s_b1 = sem("table"), sem("expert_weights"), sem("counts"), sem("b1")
        slot_expert_i, slot_row_i = sb("slot_expert", [1, SLOTS], I32), sb("slot_row", [1, SLOTS], I32)
        rows_sb = sb("rows_sb", [P, B, TOPK], I32)
        AHEAD, W_AHEAD = SLOTS_A_ROUND, 4
        ROUNDS = SLOTS // AHEAD
        xs = [sb(f"xs{v}", [P, ROW]) for v in range(AHEAD)]
        w1 = [CA.pt_all[:, v * F:(v + 1) * F] for v in range(W_AHEAD)]
        xsT = [sb(f"xsT{v}", [D, P]) for v in range(2)]
        hid = [SA.us[v][:, 0, :].rearrange("p (c n) -> p c n", c=FC) for v in range(2)]
        yb = [sb(f"yb{v}", [P, D]) for v in range(2)]
        ys = [CA.pt_all[:, W_AHEAD * F + v * D:W_AHEAD * F + (v + 1) * D] for v in range(AHEAD)]
        s_xs, s_scatter = ([sem(f"{n}{v}") for v in range(AHEAD)] for n in ("xs", "scatter"))
        s_w1 = [sem(f"w1_{v}") for v in range(W_AHEAD)]
        s_xst_ps, s_xst, s_h_ps, s_gelu, s_o_ps, s_yb, s_ys = (sem("m_" + n) for n in "xst_ps xst h_ps gelu o_ps yb ys".split())
        TN = 4
        TAIL = B // TN
        yy = [CA.pt_all[:, c * B * D:(c + 1) * B * D].rearrange("p (b d) -> p b d", b=B) for c in range(2)]
        y3, o3 = yy
        bs3, ba3, ve3, rs3 = sb("bs3", [P, B, 6]), sb("ba3", [P, B, 2]), sb("ve3", [P, B]), sb("rs3", [P, B])
        s_yy = [sem(f"yy{q}") for q in range(TAIL)]
        s_y3a, s_y3, s_bs3, s_ba3, s_ve3, s_rs3, s_xn3, s_g3, s_o3 = (sem("t_" + n) for n in "y3a y3 bs3 ba3 ve3 rs3 xn3 g3 o3".split())
        s_out, s_spread0, s_pool_ones = sem("s_out"), sem("s_spread0"), sem("pool_ones")
        SETUP = 14

        block = stack.enter_context(nc.Block())

        def after_pair(p):
            return not isinstance(p, int) or p > 0

        ORDER = [
            (CA, "norm", 1, -2), (CA, "project", 0, -1), (SA, "shift", 0, 0), (SA, "shift_rows", 0, 0),
            (SA, "scores", 1, 0), (RT, "route", 0, -2), (RT, "gate", 0, -2), (CA, "spread_terms", 0, -1),
            (CA, "spread_terms", 1, -1), (SA, "weights", 0, 0), (SA, "shift", 1, 0), (SA, "shift_rows", 1, 0),
            (SA, "mix", 0, 0), (SA, "weights", 1, 0), (RT, "choose", 0, -2), (CA, "values", 0, -1),
            (SA, "restore", 0, 0), (CA, "scores", 0, -1), (SA, "turn_heads", 0, 0), (CA, "scores", 1, -1),
            (CA, "shift", 0, -1), (CA, "shift_rows", 0, -1), (RT, "place", 0, -2), (SA, "mix", 1, 0),
            (SA, "turn", 0, 1), (CA, "shift", 1, -1), (CA, "shift_rows", 1, -1), (SA, "restore", 1, 0),
            (SA, "project", 0, 1), (SA, "spread_terms", 0, 1), (CA, "weights", 0, -1), (SA, "turn_heads", 1, 0),
            (CA, "mix", 0, -1), (SA, "norm", 0, 0), (SA, "spread_terms", 1, 1), (CA, "restore", 0, -1),
            (CA, "weights", 1, -1), (SA, "values", 0, 1), (SA, "norm", 1, 0), (CA, "mix", 1, -1),
            (SA, "scores", 0, 1), (CA, "turn_heads", 0, -1), (CA, "restore", 1, -1), (CA, "norm", 0, -1),
            (RT, "fill", 0, -1), (CA, "turn_heads", 1, -1), (CA, "turn", 0, 0)]

        def iteration(i, steps):
            for k, step, u, ahead in ORDER:
                if not isinstance(i, int) or 0 <= i + ahead < PAIRS:
                    if step in steps:
                        steps[step](k, i + ahead, u)

        FIRST_ITERATION, LAST_ITERATION = -max(o[3] for o in ORDER), PAIRS - 1 - min(o[3] for o in ORDER)

        def iterations(steps, begin=lambda i: None, end=lambda: None):
            for i in range(FIRST_ITERATION, LAST_ITERATION + 1):
                begin(i)
                iteration(i, steps)
                end()

        def slots(engine, *stages):
            def one_round(i, last=False):
                for v in range(AHEAD):
                    for stage, lead in stages:
                        if v + lead < AHEAD or not last:
                            stage(i + (v + lead) // AHEAD, (v + lead) % AHEAD)

            for stage, lead in stages:
                for v in range(lead):
                    stage(0, v)
            one_round(0)
            with engine.Fori(1, ROUNDS - 1) as i:
                one_round(i)
            one_round(ROUNDS - 1, last=True)

        @block.sync
        def _(sp):
            def load_rows(k, p):
                if k.causal:
                    sp.dma_start(k.xin[:, :, :], x[bass.ds(p * 2, 2)].rearrange("b p d -> p b d")).then_inc(k.s_ld, 16)
                else:
                    sp.dma_start(k.cin[:, :, :], ctx_1024[bass.ds(p * 2, 2)].rearrange("b p d -> p b d")).then_inc(k.s_ld, 16)

            sp.dma_start(cst[:, :], consts).then_inc(s_const, 16)
            for k in KINDS:
                sp.dma_start(k.square[:, :], k.w["square"]).then_inc(k.s_const, 16)
                if k.causal:
                    load_rows(k, 0)
                sp.dma_start(k.rows[:, :], k.w["rows"].rearrange("(o d) -> o d", o=1).to_broadcast([P, 4 * D])).then_inc(k.s_const, 16)
            sp.dma_start(residual[:, :, :], x.rearrange("b p d -> p b d")).then_inc(s_residual, 16)
            def turn(k, p, u):
                if after_pair(p):
                    sp.wait_ge(k.s_xt_ps if k.causal else k.s_ct_ps, p)
                if after_pair(p) or not k.causal:
                    load_rows(k, p)

            def fill(k, p, u):
                if after_pair(p):
                    sp.wait_ge(r.s_disp, p * 64)
                for e in (0, EXPERTS // 2):
                    regions = dispatched.rearrange("(e p q n) w -> p q e (n w)", e=EXPERTS + 1, q=P, n=2)
                    sp.dma_start(regions[bass.ds(p, 1), :, e:e + EXPERTS // 2].rearrange("o q e w -> (o q) e w"),
                                 filler[:, :, :].rearrange("q (o n) w -> q o (n w)", o=1).to_broadcast([P, EXPERTS // 2, 2 * ROW])).then_inc(s_filled, 16)

            def spread_terms(k, p, u):
                if u == 0:
                    return
                if not after_pair(p):
                    sp.wait_ge(k.s_zero, 2)
                sp.wait_ge(k.s_ku, p * 2 + 2)
                if after_pair(p):
                    sp.wait_ge(k.s_s1_ps, p * 8)
                for j in range(J):
                    rows = slice(32 * j + 8, 32 * j + 32)
                    sp.dma_start(k.km[rows, :, j, 0:2 * k.keys].bitcast(F32), k.ku[rows, :, :].bitcast(F32)).then_inc(k.s_bdk, 16)
                sp.wait_ge(k.s_qu, p * 2 + 2)
                if after_pair(p):
                    sp.wait_ge(k.s_s2_ps, p * 8)
                for j in range(J):
                    rows = slice(32 * j + 8, 32 * j + 32)
                    sp.dma_start(k.qm[rows, :, j, :].bitcast(F32), k.qu[rows, :, :].bitcast(F32)).then_inc(k.s_bdq, 16)

            sp.dma_start(rw[:, :], moe["rw"]).then_inc(s_late, 16)
            sp.dma_start(late_rows[:, :], moe["rows"].rearrange("(o d) -> o d", o=1).to_broadcast([P, late_rows.shape[1]])).then_inc(s_late, 16)
            sp.dma_start(ecst[:, :], expert_consts).then_inc(s_late, 16)
            sp.dma_start(rows_sb[:, :, :], rows_of_results).then_inc(s_late, 16)
            sp.dma_start(b1_rows[:, :], moe["b1"].rearrange("e (c f) -> (e c) f", c=FC)).then_inc(s_weights, 16)
            sp.wait_ge(s_fill, 1)
            SPARE = SLOTS * P - TOPK * T_ALL
            sp.dma_start(dispatched[EXPERTS * T_ALL:EXPERTS * T_ALL + SPARE].rearrange("(q o n) w -> q o (n w)", q=P, n=2),
                         filler[:, :, :].rearrange("q (o n) w -> q o (n w)", o=1).to_broadcast([P, SPARE // P // 2, 2 * ROW])).then_inc(s_spare, 16)

            def late_weights(i):
                if isinstance(i, int) and i == PAIRS + 1:
                    sp.wait_ge(SA.s_u_ps, PAIRS * 4)
                    for e in range(EXPERTS):
                        sp.dma_start(w2[:, e], moe["w2"][e].rearrange("(c f) d -> f c d", c=FC)).then_inc(s_weights, 16)

            iterations({"fill": fill, "turn": turn, "spread_terms": spread_terms}, late_weights)
            sp.wait_ge(SA.s_t_ps, PAIRS * 4)

            sp.wait_ge(s_spare, 16)
            sp.wait_ge(s_table, TABLE_OPS)
            sp.wait_ge(r.s_disp, PAIRS * 4 * 16)
            sp.wait_ge(CA.s_u_ps, PAIRS * 4)
            def load(i, v):
                n = i * AHEAD + v
                row = sp.value_load(slot_row_i[0:1, bass.ds(n, 1)], min_val=0, max_val=(EXPERTS + 1) * T_ALL - P)
                expert = sp.value_load(slot_expert_i[0:1, bass.ds(n, 1)], min_val=0, max_val=EXPERTS - 1)
                if after_pair(i):
                    sp.wait_ge(s_scatter[v], i * 16)
                sp.dma_start(xs[v][:, :], dispatched[bass.ds(row, P), :]).then_inc(s_xs[v], 16)
                if after_pair(i) or v >= W_AHEAD:
                    sp.wait_ge(s_h_ps, (n - W_AHEAD) * 2 + 2)
                sp.dma_start(w1[v % W_AHEAD], moe["w1"][bass.ds(expert, 1)].rearrange("o d f -> d (o f)")).then_inc(s_w1[v % W_AHEAD], 16)

            slots(sp, (load, 0))

            for v in range(AHEAD):
                sp.wait_ge(s_scatter[v], 16 * ROUNDS)
            for q in range(TAIL):
                for c in range(TOPK):
                    src = results[c * T_ALL + q * TN * P:c * T_ALL + (q + 1) * TN * P, :]
                    sp.dma_start(yy[c][:, TN * q:TN * q + TN, :], src.rearrange("(b p) d -> p b d", p=P)).then_inc(s_yy[q], 16)
            for q in range(TAIL):
                sp.wait_ge(s_o3, TN * (q + 1))
                sp.dma_start(out[TN * q:TN * q + TN].rearrange("b p d -> p b d"), o3[:, TN * q:TN * q + TN, :]).then_inc(s_out, 16)
            sp.wait_ge(s_out, 16 * TAIL)

        @block.tensor
        def _(pe):
            held = {}
            now = [0]

            def take(b):
                for s, n, c in held.get(b, ()):
                    pe.wait_ge(s, now[0] * n + c)

            def give(b, s, n, value_at_zero, *others):
                held[b] = ((s, n, value_at_zero),) + others

            off = [0]

            def turn(k, p, u):
                if k.causal:
                    pe.wait_ge(k.s_ld, p * 16 + 16)
                else:
                    pe.wait_ge(SA.s_x1, p * 2 + 2)
                src = k.xin if k.causal else SA.x1
                take(ACT_BANK)
                for v in range(2):
                    ins = pe.transpose(bank[ACT_BANK][:, P * v:P * v + P], src[:, v, :], ident)
                ins.then_inc(k.s_xt_ps, 1)
                give(ACT_BANK, k.s_xt, 1, 1 + off[0])
                if not k.causal:
                    pe.wait_ge(k.s_ld, p * 16 + 16)
                    take(DVE_BANK)
                    for v in range(2):
                        ins = pe.transpose(bank[DVE_BANK][:, SC * v:SC * v + SC], k.cin[:, v, :], ident[0:SC, 0:SC])
                    ins.then_inc(k.s_ct_ps, 1)
                    give(DVE_BANK, k.s_ct, 1, 1 + off[0])

            def project(k, p, u):
                if not after_pair(p):
                    pe.wait_ge(k.s_const, 32)
                pe.wait_ge(k.s_xt, p + 1)
                take(ACT_BANK)
                pe.matmul(bank[ACT_BANK][:, 0:2 * P], k.wq[:, :], k.xT[:, :], start=True, stop=True).then_inc(k.s_c_ps, 1)
                give(ACT_BANK, k.s_lo, 2, 1 + 2 * off[0])
                if not k.causal:
                    pe.wait_ge(k.s_ct, p + 1)
                take(DVE_BANK)
                src = k.xT if k.causal else k.cT
                pe.matmul(bank[DVE_BANK][:, 0:2 * k.keys], k.wk[:, :], src[:, :], start=True, stop=True).then_inc(k.s_c_ps, 1)
                give(DVE_BANK, k.s_lo, 2, 2 + 2 * off[0])

            def spread_terms(k, p, u):
                if not after_pair(p):
                    pe.wait_ge(s_setup, SETUP)
                for b, hi, lo, h, l, s, done, n in (
                        (ACT_BANK, "hq", "lq", k.hq, k.lq, k.s_rq_ps, k.s_qu, 1),
                        (DVE_BANK, "hk", "lk", k.hk, k.lk, k.s_rk_ps, k.s_ku, 2)):
                    pe.wait_ge(k.s_lo, p * 2 + n)
                    take(b)
                    for g in (2 * u, 2 * u + 1):
                        dst = bank[b][:, 2 * P * (g % 2):2 * P * (g % 2) + 2 * P]
                        pe.matmul(dst, spread[hi][:, g].rearrange("c j t d -> c (j t d)"), h[:, :], start=True, stop=False)
                        ins = pe.matmul(dst, spread[lo][:, g].rearrange("c j t d -> c (j t d)"), l[:, :], start=False, stop=True)
                    ins.then_inc(s, 1)
                    give(b, done, 2, u + 1 + 2 * off[0])

            def values(k, p, u):
                src = k.xT if k.causal else k.cT
                take(DVE_BANK)
                for v in range(2):
                    ins = pe.matmul(bank[DVE_BANK][0:k.keys, P * v:P * v + P], src[:, k.keys * v:k.keys * v + k.keys], k.wv[:, :], start=True, stop=True)
                ins.then_inc(k.s_v_ps, 1)
                give(DVE_BANK, k.s_vo, 1, 1 + off[0])

            def scores(k, p, u):
                if u == 0:
                    pe.wait_ge(k.s_bdk, p * 64 + 64)
                    pe.wait_ge(k.s_qu, p * 2 + 2)
                for g in range(GROUPS):
                    b = SCORE[g % 2]
                    take(b)
                    dst = bank[b][:, :].rearrange("q (j n) -> q j n", j=J)[:, :, 0:k.kpad]
                    if k.causal:
                        pe.matmul(dst, ident_bf[:, :], causal_bf[:, :].rearrange("q (o n) -> q o n", o=1).to_broadcast([P, J, P]), start=True, stop=False)
                    pe.matmul(dst, k.qu[:, g, P * u:P * u + P], k.km[:, g, :, k.keys * u:k.keys * u + k.kpad],
                              start=not k.causal, stop=True).then_inc(k.s_s1_ps, 1)
                    give(b, k.s_nm, 8, 4 * u + g + 1 + 8 * off[0])

            def shift(k, p, u):
                pe.wait_ge(k.s_mm, p * 2 + u + 1)
                take(ACT_BANK)
                pe.transpose(bank[ACT_BANK][:, 0:P], k.mm[:, u].rearrange("q j r -> q (j r)").bitcast(F32), ident).then_inc(k.s_mt_ps, 1)
                give(ACT_BANK, k.s_sha, 4, 2 * u + 2 + 4 * off[0], (k.s_shv, 4, 2 * u + 2 + 4 * off[0]))

            def weights(k, p, u):
                pe.wait_ge(k.s_sha, p * 4 + 2 * u + 2)
                pe.wait_ge(k.s_shv, p * 4 + 2 * u + 2)
                if u == 0:
                    pe.wait_ge(k.s_bdq, p * 64 + 64)
                    pe.wait_ge(k.s_ku, p * 2 + 2)
                for g in range(GROUPS):
                    b = SHIFTED[g % 2]
                    take(b)
                    pe.matmul(bank[b][0:k.keys, :], k.ku[:, g, k.keys * u:k.keys * u + k.keys], k.qm[:, g, :, P * u:P * u + P],
                              start=True, stop=True).then_inc(k.s_s2_ps, 1)
                    give(b, k.s_ex, 8, 4 * u + g + 1 + 8 * off[0])

            def mix(k, p, u):
                if u == 0:
                    pe.wait_ge(k.s_vo, p + 1)
                for g in range(GROUPS):
                    b = WEIGHED[g // 2]
                    pe.wait_ge(k.s_pm if k.causal else k.s_ex, p * 8 + 4 * u + g + 1)
                    if g % 2 == 0:
                        take(b)
                    ins = pe.matmul(bank[b][64 * (g % 2):64 * (g % 2) + 64, :], k.vo[:, u, g, :], k.pt[u][:, 512 * g:512 * g + 512], start=True, stop=True)
                    if g % 2:
                        ins.then_inc(k.s_u_ps, 1)
                        give(b, k.s_us, 4, 2 * u + g // 2 + 1 + 4 * off[0])

            def restore(k, p, u):
                for h in range(2):
                    b = WEIGHED[h]
                    take(b)
                    pe.wait_ge(k.s_us, p * 4 + 2 * u + h + 1)
                    for j in range(J):
                        ins = pe.transpose(bank[b][:, P * j:P * j + P], k.us[u][:, h, P * j:P * j + P], ident)
                    ins.then_inc(k.s_t_ps, 1)
                    give(b, k.s_on, 4, 2 * u + h + 1 + 4 * off[0])

            def turn_heads(k, p, u):
                pe.wait_ge(k.s_on, p * 4 + 2 * u + 2)
                take(ACT_BANK)
                pe.transpose(bank[ACT_BANK][:, 0:P], k.on[:, u, :], ident).then_inc(k.s_ot_ps, 1)
                give(ACT_BANK, k.s_ot, 2, u + 1 + 2 * off[0])

            def norm(k, p, u):
                pe.wait_ge(k.s_ot, p * 2 + u + 1)
                take(DVE_BANK)
                pe.matmul(bank[DVE_BANK][:, 0:D], k.oT[:, u, :], k.wo[:, :], start=True, stop=True).then_inc(k.s_w_ps, 1)
                give(DVE_BANK, k.s_y, 2, u + 1 + 2 * off[0])

            def route(k, p, u):
                if not after_pair(p):
                    pe.wait_ge(s_late, 64)
                pe.wait_ge(CA.s_x1, p * 2 + 2)
                take(ACT_BANK)
                for v in range(2):
                    ins = pe.transpose(bank[ACT_BANK][:, P * v:P * v + P], CA.x1[:, v, :], ident)
                ins.then_inc(r.s_xt_ps, 1)
                give(ACT_BANK, r.s_xT, 1, 1 + off[0])
                pe.wait_ge(r.s_xT, p + 1)
                take(DVE_BANK)
                for v in range(2):
                    ins = pe.matmul(bank[DVE_BANK][:, EXPERTS * v:EXPERTS * v + EXPERTS], r.xT[:, P * v:P * v + P], rw[:, :], start=True, stop=True)
                ins.then_inc(r.s_lg_ps, 1)
                give(DVE_BANK, r.s_rt, ROUTER_OPS, 1 + ROUTER_OPS * off[0])

            def place(k, p, u):
                pe.wait_ge(r.s_rt, p * ROUTER_OPS + SELECTED)
                take(DVE_BANK)
                for v in range(2):
                    dst = bank[DVE_BANK][:, EXPERTS * v:EXPERTS * v + EXPERTS]
                    pe.matmul(dst, cst[:, 2 * P:3 * P], r.sel[:, v, :], start=True, stop=False)
                    ins = pe.matmul(dst, ones[:, :], r.acc[:, :], start=False, stop=(v == 0))
                    if v == 1:
                        ins = pe.matmul(dst, ones[:, :], r.sel[:, 0, :], start=False, stop=True)
                ins.then_inc(r.s_rank_ps, 1)
                give(DVE_BANK, r.s_rt, ROUTER_OPS, SELECTED + 6 + ROUTER_OPS * off[0])

            pe.wait_ge(s_const, 16)
            raw = {"route": route, "place": place, "turn": turn, "project": project, "spread_terms": spread_terms, "values": values, "scores": scores, "shift": shift, "weights": weights, "mix": mix, "restore": restore, "turn_heads": turn_heads, "norm": norm}

            def at(f):
                def g(k, p, u):
                    off[0] = p - now[0]
                    f(k, p, u)
                return g

            def begin(i):
                now[0] = i

            def end():
                for b in held:
                    held[b] = tuple((s, n, c - n) for s, n, c in held[b])

            iterations({n: at(f) for n, f in raw.items()}, begin, end)
            now[0] = LAST_ITERATION + 1

            pe.wait_ge(r.s_rt, PAIRS * ROUTER_OPS)
            take(DVE_BANK)
            pe.matmul(bank[DVE_BANK][:, 0:EXPERTS], ones[:, :], r.acc[:, :], start=True, stop=True).then_inc(s_counts, 1)

            pe.wait_ge(s_weights, 16 * (EXPERTS + 1))
            take(ACT_BANK)
            pe.transpose(bank[ACT_BANK][:, 0:EXPERTS * FC], b1_rows[:, :], ident[0:EXPERTS * FC, 0:EXPERTS * FC]).then_inc(s_b1, 1)
            pe.wait_ge(s_b1, 2)
            pe.wait_ge(s_table, TABLE_OPS)

            def turn_rows(i, v):
                n, b = i * AHEAD + v, v % 2
                pe.wait_ge(s_xs[v], i * 16 + 16)
                pe.wait_ge(s_xst, n - 1) if after_pair(i) or v >= 2 else None
                pe.transpose(bank[6 + b][:, 0:P], xs[v][:, 0:P], ident).then_inc(s_xst_ps, 1)

            def hidden(i, v):
                n, b = i * AHEAD + v, v % 2
                pe.wait_ge(s_xst, n + 1)
                pe.wait_ge(s_w1[v % W_AHEAD], (i * (AHEAD // W_AHEAD) + v // W_AHEAD + 1) * 16)
                for c in range(FC):
                    if (after_pair(i) or v >= 2) and c % 2 == 0:
                        pe.wait_ge(s_gelu, (n - 2) * 4 + c + 2)
                    ins = pe.matmul(bank[2 * b + c // 2][:, P * (c % 2):P * (c % 2) + P], w1[v % W_AHEAD][:, P * c:P * c + P], xsT[b][:, :], start=True, stop=True)
                    if c % 2:
                        ins.then_inc(s_h_ps, 1)

            def output(i, v):
                n, b = i * AHEAD + v, v % 2
                expert = pe.value_load(slot_expert_i[0:1, bass.ds(n, 1)], min_val=0, max_val=EXPERTS - 1)
                if after_pair(i) or v >= 2:
                    pe.wait_ge(s_yb, n - 1)
                for c in range(FC):
                    pe.wait_ge(s_gelu, n * 4 + c + 1)
                    ins = pe.matmul(bank[4 + b][:, 0:D], hid[b][:, c, :], w2[:, bass.ds(expert, 1), c, :].rearrange("f o d -> f (o d)"), start=(c == 0), stop=(c == FC - 1))
                ins.then_inc(s_o_ps, 1)

            slots(pe, (turn_rows, 2), (hidden, 1), (output, 0))

        @block.scalar
        def _(act):

            def turn(k, p, u):
                act.wait_ge(k.s_xt_ps, p + 1)
                if after_pair(p):
                    act.wait_ge(k.s_v_ps, p) if k.causal else act.wait_ge(k.s_c_ps, p * 2)
                act.copy(k.xT[:, :], bank[ACT_BANK][:, 0:2 * P]).then_inc(k.s_xt, 1)

            def project(k, p, u):
                act.wait_ge(k.s_c_ps, p * 2 + 1)
                if after_pair(p):
                    act.wait_ge(k.s_rq_ps, p * 2)
                act.activation(k.hq[:, :], bank[ACT_BANK][:, 0:2 * P], ACT.Identity, bias=k.bq[:, :]).then_inc(k.s_hi, 1)
                act.wait_ge(k.s_c_ps, p * 2 + 2)
                if after_pair(p):
                    act.wait_ge(k.s_rk_ps, p * 2)
                n = 2 * k.keys
                act.activation(k.hk[:, 0:n], bank[DVE_BANK][:, 0:n], ACT.Identity, bias=k.bk[:, :]).then_inc(k.s_hi, 1)

            def spread_terms(k, p, u):
                act.wait_ge(k.s_rq_ps, p * 2 + u + 1)
                if after_pair(p):
                    act.wait_ge(k.s_s1_ps, p * 8)
                    act.wait_ge(k.s_bdq, p * 64)
                act.copy(k.qu[:, 2 * u:2 * u + 2, :].rearrange("r g n -> r (g n)"), bank[ACT_BANK][:, :]).then_inc(k.s_qu, 1)

            def shift(k, p, u):
                if not after_pair(p):
                    act.wait_ge(k.s_zero, 2)
                act.wait_ge(k.s_mt_ps, p * 2 + u + 1)
                if after_pair(p):
                    act.wait_ge(k.s_s2_ps, (p - 1) * 8 + 4 * u + 4)
                for j in (0, 1):
                    rows = slice(32 * j, 32 * j + 8)
                    src = bank[ACT_BANK][rows, 0:P].rearrange("r (o n) -> r o n", o=1).to_broadcast([8, GROUPS, P])
                    act.copy(k.qm[rows, :, j, P * u:P * u + P], src).then_inc(k.s_sha, 1)

            def weights(k, p, u):
                for g in range(GROUPS):
                    act.wait_ge(k.s_s2_ps, p * 8 + 4 * u + g + 1)
                    if after_pair(p) and g % 2 == 0:
                        act.wait_ge(k.s_u_ps, (p - 1) * 4 + 2 * u + g // 2 + 1)
                    act.activation(k.pt[u][:, 512 * g:512 * g + 512], bank[SHIFTED[g % 2]][0:k.keys, :], ACT.Exp, scale=SCALE).then_inc(k.s_ex, 1)

            def mix(k, p, u):
                for h in range(2):
                    act.wait_ge(k.s_u_ps, p * 4 + 2 * u + h + 1)
                    if after_pair(p):
                        act.wait_ge(k.s_t_ps, (p - 1) * 4 + 2 * u + h + 1)
                    act.copy(k.us[u][:, h, :], bank[WEIGHED[h]][:, :]).then_inc(k.s_us, 1)

            def turn_heads(k, p, u):
                act.wait_ge(k.s_ot_ps, p * 2 + u + 1)
                if after_pair(p):
                    act.wait_ge(k.s_w_ps, (p - 1) * 2 + u + 1)
                act.copy(k.oT[:, u, :], bank[ACT_BANK][:, 0:P]).then_inc(k.s_ot, 1)

            def route(k, p, u):
                act.wait_ge(r.s_xt_ps, p + 1)
                if after_pair(p):
                    act.wait_ge(r.s_lg_ps, p)
                act.copy(r.xT[:, :], bank[ACT_BANK][:, 0:2 * P]).then_inc(r.s_xT, 1)
                act.wait_ge(CA.s_x1, p * 2 + 2)
                if after_pair(p):
                    act.wait_ge(r.s_disp, p * 64)
                act.copy(r.sent[:, :, :, 0:D], CA.x1[:, :, :].rearrange("q v (o d) -> q v o d", o=1).to_broadcast([P, 2, TOPK, D])).then_inc(r.s_xe1, 1)

            def gate(k, p, u):
                act.wait_ge(r.s_rt, p * ROUTER_OPS + 3)
                act.activation(r.exl[:, :, :], r.ls[:, :, :], ACT.Exp).then_inc(r.s_exp, 1)

            def choose(k, p, u):
                act.wait_ge(r.s_rt, p * ROUTER_OPS + SELECTED + 1)
                act.activation(r.ed[:, :], r.d[:, :], ACT.Exp).then_inc(r.s_exp, 1)

            iterations({"route": route, "gate": gate, "choose": choose, "turn": turn, "project": project, "spread_terms": spread_terms, "shift": shift, "weights": weights, "mix": mix, "turn_heads": turn_heads})

            act.wait_ge(s_b1, 1)
            act.copy(b1[:, :], bank[ACT_BANK][:, 0:EXPERTS * FC]).then_inc(s_b1, 1)
            act.wait_ge(s_b1, 2)
            act.wait_ge(s_table, TABLE_OPS)

            def activate(i, v):
                n, b = i * AHEAD + v, v % 2
                expert = act.value_load(slot_expert_i[0:1, bass.ds(n, 1)], min_val=0, max_val=EXPERTS - 1)
                for c in range(FC):
                    if c % 2 == 0:
                        act.wait_ge(s_h_ps, n * 2 + c // 2 + 1)
                    if (after_pair(i) or v >= 2) and c == 0:
                        act.wait_ge(s_o_ps, n - 1)
                    act.activation(hid[b][:, c, :], bank[2 * b + c // 2][:, P * (c % 2):P * (c % 2) + P], ACT.Gelu,
                                   bias=b1[:, bass.ds(expert * FC + c, 1)]).then_inc(s_gelu, 1)

            slots(act, (activate, 0))

        @block.vector
        def _(dve):
            dve.memset(ones[:, :], 1.0).then_inc(s_pool_ones, 1)
            dve.memset(filler[:, :, :], 1.0).then_inc(s_fill, 1)
            dve.memset(r.acc[:, :], 0.0).then_inc(s_pool_ones, 1)
            n_setup = [0]

            def setup(ins):
                n_setup[0] += 1
                ins.then_inc(s_setup, 1)

            for k in KINDS:
                setup(dve.memset(k.vo[:, :, :, 32:64], 1.0))
                setup(dve.memset(k.mm[:, :, :, :].bitcast(F32), 0.0))
            setup(dve.memset(CA.hk[:, 2 * SC:].bitcast(F32), 0.0))
            setup(dve.memset(CA.lk[:, 2 * SC:].bitcast(F32), 0.0))
            zeroed = n_setup[0]
            for n in spread:
                dve.memset(spread[n][:, :, :, :, :].bitcast(F32), 0.0).then_inc(s_spread0, 1)
            dve.wait_ge(s_spread0, 4)
            dve.wait_ge(s_const, 16)
            for n, terms in (("hq", (1, 2)), ("lq", (3,)), ("hk", (1, 3)), ("lk", (2,))):
                for t in terms:
                    setup(dve.tensor_copy(spread[n][:, :, :, t, :], ident.rearrange("c (g j d) -> c g j d", g=GROUPS, j=J)))
            setup(dve.tensor_copy(ident_bf[:, :], ident))
            setup(dve.tensor_copy(causal_bf[:, :], cst[:, P:2 * P]))
            assert n_setup[0] == SETUP, n_setup[0]

            def turn(k, p, u):
                if k.causal:
                    return
                dve.wait_ge(k.s_ct_ps, p + 1)
                if after_pair(p):
                    dve.wait_ge(k.s_v_ps, p)
                dve.tensor_copy(k.cT[:, :], bank[DVE_BANK][:, 0:2 * SC]).then_inc(k.s_ct, 1)

            def project(k, p, u):
                for n, (b, bias, h, l, w, s) in enumerate(((ACT_BANK, k.bq, k.hq, k.lq, 2 * P, k.s_rq_ps), (DVE_BANK, k.bk, k.hk, k.lk, 2 * k.keys, k.s_rk_ps))):
                    dve.wait_ge(k.s_hi, p * 2 + n + 1)
                    if after_pair(p):
                        dve.wait_ge(s, p * 2)
                    dve.scalar_tensor_tensor(out=l[:, 0:w], in0=bank[b][:, 0:w], scalar=bias[:, :], in1=h[:, 0:w].bitcast(F32),
                                             op0=ALU.add, op1=ALU.subtract).then_inc(k.s_lo, 1)

            def spread_terms(k, p, u):
                dve.wait_ge(k.s_rk_ps, p * 2 + u + 1)
                if after_pair(p):
                    dve.wait_ge(k.s_s2_ps, p * 8)
                    dve.wait_ge(k.s_bdk, p * 64)
                n = 2 * k.keys
                dve.tensor_tensor(k.ku[:, 2 * u:2 * u + 2, :], bank[DVE_BANK][:, :].rearrange("r (g n) -> r g n", g=2)[:, :, 0:n],
                                  kones[:, 2 * u:2 * u + 2].rearrange("r (g o) -> r g o", o=1).to_broadcast([P, 2, n]), ALU.add).then_inc(k.s_ku, 1)

            def values(k, p, u):
                dve.wait_ge(k.s_v_ps, p + 1)
                if after_pair(p):
                    dve.wait_ge(k.s_u_ps, p * 4)
                for_all = k.bv[0:k.keys, :].rearrange("n (o g c) -> n o g c", o=1, g=GROUPS).to_broadcast([k.keys, 2, GROUPS, 32])
                dve.tensor_tensor(k.vo[:, :, :, 0:32], bank[DVE_BANK][0:k.keys, 0:2 * P].rearrange("n (b g c) -> n b g c", b=2, g=GROUPS),
                                  for_all, ALU.add).then_inc(k.s_vo, 1)

            def scores(k, p, u):
                if after_pair(p):
                    dve.wait_ge(k.s_mm, (p - 1) * 2 + u + 1)
                for g in range(GROUPS):
                    dve.wait_ge(k.s_s1_ps, p * 8 + 4 * u + g + 1)
                    dve.tensor_reduce(k.nm[:, u, g, :], bank[SCORE[g % 2]][:, :].rearrange("q (j n) -> q j n", j=J)[:, :, 0:k.keys],
                                      AX.X, ALU.max, negate=True).then_inc(k.s_nm, 1)

            def shift(k, p, u):
                if after_pair(p):
                    dve.wait_ge(k.s_mt_ps, (p - 1) * 2 + u + 1)
                dve.wait_ge(k.s_nm, p * 8 + 4 * u + 4)
                nm = k.nm[:, u].rearrange("q g j -> q j g")
                dve.tensor_copy(k.mm[:, u, :, 0:4], nm).then_inc(k.s_mmh, 1)
                dve.wait_ge(k.s_mmh, p * 2 + u + 1)
                dve.tensor_tensor(k.mm[:, u, :, 4:8], nm, k.mm[:, u, :, 0:4].bitcast(F32), ALU.subtract).then_inc(k.s_mm, 1)

            def shift_rows(k, p, u):
                if not after_pair(p):
                    dve.wait_ge(k.s_zero, 2)
                dve.wait_ge(k.s_mt_ps, p * 2 + u + 1)
                if after_pair(p):
                    dve.wait_ge(k.s_s2_ps, (p - 1) * 8 + 4 * u + 4)
                for j in (2, 3):
                    rows = slice(32 * j, 32 * j + 8)
                    src = bank[ACT_BANK][rows, 0:P].rearrange("r (o n) -> r o n", o=1).to_broadcast([8, GROUPS, P])
                    dve.tensor_copy(k.qm[rows, :, j, P * u:P * u + P], src).then_inc(k.s_shv, 1)

            def restore(k, p, u):
                if after_pair(p):
                    dve.wait_ge(k.s_on, (p - 1) * 4 + 2 * u + 2)
                    dve.wait_ge(k.s_ot_ps, (p - 1) * 2 + u + 1)
                for h in range(2):
                    dve.wait_ge(k.s_t_ps, p * 4 + 2 * u + h + 1)
                    t = bank[WEIGHED[h]][:, :]
                    sums = t.rearrange("q (j s r) -> q s j r", j=J, s=2)[:, :, :, 32]
                    dve.reciprocal(k.rd[:, u, h], sums).then_inc(k.s_rd, 1)
                    dve.wait_ge(k.s_rd, p * 4 + 2 * u + h + 1)
                    vals = bass.AP(t.tensor, t.offset, [list(t.ap[0]), [64, 2], [P + HD, J], [1, HD]])
                    dve.tensor_tensor(k.on[:, u, 64 * h:64 * h + 64].rearrange("q (s j d) -> q s j d", s=2, j=J), vals,
                                      k.rd[:, u, h].rearrange("q s (j o) -> q s j o", o=1).to_broadcast([P, 2, J, HD]), ALU.mult).then_inc(k.s_on, 1)

            def norm(k, p, u):
                n = p * 2 + u + 1
                dve.wait_ge(k.s_w_ps, n)
                if not k.causal:
                    dve.wait_ge(SA.s_xr, n)
                elif not after_pair(p):
                    dve.wait_ge(s_pool_setup, 4)
                if after_pair(p):
                    dve.wait_ge(k.s_xn, n - 2)
                dve.tensor_tensor(k.y[:, u, :], bank[DVE_BANK][:, 0:D], residual[:, bass.ds(p * 2 + u, 1), :].rearrange("q o d -> q (o d)"), ALU.add).then_inc(k.s_y, 1)
                dve.wait_ge(k.s_y, n)
                dve.bn_stats(k.bs[:, u, :], k.y[:, u, :]).then_inc(k.s_bs, 1)
                dve.wait_ge(k.s_bs, n)
                if after_pair(p):
                    dve.wait_ge(k.s_ve, n - 2)
                dve.bn_aggr(k.ba[:, u, :], k.bs[:, u, :]).then_inc(k.s_ba, 1)
                dve.wait_ge(k.s_rs, n)
                dve.wait_ge(k.s_ba, n)
                if after_pair(p):
                    dve.wait_ge(k.s_xg, n - 2)
                dve.tensor_scalar(k.xn[:, u, :], k.y[:, u, :], k.ba[:, u, 0:1], k.rs[:, u:u + 1], ALU.subtract, ALU.mult).then_inc(k.s_xn, 1)

            done = [0]

            def routed(p, ins):
                done[0] = done[0] % ROUTER_OPS + 1
                ins.then_inc(r.s_rt, 1)
                dve.wait_ge(r.s_rt, p * ROUTER_OPS + done[0])

            def wide(t):
                return t[:, :].rearrange("q (v o) -> q v o", o=1).to_broadcast([P, 2, EXPERTS])

            def each(t):
                return t.rearrange("q (o e) -> q o e", o=1).to_broadcast([P, 2, EXPERTS])

            def gate(k, p, u):
                if not after_pair(p):
                    dve.wait_ge(s_late, 64)
                dve.wait_ge(r.s_lg_ps, p + 1)
                if after_pair(p):
                    dve.wait_ge(r.s_disp, p * 64)
                    dve.wait_ge(r.s_rank_ps, p)
                routed(p, dve.tensor_tensor(r.lg[:, :, :], bank[DVE_BANK][:, 0:2 * EXPERTS].rearrange("q (v e) -> q v e", v=2), each(rb), ALU.add))
                routed(p, dve.tensor_reduce(r.nmx[:, :], r.lg[:, :, :], AX.X, ALU.max, negate=True))
                routed(p, dve.tensor_tensor(r.ls[:, :, :], r.lg[:, :, :], wide(r.nmx), ALU.add))

            def choose(k, p, u):
                dve.wait_ge(r.s_exp, p * 2 + 1)
                routed(p, dve.tensor_reduce(r.sm[:, :], r.exl[:, :, :], AX.X, ALU.add))
                routed(p, dve.reciprocal(r.rsm[:, :], r.sm[:, :]))
                routed(p, dve.tensor_tensor(r.p[:, :, :], r.exl[:, :, :], wide(r.rsm), ALU.mult))
                for prob, best, eq, key, km, oh in ((r.p, r.p1, r.eq, r.key, r.km, r.oh1), (r.pm, r.p2, r.eq2, r.key2, r.km2, r.oh2)):
                    if oh is r.oh2:
                        routed(p, dve.scalar_tensor_tensor(out=r.pm[:, :, :], in0=r.oh1[:, :, :], scalar=-2.0, in1=r.p[:, :, :], op0=ALU.mult, op1=ALU.add))
                    routed(p, dve.tensor_reduce(best[:, :], prob[:, :, :], AX.X, ALU.max))
                    routed(p, dve.tensor_tensor(eq[:, :, :], prob[:, :, :], wide(best), ALU.is_equal))
                    routed(p, dve.tensor_tensor(key[:, :, :], eq[:, :, :], each(falling), ALU.mult))
                    routed(p, dve.tensor_reduce(km[:, :], key[:, :, :], AX.X, ALU.max))
                    routed(p, dve.tensor_tensor(oh[:, :, :], each(falling), wide(km), ALU.is_equal))
                routed(p, dve.tensor_tensor(r.sel[:, :, :], r.oh1[:, :, :], r.oh2[:, :, :], ALU.add))
                assert done[0] == SELECTED, done[0]
                routed(p, dve.tensor_tensor(r.d[:, :], r.p2[:, :], r.p1[:, :], ALU.subtract))

            def place(k, p, u):
                dve.wait_ge(r.s_exp, p * 2 + 2)
                routed(p, dve.tensor_scalar(r.den[:, :], r.ed[:, :], 1.0, None, ALU.add))
                routed(p, dve.reciprocal(r.w1[:, :], r.den[:, :]))
                tile = lambda c, col: r.sent[:, :, c, col]
                routed(p, dve.tensor_tensor(tile(1, ROW - 1), r.ed[:, :], r.w1[:, :], ALU.mult))
                routed(p, dve.tensor_copy(tile(0, ROW - 1), r.w1[:, :]))
                dve.wait_ge(r.s_rank_ps, p + 1)
                routed(p, dve.tensor_tensor(r.base[:, :, :], bank[DVE_BANK][:, 0:2 * EXPERTS].rearrange("q (v e) -> q v e", v=2), each(region), ALU.add))
                assert done[0] == SELECTED + 6, done[0]
                routed(p, dve.tensor_tensor(r.t1[:, :, :], r.base[:, :, :], r.oh1[:, :, :], ALU.mult))
                routed(p, dve.tensor_tensor(r.t2[:, :, :], r.base[:, :, :], r.oh2[:, :, :], ALU.mult))
                routed(p, dve.tensor_reduce(r.pos[:, 0, :], r.t1[:, :, :], AX.X, ALU.add))
                routed(p, dve.tensor_reduce(r.pos[:, 1, :], r.t2[:, :, :], AX.X, ALU.add))
                routed(p, dve.tensor_tensor(r.acc[:, :], r.acc[:, :], r.sel[:, 0, :], ALU.add))
                routed(p, dve.tensor_tensor(r.acc[:, :], r.acc[:, :], r.sel[:, 1, :], ALU.add))
                routed(p, dve.tensor_copy(r.row[:, :, :], r.pos[:, :, :].rearrange("q c v -> q v c")))
                routed(p, dve.tensor_copy(r.sent[:, :, :, P].bitcast(I32), rows_sb[:, bass.ds(p * 2, 2), :]))
                assert done[0] == ROUTER_OPS, done[0]

            dve.wait_ge(s_pool_ones, 2)
            dve.wait_ge(s_setup, SETUP)
            iterations({"gate": gate, "choose": choose, "place": place, "turn": turn, "project": project, "spread_terms": spread_terms, "values": values, "scores": scores, "shift": shift, "shift_rows": shift_rows, "restore": restore, "norm": norm})

            tables = [0]

            def listed(ins):
                tables[0] += 1
                ins.then_inc(s_table, 1)
                dve.wait_ge(s_table, tables[0])

            row0 = lambda t, a, b, inner=True: (t.rearrange("q (o n) -> q o n", o=1) if inner else t.rearrange("q (n o) -> q n o", o=1)).to_broadcast([1, a, b])
            dve.wait_ge(s_counts, 1)
            listed(dve.tensor_copy(tb.count[:, :], bank[DVE_BANK][0:1, 0:EXPERTS]))
            listed(dve.tensor_tensor(tb.full[:, :, :], row0(tb.count[:, :], EXPERTS, T_ALL // P, False), row0(tile_starts[0:1], EXPERTS, T_ALL // P), ALU.is_gt))
            listed(dve.tensor_reduce(tb.tiles[:, :], tb.full[:, :, :], AX.X, ALU.add))
            listed(dve.tensor_tensor(tb.before[:, :, :], row0(tb.tiles[:, :], E9, EXPERTS), below[0:1].rearrange("q (a b) -> q a b", a=E9), ALU.mult))
            listed(dve.tensor_reduce(tb.first[:, :], tb.before[:, :, :], AX.X, ALU.add))
            listed(dve.tensor_tensor(tb.past[:, :, :], row0(slot_no[0:1], SLOTS, EXPERTS, False), row0(tb.first[:, 1:E9], SLOTS, EXPERTS), ALU.is_ge))
            listed(dve.tensor_reduce(tb.expert[:, :], tb.past[:, :, :], AX.X, ALU.add))
            listed(dve.tensor_scalar(slot_expert_i[:, :], tb.expert[:, :], float(EXPERTS - 1), None, ALU.min))
            listed(dve.scalar_tensor_tensor(out=tb.shift[:, :], in0=tb.first[:, :], scalar=-float(P), in1=region9[0:1], op0=ALU.mult, op1=ALU.add))
            listed(dve.tensor_tensor(tb.one[:, :, :], row0(tb.expert[:, :], SLOTS, E9, False), row0(expert_no[0:1], SLOTS, E9), ALU.is_equal))
            listed(dve.tensor_tensor(tb.prod[:, :, :], tb.one[:, :, :], row0(tb.shift[:, :], SLOTS, E9), ALU.mult))
            listed(dve.tensor_reduce(tb.start[:, :], tb.prod[:, :, :], AX.X, ALU.add))
            listed(dve.tensor_tensor(slot_row_i[:, :], tb.start[:, :], slot_rows[0:1], ALU.add))
            assert tables[0] == TABLE_OPS

            dve.wait_ge(s_weights, 16 * (EXPERTS + 1))

            def turned(i, v):
                n, b = i * AHEAD + v, v % 2
                dve.wait_ge(s_xst_ps, n + 1)
                if after_pair(i) or v >= 2:
                    dve.wait_ge(s_h_ps, (n - 2) * 2 + 2)
                dve.tensor_copy(xsT[b][:, :], bank[6 + b][:, 0:P]).then_inc(s_xst, 1)

            def gated(i, v):
                n, b = i * AHEAD + v, v % 2
                expert = dve.value_load(slot_expert_i[0:1, bass.ds(n, 1)], min_val=0, max_val=EXPERTS - 1)
                dve.wait_ge(s_o_ps, n + 1)
                if after_pair(i) or v >= 2:
                    dve.wait_ge(s_ys, n - 1)
                if after_pair(i):
                    dve.wait_ge(s_scatter[v], i * 16)
                dve.tensor_tensor(yb[b][:, :], bank[4 + b][:, 0:D], b2[:, bass.ds(expert, 1), :].rearrange("q o d -> q (o d)"), ALU.add).then_inc(s_yb, 1)
                dve.wait_ge(s_yb, n + 1)
                dve.tensor_scalar(ys[v], yb[b][:, :], xs[v][:, ROW - 1:ROW], None, ALU.mult).then_inc(s_ys, 1)

            slots(dve, (turned, 2), (gated, 0))

            for q in range(TAIL):
                t = slice(TN * q, TN * q + TN)
                dve.wait_ge(s_yy[q], 32)
                dve.tensor_tensor(y3[:, t, :], yy[0][:, t, :], residual[:, t, :], ALU.add).then_inc(s_y3a, 1)
                dve.wait_ge(s_y3a, q + 1)
                dve.tensor_tensor(y3[:, t, :], y3[:, t, :], yy[1][:, t, :], ALU.add).then_inc(s_y3, 1)
                dve.wait_ge(s_y3, q + 1)
                for b in range(TN * q, TN * q + TN):
                    dve.bn_stats(bs3[:, b, :], y3[:, b, :]).then_inc(s_bs3, 1)
                for b in range(TN * q, TN * q + TN):
                    dve.wait_ge(s_bs3, b + 1)
                    dve.bn_aggr(ba3[:, b, :], bs3[:, b, :]).then_inc(s_ba3, 1)
                dve.wait_ge(s_rs3, q + 1)
                for b in range(TN * q, TN * q + TN):
                    dve.wait_ge(s_ba3, b + 1)
                    dve.tensor_scalar(y3[:, b, :], y3[:, b, :], ba3[:, b, 0:1], rs3[:, b:b + 1], ALU.subtract, ALU.mult).then_inc(s_xn3, 1)
                dve.wait_ge(s_xn3, TN * (q + 1))
                dve.tensor_tensor(y3[:, t, :], y3[:, t, :], g3[:, :].rearrange("q (o d) -> q o d", o=1).to_broadcast([P, TN, D]), ALU.mult).then_inc(s_g3, 1)
                dve.wait_ge(s_g3, q + 1)
                dve.tensor_tensor(o3[:, t, :], y3[:, t, :], beta3[:, :].rearrange("q (o d) -> q o d", o=1).to_broadcast([P, TN, D]), ALU.add).then_inc(s_o3, TN)

        @block.gpsimd
        def _(pool):
            for k in KINDS:
                pool.memset(k.qm[:, :, :, :].bitcast(F32), 0.0).then_inc(k.s_zero, 1)
                pool.memset(k.km[:, :, :, :].bitcast(F32), 0.0).then_inc(k.s_zero, 1)
            pool.memset(half[:, :], -0.5).then_inc(s_pool_setup, 1)
            pool.wait_ge(SA.s_const, 32)
            pool.wait_ge(CA.s_const, 32)
            pool.wait_ge(s_residual, 16)
            pool.tensor_tensor(residual[:, :, :], residual[:, :, :], SA.bo[:, :].rearrange("p (o d) -> p o d", o=1).to_broadcast([P, B, D]), ALU.add).then_inc(s_pool_setup, 3)

            def weights(k, p, u):
                if not k.causal:
                    return
                for g in range(GROUPS):
                    n = p * 8 + 4 * u + g + 1
                    pool.wait_ge(k.s_ex, n)
                    blockg = k.pt[u][:, 512 * g:512 * g + 512]
                    pool.affine_select(out=blockg, in_=blockg, compare_op=ALU.is_ge, fill=0.0, base=0,
                                       pattern=[[0, J], [1, P]], channel_multiplier=-1).then_inc(k.s_pm, 1)

            def norm(k, p, u):
                n = p * 2 + u + 1
                pool.wait_ge(k.s_ba, n)
                if after_pair(p):
                    pool.wait_ge(k.s_xn, n - 2)
                pool.tensor_scalar(k.ve[:, u:u + 1], k.ba[:, u, 1:2], EPS, None, ALU.add).then_inc(k.s_ve, 1)
                pool.wait_ge(k.s_ve, n)
                pool.tensor_tensor(k.rs[:, u:u + 1], k.ve[:, u:u + 1], half[:, :], ALU.pow).then_inc(k.s_rs, 1)
                pool.wait_ge(k.s_xn, n)
                if after_pair(p):
                    pool.wait_ge(k.s_x1, n - 2)
                pool.tensor_tensor(k.xg[:, u, :], k.xn[:, u, :], k.g[:, :], ALU.mult).then_inc(k.s_xg, 1)
                pool.wait_ge(k.s_xg, n)
                if after_pair(p):
                    pool.wait_ge(CA.s_xt_ps, p) if k.causal else pool.wait_ge(r.s_xt_ps, p)
                    if not k.causal:
                        pool.wait_ge(r.s_xe1, p)
                    pool.wait_ge(k.s_xr, n - 2)
                pool.tensor_tensor(k.x1[:, u, :], k.xg[:, u, :], k.b[:, :], ALU.add).then_inc(k.s_x1, 1)
                pool.wait_ge(k.s_x1, n)
                if k.causal:
                    pool.tensor_tensor(residual[:, bass.ds(p * 2 + u, 1), :].rearrange("q o d -> q (o d)"), k.x1[:, u, :], CA.bo[:, :], ALU.add).then_inc(k.s_xr, 1)
                else:
                    pool.tensor_copy(residual[:, bass.ds(p * 2 + u, 1), :].rearrange("q o d -> q (o d)"), k.x1[:, u, :]).then_inc(k.s_xr, 1)

            def place(k, p, u):
                pool.wait_ge(s_filled, p * 32 + 32)
                pool.wait_ge(r.s_rt, p * ROUTER_OPS + ROUTER_OPS)
                pool.wait_ge(r.s_xe1, p + 1)
                pool.wait_ge(CA.s_xr, p * 2 + 2)
                for v in range(2):
                    for c in range(TOPK):
                        pool.indirect_dma_start(out=dispatched, out_offset=bass.IndirectOffsetOnAxis(ap=r.row[:, v, c:c + 1], axis=0),
                                                in_=r.sent[:, v, c, :], in_offset=None).then_inc(r.s_disp, 16)

            iterations({"place": place, "weights": weights, "norm": norm})


            def scatter(i, v):
                pool.wait_ge(s_ys, i * AHEAD + v + 1)
                pool.indirect_dma_start(out=results, out_offset=bass.IndirectOffsetOnAxis(ap=xs[v][:, P:P + 1].bitcast(I32), axis=0),
                                        in_=ys[v], in_offset=None, bounds_check=TOPK * T_ALL - 1, oob_is_err=False).then_inc(s_scatter[v], 16)

            for i in range(ROUNDS):
                for v in range(AHEAD):
                    scatter(i, v)
            for q in range(TAIL):
                pool.wait_ge(s_ba3, TN * (q + 1))
                t = slice(TN * q, TN * q + TN)
                pool.tensor_scalar(ve3[:, t], ba3[:, t, 1], EPS, None, ALU.add).then_inc(s_ve3, 1)
                pool.wait_ge(s_ve3, q + 1)
                pool.tensor_tensor(rs3[:, t], ve3[:, t], half[:, :].to_broadcast([P, TN]), ALU.pow).then_inc(s_rs3, 1)




def kernel(**inputs):
    import concourse.bacc as bacc
    from concourse.bass_utils import run_bass_kernel_spmd

    nc = bacc.Bacc("TRN2", target_bir_lowering=False, num_devices=1)
    arrays = {}

    def given(name, a):
        a = np.ascontiguousarray(a)
        arrays[f"in_{name}"] = a
        return nc.dram_tensor(f"in_{name}", a.shape, mybir.dt.from_np(a.dtype), kind="ExternalInput").ap()

    x, ctx = given("x", inputs["x"]), given("ctx", inputs["ctx_1024"])
    layer = lambda name: given(name, inputs["L0_xattn_" + name])

    def packed(a, norm):
        get = lambda n: inputs[f"L0_xattn_{n}"]
        columns = [get(f"{a}_{n}") for n in ("wq", "wk", "wv", "wo")] + [get(f"{a}_{n}")[:, None] for n in ("bq", "bk")]
        rows = [get(f"{a}_bv"), get(f"{a}_bo"), get(f"{norm}_g"), get(f"{norm}_b")]
        return {"square": given(f"{a}_square", np.concatenate(columns, axis=1)), "rows": given(f"{a}_rows", np.concatenate(rows))}

    sa, ca = (packed(a, l) for a, l in (("sa", "ln1"), ("ca", "ln2")))
    moe = dict(rw=layer("router_w"), w1=layer("e_w1"), b1=layer("e_b1"), w2=layer("e_w2"),
               rows=given("late_rows", np.concatenate([inputs["L0_xattn_" + n].ravel() for n in ("router_b", "e_b2", "ln3_g", "ln3_b")])))
    tokens = x.shape[0] * x.shape[1]
    consts = given("shape_constants", shape_constants())
    expert_consts = given("expert_constants", expert_constants(tokens, slot_count(tokens)))
    rows = given("result_rows", result_rows(x.shape[0]))
    out = nc.dram_tensor("out", x.shape, F32, kind="ExternalOutput").ap()
    build(nc, x, ctx, sa, ca, moe, out, consts, expert_consts, rows)
    return run_bass_kernel_spmd(nc, [arrays], core_ids=[0]).results[0]["out"]
```

```python
from contextlib import ExitStack

import numpy as np
import concourse.bass as bass
from concourse import mybir

F32, F32R, BF16, I32 = mybir.dt.float32, mybir.dt.float32r, mybir.dt.bfloat16, mybir.dt.int32
ALU, ACT, AX = mybir.AluOpType, mybir.ActivationFunctionType, mybir.AxisListType

P = 128
HEADS, HD = 16, 8
GROUPS, J = 4, 4
EPS = 1e-5
EXPERTS, TOPK = 8, 2
CONSTS = 3 * P + GROUPS
SLOTS_A_ROUND = 8
ROW = P + 2


class Attention:

    def __init__(self, name, keys, w):
        self.name, self.keys, self.w = name, keys, w
        self.kpad = keys + keys % 2
        self.causal = name == "sa"


class Router:
    pass


class SlotTable:
    pass


def shape_constants():
    row = np.arange(P)
    c = np.zeros((P, CONSTS), np.float32)
    c[:, 0:P] = np.eye(P)
    c[:, P:2 * P] = np.where(row[None, :] > row[:, None], -1e30, 0.0)
    c[:, 2 * P:3 * P] = row[:, None] < row[None, :]
    for g in range(GROUPS):
        c[:, 3 * P + g] = (row % 32 < 8) & (row % GROUPS == g)
    return c


def expert_constants(tokens, slots):
    e, e9, m, s = np.arange(EXPERTS), np.arange(EXPERTS + 1), np.arange(tokens // P), np.arange(slots)
    parts = [EXPERTS - e, e * tokens, m * P, (e[None, :] < e9[:, None]).ravel(), s, e9, e9 * tokens, s * P]
    return np.tile(np.concatenate(parts).astype(np.float32)[None, :], (P, 1))


def result_rows(batch):
    p, b, c = np.ogrid[:P, :batch, :TOPK]
    return (c * batch * P + b * P + p).astype(np.int32)


def slot_count(tokens):
    n = (TOPK * tokens + EXPERTS * (P - 1)) // P
    return -(-n // SLOTS_A_ROUND) * SLOTS_A_ROUND


def build(nc, x, ctx_1024, sa, ca, moe, out, consts, expert_consts, rows_of_results):
    B, S, D = x.shape
    T_ALL = B * S
    F = moe["w1"].shape[2]
    FC = F // P
    SLOTS = slot_count(T_ALL)
    SC = ctx_1024.shape[1]
    PAIRS = B // 2
    SCALE = float(HD) ** -0.5

    stack = ExitStack()
    with stack:
        def sb(name, shape, dt=F32):
            return stack.enter_context(nc.sbuf_tensor(name, shape, dt))

        def sem(name):
            return stack.enter_context(nc.semaphore(name))

        bank = [stack.enter_context(nc.psum_tensor(f"bank{n}", [P, 512], F32)) for n in range(8)]
        ACT_BANK, DVE_BANK = 6, 7

        cst = sb("cst", [P, CONSTS])
        ident, kones = cst[:, 0:P], cst[:, 3 * P:3 * P + GROUPS]
        ident_bf = sb("ident_bf", [P, P], BF16)
        causal_bf = sb("causal_bf", [P, P], BF16)
        half, warm = sb("half", [P, 1]), sb("warm", [P, 1])
        spread = {n: sb(f"spread_{n}", [P, GROUPS, J, 4, HD], F32R) for n in ("hq", "lq", "hk", "lk")}
        ones_bf, triangle_bf = sb("ones_bf", [P, P], BF16), sb("triangle_bf", [P, P], BF16)
        ecst = sb("ecst", [P, expert_consts.shape[1]])
        cut = np.cumsum([0, EXPERTS, EXPERTS, T_ALL // P, (EXPERTS + 1) * EXPERTS, SLOTS, EXPERTS + 1, EXPERTS + 1, SLOTS])
        falling, region, tile_starts, below, slot_no, expert_no, region9, slot_rows = (
            ecst[:, int(a):int(b)] for a, b in zip(cut[:-1], cut[1:]))
        residual = sb("residual", [P, B, D])
        rw = sb("router_w", [D, EXPERTS])
        late_rows = sb("late_rows", [P, EXPERTS + EXPERTS * D + 2 * D])
        rb, g3, beta3 = late_rows[:, 0:EXPERTS], late_rows[:, EXPERTS * (D + 1):EXPERTS * (D + 1) + D], late_rows[:, EXPERTS * (D + 1) + D:]
        b2 = late_rows[:, EXPERTS:EXPERTS * (D + 1)].rearrange("p (e d) -> p e d", e=EXPERTS)
        b1_rows, b1 = sb("b1_rows", [EXPERTS * FC, P]), sb("expert_b1", [P, EXPERTS * FC])
        dispatched = nc.dram_tensor("dispatched", [(EXPERTS + 1) * T_ALL, ROW], F32).ap()
        results = nc.dram_tensor("results", [TOPK * T_ALL, D], F32).ap()
        r = RT = Router()
        r.xT = sb("r_xT", [D, 2 * P])
        r.lg, r.ls, r.exl, r.p, r.eq, r.key, r.oh1, r.pm, r.eq2, r.key2, r.oh2, r.base, r.t1, r.t2 = (
            sb(f"r_by_expert{n}", [P, 2, EXPERTS]) for n in range(14))
        r.nmx, r.sm, r.rsm, r.p1, r.km, r.p2, r.km2, r.d, r.ed, r.den, r.w1 = (
            sb(f"r_by_token{n}", [P, 2]) for n in range(11))
        r.pos = sb("r_pos", [P, TOPK, 2])
        r.sent = sb("r_sent", [P, 2, TOPK, ROW])
        r.row = sb("r_row", [P, 2, TOPK], I32)
        r.sel = sb("r_sel", [P, 2, EXPERTS], BF16)
        r.acc = sb("r_acc", [P, 2, EXPERTS], BF16)
        r.s_xt_ps = sem("r_xt_ps")
        r.s_xT = sem("r_xT")
        r.s_xe1 = sem("r_xe1")
        r.s_lg_ps = sem("r_lg_ps")
        r.s_rt = sem("r_rt")
        r.s_exp = sem("r_exp")
        r.s_rank_ps = sem("r_rank_ps")
        r.s_disp = sem("r_disp")
        s_fill, s_filled, s_late = sem("fill"), sem("filled"), sem("late")
        s_spare, s_residual = sem("spare"), sem("residual_loaded")
        s_const = sem("s_const")
        s_setup, s_pool_setup = sem("s_setup"), sem("s_pool_setup")

        def kind(name, keys, w):
            k = Attention(name, keys, w)
            t = lambda n, shape, dt=F32: sb(f"{name}_{n}", shape, dt)
            k.square = t("square", [D, 4 * D + 2])
            k.wq, k.wk, k.wv, k.wo = (k.square[:, n * D:(n + 1) * D] for n in range(4))
            k.bq, k.bk = (k.square[:, 4 * D + n:4 * D + n + 1] for n in range(2))
            k.rows = t("rows", [P, 4 * D])
            k.bv, k.bo, k.g, k.b = (k.rows[:, n * D:(n + 1) * D] for n in range(4))
            k.s_const, k.s_zero = sem(f"{name}_const"), sem(f"{name}_zero")
            k.xin = t("xin", [P, 2, D])
            k.xT = t("xT", [D, 2 * P])
            if not k.causal:
                k.cin, k.cT = t("cin", [keys, 2, D]), t("cT", [D, 2 * keys])
            k.hq, k.lq, k.hk, k.lk = (t(n, [P, 2 * P], F32R) for n in ("hq", "lq", "hk", "lk"))
            k.qu = t("qu", [P, GROUPS, 2 * P], F32R)
            k.ku = t("ku", [P, GROUPS, 2 * keys], F32R)
            k.qm = t("qm", [P, GROUPS, J, 2 * P], F32R)
            k.km = t("km", [P, GROUPS, J, 2 * k.kpad], F32R)
            k.vo = t("vo", [keys, 2, GROUPS, 64])
            k.nm = t("nm", [P, 2, GROUPS, J])
            k.mm = t("mm", [P, 2, J, 32], F32R)
            k.pt_all = t("pt", [P, 2 * GROUPS * 512])
            k.pt = [k.pt_all[0:keys, u * GROUPS * 512:(u + 1) * GROUPS * 512] for u in range(2)]
            k.us = [t(f"us{u}", [P, 2, 512]) for u in range(2)]
            k.rd = t("rd", [P, 2, 2, 2, J])
            k.on, k.oT, k.y, k.xn = (t(n, [P, 2, D]) for n in ("on", "oT", "y", "xn"))
            k.bs, k.ba, k.ve, k.rs = t("bs", [P, 2, 6]), t("ba", [P, 2, 2]), t("ve", [P, 2]), t("rs", [P, 2])
            k.x1 = t("x1", [P, 2, D])
            k.s_ld = sem(f"{name}_ld")
            k.s_xt_ps = sem(f"{name}_xt_ps")
            k.s_xt = sem(f"{name}_xt")
            k.s_ct_ps = sem(f"{name}_ct_ps")
            k.s_ct = sem(f"{name}_ct")
            k.s_c_ps = sem(f"{name}_c_ps")
            k.s_hi = sem(f"{name}_hi")
            k.s_lo = sem(f"{name}_lo")
            k.s_rq_ps = sem(f"{name}_rq_ps")
            k.s_rk_ps = sem(f"{name}_rk_ps")
            k.s_qu = sem(f"{name}_qu")
            k.s_ku = sem(f"{name}_ku")
            k.s_v_ps = sem(f"{name}_v_ps")
            k.s_vo = sem(f"{name}_vo")
            k.s_bdq = sem(f"{name}_bdq")
            k.s_bdk = sem(f"{name}_bdk")
            k.s_s1_ps = sem(f"{name}_s1_ps")
            k.s_nm = sem(f"{name}_nm")
            k.s_mmh = sem(f"{name}_mmh")
            k.s_mm = sem(f"{name}_mm")
            k.s_mt_ps = sem(f"{name}_mt_ps")
            k.s_sha = sem(f"{name}_sha")
            k.s_s2_ps = sem(f"{name}_s2_ps")
            k.s_ex = sem(f"{name}_ex")
            k.s_pm = sem(f"{name}_pm")
            k.s_u_ps = sem(f"{name}_u_ps")
            k.s_us = sem(f"{name}_us")
            k.s_t_ps = sem(f"{name}_t_ps")
            k.s_rd = sem(f"{name}_rd")
            k.s_on = sem(f"{name}_on")
            k.s_ot_ps = sem(f"{name}_ot_ps")
            k.s_ot = sem(f"{name}_ot")
            k.s_w_ps = sem(f"{name}_w_ps")
            k.s_y = sem(f"{name}_y")
            k.s_bs = sem(f"{name}_bs")
            k.s_ba = sem(f"{name}_ba")
            k.s_ve = sem(f"{name}_ve")
            k.s_rs = sem(f"{name}_rs")
            k.s_xn = sem(f"{name}_xn")
            k.s_x1 = sem(f"{name}_x1")
            k.s_xr = sem(f"{name}_xr")
            return k

        SA = kind("sa", S, sa)
        CA = kind("ca", SC, ca)
        KINDS = (SA, CA)
        filler = sb("filler", [P, 2, ROW])
        w2 = SA.pt_all[:, :].rearrange("p (e c d) -> p e c d", e=EXPERTS, c=FC)
        ROUTER_OPS = 32
        SELECTED = 19
        tb = SlotTable()
        TABLE_OPS = 13
        E9 = EXPERTS + 1
        tb.count, tb.tiles, tb.first, tb.shift, tb.expert, tb.start = (
            sb(f"tb_row{n}", [1, size]) for n, size in enumerate((EXPERTS, EXPERTS, E9, E9, SLOTS, SLOTS)))
        tb.full, tb.before, tb.past, tb.one, tb.prod = (
            sb(f"tb_square{n}", [1, a, b]) for n, (a, b) in enumerate(((EXPERTS, T_ALL // P), (E9, EXPERTS), (SLOTS, EXPERTS), (SLOTS, E9), (SLOTS, E9))))
        s_table, s_weights, s_counts, s_b1 = sem("table"), sem("expert_weights"), sem("counts"), sem("b1")
        slot_expert_i, slot_row_i = sb("slot_expert", [1, SLOTS], I32), sb("slot_row", [1, SLOTS], I32)
        rows_sb = sb("rows_sb", [P, B, TOPK], I32)
        AHEAD, W_AHEAD = SLOTS_A_ROUND, 4
        ROUNDS = SLOTS // AHEAD
        xs = [sb(f"xs{v}", [P, ROW]) for v in range(AHEAD)]
        w1 = [CA.pt_all[:, v * F:(v + 1) * F] for v in range(W_AHEAD)]
        xsT = [sb(f"xsT{v}", [D, P]) for v in range(2)]
        hid = [SA.us[v][:, 0, :].rearrange("p (c n) -> p c n", c=FC) for v in range(2)]
        yb = [sb(f"yb{v}", [P, D]) for v in range(2)]
        ys = [CA.pt_all[:, W_AHEAD * F + v * D:W_AHEAD * F + (v + 1) * D] for v in range(AHEAD)]
        s_xs, s_scatter = ([sem(f"{n}{v}") for v in range(AHEAD)] for n in ("xs", "scatter"))
        s_w1 = [sem(f"w1_{v}") for v in range(W_AHEAD)]
        s_xst_ps, s_xst, s_h_ps, s_gelu, s_o_ps, s_yb, s_ys = (sem("m_" + n) for n in "xst_ps xst h_ps gelu o_ps yb ys".split())
        TN = 4
        TAIL = B // TN
        yy = [CA.pt_all[:, c * B * D:(c + 1) * B * D].rearrange("p (b d) -> p b d", b=B) for c in range(2)]
        y3, o3 = yy
        bs3, off3, ba3, ve3, rs3 = sb("bs3", [P, B, 6]), sb("off3", [P, B]), sb("ba3", [P, B, 2]), sb("ve3", [P, B]), sb("rs3", [P, B])
        s_yy = [sem(f"yy{q}") for q in range(TAIL)]
        s_off3, s_y3a, s_y3, s_bs3, s_ba3, s_ve3, s_rs3, s_xn3, s_g3, s_o3 = (sem("t_" + n) for n in "off3 y3a y3 bs3 ba3 ve3 rs3 xn3 g3 o3".split())
        s_warm, s_out, s_spread0, s_pool_ones = sem("warm"), sem("s_out"), sem("s_spread0"), sem("pool_ones")
        SETUP = 15

        block = stack.enter_context(nc.Block())

        def after_pair(p):
            return not isinstance(p, int) or p > 0

        ORDER = [
            (SA, "scores", 2, 0), (CA, "turn_heads", 1, -2), (CA, "spread_terms", 0, -1), (CA, "spread_terms", 1, -1),
            (CA, "norm", 1, -2), (SA, "weights", 0, 0), (SA, "scores", 3, 0), (SA, "weights", 1, 0),
            (CA, "values", 0, -1), (RT, "route", 0, -2), (RT, "gate", 0, -2), (SA, "mix", 0, 0), (SA, "shift", 1, 0),
            (CA, "scores", 0, -1), (RT, "choose", 0, -2), (SA, "restore", 0, 0), (SA, "mix", 1, 0),
            (CA, "scores", 1, -1), (SA, "weights", 2, 0), (CA, "scores", 2, -1), (SA, "turn", 0, 1),
            (SA, "weights", 3, 0), (CA, "shift", 0, -1), (RT, "second", 0, -2), (CA, "scores", 3, -1),
            (SA, "restore", 1, 0), (SA, "project", 0, 1), (SA, "mix", 2, 0), (CA, "weights", 0, -1),
            (SA, "mix", 3, 0), (SA, "turn_heads", 0, 0), (CA, "shift", 1, -1), (RT, "place", 0, -2),
            (SA, "spread_terms", 0, 1), (SA, "restore", 2, 0), (SA, "spread_terms", 1, 1), (SA, "restore", 3, 0),
            (SA, "norm", 0, 0), (SA, "values", 0, 1), (CA, "mix", 0, -1), (SA, "turn_heads", 1, 0),
            (CA, "weights", 1, -1), (SA, "norm", 1, 0), (CA, "weights", 2, -1), (RT, "number", 0, -2),
            (CA, "restore", 0, -1), (CA, "mix", 1, -1), (SA, "scores", 0, 1), (CA, "weights", 3, -1),
            (CA, "restore", 1, -1), (CA, "mix", 2, -1), (SA, "scores", 1, 1), (CA, "turn_heads", 0, -1),
            (CA, "turn", 0, 0), (RT, "fill", 0, -1), (CA, "mix", 3, -1), (SA, "shift", 0, 1), (CA, "norm", 0, -1),
            (CA, "restore", 2, -1), (CA, "restore", 3, -1), (CA, "project", 0, 0)]

        home = {
            (CA, "mix", 0): (6, 3), (CA, "mix", 1): (5, 2), (CA, "norm", 0): (5,), (CA, "norm", 1): (1,),
            (CA, "project", 0): (0, 3), (CA, "scores", 0): (2, 3), (CA, "scores", 1): (6, 0), (CA, "shift", 0): (3,),
            (CA, "shift", 1): (7,), (CA, "spread_terms", 0): (4, 6), (CA, "spread_terms", 1): (3, 0),
            (CA, "turn", 0): (6, 7), (CA, "turn_heads", 0): (4,), (CA, "turn_heads", 1): (5,),
            (CA, "values", 0): (4,), (CA, "weights", 0): (3, 0), (CA, "weights", 1): (7, 4), (RT, "place", 0): (2,),
            (RT, "route", 0): (5, 1), (SA, "mix", 0): (0, 1), (SA, "mix", 1): (5, 4), (SA, "norm", 0): (1,),
            (SA, "norm", 1): (1,), (SA, "project", 0): (2, 7), (SA, "scores", 0): (0, 1), (SA, "scores", 1): (1, 7),
            (SA, "shift", 0): (4,), (SA, "shift", 1): (5,), (SA, "spread_terms", 0): (3, 1),
            (SA, "spread_terms", 1): (0, 6), (SA, "turn", 0): (5,), (SA, "turn_heads", 0): (6,),
            (SA, "turn_heads", 1): (4,), (SA, "values", 0): (5,), (SA, "weights", 0): (3, 2),
            (SA, "weights", 1): (4, 7)}

        def iteration(i, steps):
            for k, step, u, ahead in ORDER:
                if 0 <= i + ahead < PAIRS:
                    if step in steps:
                        steps[step](k, i + ahead, u)

        FIRST_ITERATION, LAST_ITERATION = -max(o[3] for o in ORDER), PAIRS - 1 - min(o[3] for o in ORDER)

        def iterations(steps, begin=lambda i: None):
            for i in range(FIRST_ITERATION, LAST_ITERATION + 1):
                begin(i)
                iteration(i, steps)

        def slots(engine, *stages):
            def one_round(i, last=False):
                for v in range(AHEAD):
                    for stage, lead in stages:
                        if v + lead < AHEAD or not last:
                            stage(i + (v + lead) // AHEAD, (v + lead) % AHEAD)

            for stage, lead in stages:
                for v in range(lead):
                    stage(0, v)
            one_round(0)
            with engine.Fori(1, ROUNDS - 1) as i:
                one_round(i)
            one_round(ROUNDS - 1, last=True)

        @block.sync
        def _(sp):
            def load_rows(k, p):
                if k.causal:
                    sp.dma_start(k.xin[:, :, :], x[bass.ds(p * 2, 2)].rearrange("b p d -> p b d")).then_inc(k.s_ld, 16)
                else:
                    sp.dma_start(k.cin[:, :, :], ctx_1024[bass.ds(p * 2, 2)].rearrange("b p d -> p b d")).then_inc(k.s_ld, 16)

            sp.dma_start(cst[:, :], consts).then_inc(s_const, 16)
            for k in KINDS:
                sp.dma_start(k.square[:, :], k.w["square"]).then_inc(k.s_const, 16)
                if k.causal:
                    load_rows(k, 0)
                sp.dma_start(k.rows[:, :], k.w["rows"].rearrange("(o d) -> o d", o=1).to_broadcast([P, 4 * D])).then_inc(k.s_const, 16)
            sp.dma_start(residual[:, :, :], x.rearrange("b p d -> p b d")).then_inc(s_residual, 16)
            def turn(k, p, u):
                if after_pair(p):
                    sp.wait_ge(k.s_xt_ps if k.causal else k.s_ct_ps, p)
                if after_pair(p) or not k.causal:
                    load_rows(k, p)

            def fill(k, p, u):
                if after_pair(p):
                    sp.wait_ge(r.s_disp, p * 64)
                for e in (0, EXPERTS // 2):
                    regions = dispatched.rearrange("(e p q n) w -> p q e (n w)", e=EXPERTS + 1, q=P, n=2)
                    sp.dma_start(regions[bass.ds(p, 1), :, e:e + EXPERTS // 2].rearrange("o q e w -> (o q) e w"),
                                 filler[:, :, :].rearrange("q (o n) w -> q o (n w)", o=1).to_broadcast([P, EXPERTS // 2, 2 * ROW])).then_inc(s_filled, 16)

            def spread_terms(k, p, u):
                if u == 0:
                    return
                if not after_pair(p):
                    sp.wait_ge(k.s_zero, 2)
                sp.wait_ge(k.s_ku, p * 2 + 2)
                if after_pair(p):
                    sp.wait_ge(k.s_s1_ps, p * 8)
                for j in range(J):
                    rows = slice(32 * j + 8, 32 * j + 32)
                    sp.dma_start(k.km[rows, :, j, 0:2 * k.keys].bitcast(F32), k.ku[rows, :, :].bitcast(F32)).then_inc(k.s_bdk, 16)
                sp.wait_ge(k.s_qu, p * 2 + 2)
                if after_pair(p):
                    sp.wait_ge(k.s_s2_ps, p * 8)
                for j in range(J):
                    rows = slice(32 * j + 8, 32 * j + 32)
                    sp.dma_start(k.qm[rows, :, j, :].bitcast(F32), k.qu[rows, :, :].bitcast(F32)).then_inc(k.s_bdq, 16)

            sp.dma_start(rw[:, :], moe["rw"]).then_inc(s_late, 16)
            sp.dma_start(late_rows[:, :], moe["rows"].rearrange("(o d) -> o d", o=1).to_broadcast([P, late_rows.shape[1]])).then_inc(s_late, 16)
            sp.dma_start(ecst[:, :], expert_consts).then_inc(s_late, 16)
            sp.dma_start(rows_sb[:, :, :], rows_of_results).then_inc(s_late, 16)
            sp.dma_start(b1_rows[:, :], moe["b1"].rearrange("e (c f) -> (e c) f", c=FC)).then_inc(s_weights, 16)
            sp.wait_ge(s_fill, 1)
            SPARE = SLOTS * P - TOPK * T_ALL
            sp.dma_start(dispatched[EXPERTS * T_ALL:EXPERTS * T_ALL + SPARE].rearrange("(q o n) w -> q o (n w)", q=P, n=2),
                         filler[:, :, :].rearrange("q (o n) w -> q o (n w)", o=1).to_broadcast([P, SPARE // P // 2, 2 * ROW])).then_inc(s_spare, 16)

            def late_weights(i):
                if i == PAIRS + 1:
                    sp.wait_ge(SA.s_u_ps, PAIRS * 4)
                    for e in range(EXPERTS):
                        sp.dma_start(w2[:, e], moe["w2"][e].rearrange("(c f) d -> f c d", c=FC)).then_inc(s_weights, 16)

            iterations({"fill": fill, "turn": turn, "spread_terms": spread_terms}, late_weights)
            sp.wait_ge(SA.s_t_ps, PAIRS * 4)

            sp.wait_ge(s_spare, 16)
            sp.wait_ge(s_table, TABLE_OPS)
            sp.wait_ge(r.s_disp, PAIRS * 4 * 16)
            sp.wait_ge(CA.s_u_ps, PAIRS * 4)
            def load(i, v):
                n = i * AHEAD + v
                row = sp.value_load(slot_row_i[0:1, bass.ds(n, 1)], min_val=0, max_val=(EXPERTS + 1) * T_ALL - P)
                expert = sp.value_load(slot_expert_i[0:1, bass.ds(n, 1)], min_val=0, max_val=EXPERTS - 1)
                if after_pair(i):
                    sp.wait_ge(s_scatter[v], i * 16)
                sp.dma_start(xs[v][:, :], dispatched[bass.ds(row, P), :]).then_inc(s_xs[v], 16)
                if after_pair(i) or v >= W_AHEAD:
                    sp.wait_ge(s_h_ps, (n - W_AHEAD) * 2 + 2)
                sp.dma_start(w1[v % W_AHEAD], moe["w1"][bass.ds(expert, 1)].rearrange("o d f -> d (o f)")).then_inc(s_w1[v % W_AHEAD], 16)

            slots(sp, (load, 0))

            for v in range(AHEAD):
                sp.wait_ge(s_scatter[v], 16 * ROUNDS)
            for q in range(TAIL):
                for c in range(TOPK):
                    src = results[c * T_ALL + q * TN * P:c * T_ALL + (q + 1) * TN * P, :]
                    sp.dma_start(yy[c][:, TN * q:TN * q + TN, :], src.rearrange("(b p) d -> p b d", p=P)).then_inc(s_yy[q], 16)
            for q in range(TAIL):
                sp.wait_ge(s_o3, TN * (q + 1))
                sp.dma_start(out[TN * q:TN * q + TN].rearrange("b p d -> p b d"), o3[:, TN * q:TN * q + TN, :]).then_inc(s_out, 16)
            sp.wait_ge(s_out, 16 * TAIL)

        @block.tensor
        def _(pe):
            held = {}

            def take(b):
                for made, value in held.get(b, ()):
                    pe.wait_ge(made, value)

            def give(b, made, value, *others):
                held[b] = ((made, value),) + others

            def turn(k, p, u):
                if k.causal:
                    pe.wait_ge(k.s_ld, p * 16 + 16)
                else:
                    pe.wait_ge(SA.s_x1, p * 2 + 2)
                src = k.xin if k.causal else SA.x1
                take(home[k, "turn", u][0])
                for v in range(2):
                    ins = pe.transpose(bank[home[k, "turn", u][0]][:, P * v:P * v + P], src[:, v, :], ident)
                ins.then_inc(k.s_xt_ps, 1)
                give(home[k, "turn", u][0], k.s_xt, p + 1)
                if not k.causal:
                    pe.wait_ge(k.s_ld, p * 16 + 16)
                    take(home[k, "turn", u][1])
                    for v in range(2):
                        ins = pe.transpose(bank[home[k, "turn", u][1]][:, SC * v:SC * v + SC], k.cin[:, v, :], ident[0:SC, 0:SC])
                    ins.then_inc(k.s_ct_ps, 1)
                    give(home[k, "turn", u][1], k.s_ct, p + 1)

            def project(k, p, u):
                if not after_pair(p):
                    pe.wait_ge(k.s_const, 32)
                pe.wait_ge(k.s_xt, p + 1)
                take(home[k, "project", u][0])
                pe.matmul(bank[home[k, "project", u][0]][:, 0:2 * P], k.wq[:, :], k.xT[:, :], start=True, stop=True).then_inc(k.s_c_ps, 1)
                give(home[k, "project", u][0], k.s_lo, p * 2 + 1)
                if not k.causal:
                    pe.wait_ge(k.s_ct, p + 1)
                take(home[k, "project", u][1])
                src = k.xT if k.causal else k.cT
                pe.matmul(bank[home[k, "project", u][1]][:, 0:2 * k.keys], k.wk[:, :], src[:, :], start=True, stop=True).then_inc(k.s_c_ps, 1)
                give(home[k, "project", u][1], k.s_lo, p * 2 + 2)

            def spread_terms(k, p, u):
                if not after_pair(p):
                    pe.wait_ge(s_setup, SETUP)
                for b, hi, lo, h, l, s, done, n in (
                        (home[k, "spread_terms", u][0], "hq", "lq", k.hq, k.lq, k.s_rq_ps, k.s_qu, 1),
                        (home[k, "spread_terms", u][1], "hk", "lk", k.hk, k.lk, k.s_rk_ps, k.s_ku, 2)):
                    pe.wait_ge(k.s_lo, p * 2 + n)
                    take(b)
                    for g in (2 * u, 2 * u + 1):
                        dst = bank[b][:, 2 * P * (g % 2):2 * P * (g % 2) + 2 * P]
                        pe.matmul(dst, spread[hi][:, g].rearrange("c j t d -> c (j t d)"), h[:, :], start=True, stop=False)
                        ins = pe.matmul(dst, spread[lo][:, g].rearrange("c j t d -> c (j t d)"), l[:, :], start=False, stop=True)
                    ins.then_inc(s, 1)
                    give(b, done, p * 2 + u + 1)

            def values(k, p, u):
                src = k.xT if k.causal else k.cT
                take(home[k, "values", u][0])
                for v in range(2):
                    ins = pe.matmul(bank[home[k, "values", u][0]][0:k.keys, P * v:P * v + P], src[:, k.keys * v:k.keys * v + k.keys], k.wv[:, :], start=True, stop=True)
                ins.then_inc(k.s_v_ps, 1)
                give(home[k, "values", u][0], k.s_vo, p + 1)

            def scores(k, p, part):
                u, half = divmod(part, 2)
                if part == 0:
                    pe.wait_ge(k.s_bdk, p * 64 + 64)
                    pe.wait_ge(k.s_qu, p * 2 + 2)
                for g in (2 * half, 2 * half + 1):
                    b = home[k, "scores", u][g % 2]
                    take(b)
                    dst = bank[b][:, :].rearrange("q (j n) -> q j n", j=J)[:, :, 0:k.kpad]
                    if k.causal:
                        pe.matmul(dst, ident_bf[:, :], causal_bf[:, :].rearrange("q (o n) -> q o n", o=1).to_broadcast([P, J, P]), start=True, stop=False)
                    pe.matmul(dst, k.qu[:, g, P * u:P * u + P], k.km[:, g, :, k.keys * u:k.keys * u + k.kpad],
                              start=not k.causal, stop=True).then_inc(k.s_s1_ps, 1)
                    give(b, k.s_nm, p * 8 + 4 * u + g + 1)

            def shift(k, p, u):
                pe.wait_ge(k.s_mm, p * 2 + u + 1)
                take(home[k, "shift", u][0])
                pe.transpose(bank[home[k, "shift", u][0]][:, 0:P], k.mm[:, u].rearrange("q j r -> q (j r)").bitcast(F32), ident).then_inc(k.s_mt_ps, 1)
                give(home[k, "shift", u][0], k.s_sha, p * 8 + 4 * u + 4)

            def weights(k, p, part):
                u, half = divmod(part, 2)
                pe.wait_ge(k.s_sha, p * 8 + 4 * u + 4)
                if part == 0:
                    pe.wait_ge(k.s_bdq, p * 64 + 64)
                    pe.wait_ge(k.s_ku, p * 2 + 2)
                for g in (2 * half, 2 * half + 1):
                    b = home[k, "weights", u][g % 2]
                    take(b)
                    pe.matmul(bank[b][0:k.keys, :], k.ku[:, g, k.keys * u:k.keys * u + k.keys], k.qm[:, g, :, P * u:P * u + P],
                              start=True, stop=True).then_inc(k.s_s2_ps, 1)
                    give(b, k.s_ex, p * 8 + 4 * u + g + 1)

            def mix(k, p, part):
                u, half = divmod(part, 2)
                if part == 0:
                    pe.wait_ge(k.s_vo, p + 1)
                for g in (2 * half, 2 * half + 1):
                    b = home[k, "mix", u][g // 2]
                    pe.wait_ge(k.s_pm if k.causal else k.s_ex, p * 8 + 4 * u + g + 1)
                    if g % 2 == 0:
                        take(b)
                    ins = pe.matmul(bank[b][64 * (g % 2):64 * (g % 2) + 64, :], k.vo[:, u, g, :], k.pt[u][:, 512 * g:512 * g + 512], start=True, stop=True)
                    if g % 2:
                        ins.then_inc(k.s_u_ps, 1)
                        give(b, k.s_us, p * 4 + 2 * u + g // 2 + 1)

            def restore(k, p, part):
                u, h = divmod(part, 2)
                b = home[k, "mix", u][h]
                take(b)
                pe.wait_ge(k.s_us, p * 4 + 2 * u + h + 1)
                for j in range(J):
                    ins = pe.transpose(bank[b][:, P * j:P * j + P], k.us[u][:, h, P * j:P * j + P], ident)
                ins.then_inc(k.s_t_ps, 1)
                give(b, k.s_on, p * 4 + 2 * u + h + 1)

            def turn_heads(k, p, u):
                pe.wait_ge(k.s_on, p * 4 + 2 * u + 2)
                take(home[k, "turn_heads", u][0])
                pe.transpose(bank[home[k, "turn_heads", u][0]][:, 0:P], k.on[:, u, :], ident).then_inc(k.s_ot_ps, 1)
                give(home[k, "turn_heads", u][0], k.s_ot, p * 2 + u + 1)

            def norm(k, p, u):
                pe.wait_ge(k.s_ot, p * 2 + u + 1)
                take(home[k, "norm", u][0])
                pe.matmul(bank[home[k, "norm", u][0]][:, 0:D], k.oT[:, u, :], k.wo[:, :], start=True, stop=True).then_inc(k.s_w_ps, 1)
                give(home[k, "norm", u][0], k.s_y, p * 2 + u + 1)

            def route(k, p, u):
                if not after_pair(p):
                    pe.wait_ge(s_late, 64)
                pe.wait_ge(CA.s_x1, p * 2 + 2)
                take(home[k, "route", u][0])
                for v in range(2):
                    ins = pe.transpose(bank[home[k, "route", u][0]][:, P * v:P * v + P], CA.x1[:, v, :], ident)
                ins.then_inc(r.s_xt_ps, 1)
                give(home[k, "route", u][0], r.s_xT, p + 1)
                pe.wait_ge(r.s_xT, p + 1)
                take(home[k, "route", u][1])
                for v in range(2):
                    ins = pe.matmul(bank[home[k, "route", u][1]][:, EXPERTS * v:EXPERTS * v + EXPERTS], r.xT[:, P * v:P * v + P], rw[:, :], start=True, stop=True)
                ins.then_inc(r.s_lg_ps, 1)
                give(home[k, "route", u][1], r.s_rt, p * ROUTER_OPS + 1)

            def place(k, p, u):
                pe.wait_ge(r.s_rt, p * ROUTER_OPS + SELECTED)
                take(home[k, "place", u][0])
                dst = bank[home[k, "place", u][0]][:, 0:2 * EXPERTS]
                pe.matmul(dst, triangle_bf[:, :], r.sel[:, :, :].rearrange("q v e -> q (v e)"), start=True, stop=False)
                ins = pe.matmul(dst, ones_bf[:, :], r.acc[:, :, :].rearrange("q v e -> q (v e)"), start=False, stop=True)
                ins.then_inc(r.s_rank_ps, 1)
                give(home[k, "place", u][0], r.s_rt, p * ROUTER_OPS + SELECTED + 6)

            pe.wait_ge(s_const, 16)
            iterations({"route": route, "place": place, "turn": turn, "project": project, "spread_terms": spread_terms, "values": values, "scores": scores, "shift": shift, "weights": weights, "mix": mix, "restore": restore, "turn_heads": turn_heads, "norm": norm})

            pe.wait_ge(r.s_rt, PAIRS * ROUTER_OPS)
            take(DVE_BANK)
            pe.matmul(bank[DVE_BANK][:, 0:EXPERTS], ones_bf[:, :], r.acc[:, 0, :], start=True, stop=True).then_inc(s_counts, 1)

            pe.wait_ge(s_weights, 16 * (EXPERTS + 1))
            take(ACT_BANK)
            pe.transpose(bank[ACT_BANK][:, 0:EXPERTS * FC], b1_rows[:, :], ident[0:EXPERTS * FC, 0:EXPERTS * FC]).then_inc(s_b1, 1)
            pe.wait_ge(s_b1, 2)
            pe.wait_ge(s_table, TABLE_OPS)

            def turn_rows(i, v):
                n, b = i * AHEAD + v, v % 2
                pe.wait_ge(s_xs[v], i * 16 + 16)
                pe.wait_ge(s_xst, n - 1) if after_pair(i) or v >= 2 else None
                pe.transpose(bank[6 + b][:, 0:P], xs[v][:, 0:P], ident).then_inc(s_xst_ps, 1)

            def hidden(i, v):
                n, b = i * AHEAD + v, v % 2
                pe.wait_ge(s_xst, n + 1)
                pe.wait_ge(s_w1[v % W_AHEAD], (i * (AHEAD // W_AHEAD) + v // W_AHEAD + 1) * 16)
                for c in range(FC):
                    if (after_pair(i) or v >= 2) and c % 2 == 0:
                        pe.wait_ge(s_gelu, (n - 2) * 4 + c + 2)
                    ins = pe.matmul(bank[2 * b + c // 2][:, P * (c % 2):P * (c % 2) + P], w1[v % W_AHEAD][:, P * c:P * c + P], xsT[b][:, :], start=True, stop=True)
                    if c % 2:
                        ins.then_inc(s_h_ps, 1)

            def output(i, v):
                n, b = i * AHEAD + v, v % 2
                expert = pe.value_load(slot_expert_i[0:1, bass.ds(n, 1)], min_val=0, max_val=EXPERTS - 1)
                if after_pair(i) or v >= 2:
                    pe.wait_ge(s_yb, n - 1)
                for c in range(FC):
                    pe.wait_ge(s_gelu, n * 4 + c + 1)
                    ins = pe.matmul(bank[4 + b][:, 0:D], hid[b][:, c, :], w2[:, bass.ds(expert, 1), c, :].rearrange("f o d -> f (o d)"), start=(c == 0), stop=(c == FC - 1))
                ins.then_inc(s_o_ps, 1)

            slots(pe, (turn_rows, 2), (hidden, 1), (output, 0))

        @block.scalar
        def _(act):

            def turn(k, p, u):
                act.wait_ge(k.s_xt_ps, p + 1)
                if after_pair(p):
                    act.wait_ge(k.s_v_ps, p) if k.causal else act.wait_ge(k.s_c_ps, p * 2)
                act.copy(k.xT[:, :], bank[home[k, "turn", u][0]][:, 0:2 * P]).then_inc(k.s_xt, 1)
                if not k.causal:
                    act.wait_ge(k.s_ct_ps, p + 1)
                    if after_pair(p):
                        act.wait_ge(k.s_v_ps, p)
                    act.copy(k.cT[:, :], bank[home[k, "turn", u][1]][:, 0:2 * SC]).then_inc(k.s_ct, 1)

            def project(k, p, u):
                act.wait_ge(k.s_c_ps, p * 2 + 1)
                if after_pair(p):
                    act.wait_ge(k.s_rq_ps, p * 2)
                act.activation(k.hq[:, :], bank[home[k, "project", u][0]][:, 0:2 * P], ACT.Identity, bias=k.bq[:, :]).then_inc(k.s_hi, 1)
                act.wait_ge(k.s_c_ps, p * 2 + 2)
                if after_pair(p):
                    act.wait_ge(k.s_rk_ps, p * 2)
                n = 2 * k.keys
                act.activation(k.hk[:, 0:n], bank[home[k, "project", u][1]][:, 0:n], ACT.Identity, bias=k.bk[:, :]).then_inc(k.s_hi, 1)

            def spread_terms(k, p, u):
                act.wait_ge(k.s_rq_ps, p * 2 + u + 1)
                if after_pair(p):
                    act.wait_ge(k.s_s1_ps, p * 8)
                    act.wait_ge(k.s_bdq, p * 64)
                act.copy(k.qu[:, 2 * u:2 * u + 2, :].rearrange("r g n -> r (g n)"), bank[home[k, "spread_terms", u][0]][:, :]).then_inc(k.s_qu, 1)

            def shift(k, p, u):
                if not after_pair(p):
                    act.wait_ge(k.s_zero, 2)
                act.wait_ge(k.s_mt_ps, p * 2 + u + 1)
                if after_pair(p):
                    act.wait_ge(k.s_s2_ps, (p - 1) * 8 + 4 * u + 4)
                for j in range(J):
                    rows = slice(32 * j, 32 * j + 8)
                    src = bank[home[k, "shift", u][0]][rows, 0:P].rearrange("r (o n) -> r o n", o=1).to_broadcast([8, GROUPS, P])
                    act.copy(k.qm[rows, :, j, P * u:P * u + P], src).then_inc(k.s_sha, 1)

            def weights(k, p, part):
                u, half = divmod(part, 2)
                for g in (2 * half, 2 * half + 1):
                    act.wait_ge(k.s_s2_ps, p * 8 + 4 * u + g + 1)
                    if after_pair(p) and g % 2 == 0:
                        act.wait_ge(k.s_u_ps, (p - 1) * 4 + 2 * u + g // 2 + 1)
                    act.activation(k.pt[u][:, 512 * g:512 * g + 512], bank[home[k, "weights", u][g % 2]][0:k.keys, :], ACT.Exp, scale=SCALE).then_inc(k.s_ex, 1)

            def mix(k, p, part):
                u, h = divmod(part, 2)
                act.wait_ge(k.s_u_ps, p * 4 + 2 * u + h + 1)
                if after_pair(p):
                    act.wait_ge(k.s_t_ps, (p - 1) * 4 + 2 * u + h + 1)
                act.copy(k.us[u][:, h, :], bank[home[k, "mix", u][h]][:, :]).then_inc(k.s_us, 1)

            def turn_heads(k, p, u):
                act.wait_ge(k.s_ot_ps, p * 2 + u + 1)
                if after_pair(p):
                    act.wait_ge(k.s_w_ps, (p - 1) * 2 + u + 1)
                act.copy(k.oT[:, u, :], bank[home[k, "turn_heads", u][0]][:, 0:P]).then_inc(k.s_ot, 1)

            def route(k, p, u):
                act.wait_ge(r.s_xt_ps, p + 1)
                if after_pair(p):
                    act.wait_ge(r.s_lg_ps, p)
                act.copy(r.xT[:, :], bank[home[k, "route", u][0]][:, 0:2 * P]).then_inc(r.s_xT, 1)
                act.wait_ge(CA.s_x1, p * 2 + 2)
                if after_pair(p):
                    act.wait_ge(r.s_disp, p * 64)
                act.copy(r.sent[:, :, :, 0:D], CA.x1[:, :, :].rearrange("q v (o d) -> q v o d", o=1).to_broadcast([P, 2, TOPK, D])).then_inc(r.s_xe1, 1)

            def gate(k, p, u):
                act.wait_ge(r.s_rt, p * ROUTER_OPS + 3)
                act.activation(r.exl[:, :, :], r.ls[:, :, :], ACT.Exp).then_inc(r.s_exp, 1)

            def second(k, p, u):
                act.wait_ge(r.s_rt, p * ROUTER_OPS + SELECTED + 1)
                act.activation(r.ed[:, :], r.d[:, :], ACT.Exp).then_inc(r.s_exp, 1)

            iterations({"route": route, "gate": gate, "second": second, "turn": turn, "project": project, "spread_terms": spread_terms, "shift": shift, "weights": weights, "mix": mix, "turn_heads": turn_heads})

            act.wait_ge(s_pool_setup, 1)
            act.activation(warm[:, :], half[:, :], ACT.Gelu).then_inc(s_warm, 1)
            act.wait_ge(s_b1, 1)
            act.copy(b1[:, :], bank[ACT_BANK][:, 0:EXPERTS * FC]).then_inc(s_b1, 1)
            act.wait_ge(s_b1, 2)
            act.wait_ge(s_table, TABLE_OPS)

            def activate(i, v):
                n, b = i * AHEAD + v, v % 2
                expert = act.value_load(slot_expert_i[0:1, bass.ds(n, 1)], min_val=0, max_val=EXPERTS - 1)
                for c in range(FC):
                    if c % 2 == 0:
                        act.wait_ge(s_h_ps, n * 2 + c // 2 + 1)
                    if (after_pair(i) or v >= 2) and c == 0:
                        act.wait_ge(s_o_ps, n - 1)
                    act.activation(hid[b][:, c, :], bank[2 * b + c // 2][:, P * (c % 2):P * (c % 2) + P], ACT.Gelu,
                                   bias=b1[:, bass.ds(expert * FC + c, 1)]).then_inc(s_gelu, 1)

            slots(act, (activate, 0))

            for q in range(TAIL):
                act.wait_ge(s_off3, q + 1)
                act.wait_ge(s_rs3, q + 1)
                act.wait_ge(s_y3, q + 1)
                for b in range(TN * q, TN * q + TN):
                    act.activation(y3[:, b, :], y3[:, b, :], ACT.Identity, bias=off3[:, b:b + 1], scale=rs3[:, b:b + 1]).then_inc(s_xn3, 1)

        @block.vector
        def _(dve):
            dve.memset(ones_bf[:, :], 1.0).then_inc(s_pool_ones, 1)
            dve.memset(filler[:, :, :], 1.0).then_inc(s_fill, 1)
            dve.memset(r.acc[:, :, :], 0.0).then_inc(s_pool_ones, 1)
            n_setup = [0]

            def setup(ins):
                n_setup[0] += 1
                ins.then_inc(s_setup, 1)

            for k in KINDS:
                setup(dve.memset(k.vo[:, :, :, 32:64], 1.0))
                setup(dve.memset(k.mm[:, :, :, :].bitcast(F32), 0.0))
            setup(dve.memset(CA.hk[:, 2 * SC:].bitcast(F32), 0.0))
            setup(dve.memset(CA.lk[:, 2 * SC:].bitcast(F32), 0.0))
            zeroed = n_setup[0]
            for n in spread:
                dve.memset(spread[n][:, :, :, :, :].bitcast(F32), 0.0).then_inc(s_spread0, 1)
            dve.wait_ge(s_spread0, 4)
            dve.wait_ge(s_const, 16)
            for n, terms in (("hq", (1, 2)), ("lq", (3,)), ("hk", (1, 3)), ("lk", (2,))):
                for t in terms:
                    setup(dve.tensor_copy(spread[n][:, :, :, t, :], ident.rearrange("c (g j d) -> c g j d", g=GROUPS, j=J)))
            setup(dve.tensor_copy(ident_bf[:, :], ident))
            setup(dve.tensor_copy(causal_bf[:, :], cst[:, P:2 * P]))
            setup(dve.tensor_copy(triangle_bf[:, :], cst[:, 2 * P:3 * P]))
            assert n_setup[0] == SETUP, n_setup[0]

            def project(k, p, u):
                for n, (b, bias, h, l, w, s) in enumerate(((home[k, "project", u][0], k.bq, k.hq, k.lq, 2 * P, k.s_rq_ps), (home[k, "project", u][1], k.bk, k.hk, k.lk, 2 * k.keys, k.s_rk_ps))):
                    dve.wait_ge(k.s_hi, p * 2 + n + 1)
                    if after_pair(p):
                        dve.wait_ge(s, p * 2)
                    dve.scalar_tensor_tensor(out=l[:, 0:w], in0=bank[b][:, 0:w], scalar=bias[:, :], in1=h[:, 0:w].bitcast(F32),
                                             op0=ALU.add, op1=ALU.subtract).then_inc(k.s_lo, 1)

            def spread_terms(k, p, u):
                dve.wait_ge(k.s_rk_ps, p * 2 + u + 1)
                if after_pair(p):
                    dve.wait_ge(k.s_s2_ps, p * 8)
                    dve.wait_ge(k.s_bdk, p * 64)
                n = 2 * k.keys
                dve.tensor_tensor(k.ku[:, 2 * u:2 * u + 2, :], bank[home[k, "spread_terms", u][1]][:, :].rearrange("r (g n) -> r g n", g=2)[:, :, 0:n],
                                  kones[:, 2 * u:2 * u + 2].rearrange("r (g o) -> r g o", o=1).to_broadcast([P, 2, n]), ALU.add).then_inc(k.s_ku, 1)

            def values(k, p, u):
                dve.wait_ge(k.s_v_ps, p + 1)
                if after_pair(p):
                    dve.wait_ge(k.s_u_ps, p * 4)
                for_all = k.bv[0:k.keys, :].rearrange("n (o g c) -> n o g c", o=1, g=GROUPS).to_broadcast([k.keys, 2, GROUPS, 32])
                dve.tensor_tensor(k.vo[:, :, :, 0:32], bank[home[k, "values", u][0]][0:k.keys, 0:2 * P].rearrange("n (b g c) -> n b g c", b=2, g=GROUPS),
                                  for_all, ALU.add).then_inc(k.s_vo, 1)

            def scores(k, p, part):
                u, half = divmod(part, 2)
                if after_pair(p) and half == 0:
                    dve.wait_ge(k.s_mm, (p - 1) * 2 + u + 1)
                for g in (2 * half, 2 * half + 1):
                    dve.wait_ge(k.s_s1_ps, p * 8 + 4 * u + g + 1)
                    dve.tensor_reduce(k.nm[:, u, g, :], bank[home[k, "scores", u][g % 2]][:, :].rearrange("q (j n) -> q j n", j=J)[:, :, 0:k.keys],
                                      AX.X, ALU.max, negate=True).then_inc(k.s_nm, 1)

            def shift(k, p, u):
                if after_pair(p):
                    dve.wait_ge(k.s_mt_ps, (p - 1) * 2 + u + 1)
                dve.wait_ge(k.s_nm, p * 8 + 4 * u + 4)
                nm = k.nm[:, u].rearrange("q g j -> q j g")
                dve.tensor_copy(k.mm[:, u, :, 0:4], nm).then_inc(k.s_mmh, 1)
                dve.wait_ge(k.s_mmh, p * 2 + u + 1)
                dve.tensor_tensor(k.mm[:, u, :, 4:8], nm, k.mm[:, u, :, 0:4].bitcast(F32), ALU.subtract).then_inc(k.s_mm, 1)

            def restore(k, p, part):
                u, half = divmod(part, 2)
                if after_pair(p) and half == 0:
                    dve.wait_ge(k.s_on, (p - 1) * 4 + 2 * u + 2)
                    dve.wait_ge(k.s_ot_ps, (p - 1) * 2 + u + 1)
                h = half
                dve.wait_ge(k.s_t_ps, p * 4 + 2 * u + h + 1)
                t = bank[home[k, "mix", u][h]][:, :]
                sums = t.rearrange("q (j s r) -> q s j r", j=J, s=2)[:, :, :, 32]
                dve.reciprocal(k.rd[:, u, h], sums).then_inc(k.s_rd, 1)
                dve.wait_ge(k.s_rd, p * 4 + 2 * u + h + 1)
                vals = bass.AP(t.tensor, t.offset, [list(t.ap[0]), [64, 2], [P + HD, J], [1, HD]])
                dve.tensor_tensor(k.on[:, u, 64 * h:64 * h + 64].rearrange("q (s j d) -> q s j d", s=2, j=J), vals,
                                  k.rd[:, u, h].rearrange("q s (j o) -> q s j o", o=1).to_broadcast([P, 2, J, HD]), ALU.mult).then_inc(k.s_on, 1)

            def norm(k, p, u):
                n = p * 2 + u + 1
                dve.wait_ge(k.s_w_ps, n)
                if not k.causal:
                    dve.wait_ge(SA.s_xr, n)
                elif not after_pair(p):
                    dve.wait_ge(s_pool_setup, 4)
                if after_pair(p):
                    dve.wait_ge(k.s_xn, n - 2)
                dve.tensor_tensor(k.y[:, u, :], bank[home[k, "norm", u][0]][:, 0:D], residual[:, bass.ds(p * 2 + u, 1), :].rearrange("q o d -> q (o d)"), ALU.add).then_inc(k.s_y, 1)
                dve.wait_ge(k.s_y, n)
                dve.bn_stats(k.bs[:, u, :], k.y[:, u, :]).then_inc(k.s_bs, 1)
                dve.wait_ge(k.s_bs, n)
                if after_pair(p):
                    dve.wait_ge(k.s_ve, n - 2)
                dve.bn_aggr(k.ba[:, u, :], k.bs[:, u, :]).then_inc(k.s_ba, 1)
                dve.wait_ge(k.s_ba, n)
                dve.scalar_tensor_tensor(out=k.xn[:, u, :], in0=k.y[:, u, :], scalar=k.ba[:, u, 0:1], in1=k.g, op0=ALU.subtract, op1=ALU.mult).then_inc(k.s_xn, 1)
                dve.wait_ge(k.s_xn, n)
                dve.wait_ge(k.s_rs, n)
                if after_pair(p):
                    dve.wait_ge(CA.s_xt_ps, p) if k.causal else dve.wait_ge(r.s_xt_ps, p)
                    if not k.causal:
                        dve.wait_ge(r.s_xe1, p)
                    dve.wait_ge(k.s_xr, n - 2)
                dve.scalar_tensor_tensor(out=k.x1[:, u, :], in0=k.xn[:, u, :], scalar=k.rs[:, u:u + 1], in1=k.b, op0=ALU.mult, op1=ALU.add).then_inc(k.s_x1, 1)

            done = [0]

            def routed(p, ins):
                done[0] = done[0] % ROUTER_OPS + 1
                ins.then_inc(r.s_rt, 1)
                dve.wait_ge(r.s_rt, p * ROUTER_OPS + done[0])

            def wide(t):
                return t[:, :].rearrange("q (v o) -> q v o", o=1).to_broadcast([P, 2, EXPERTS])

            def each(t):
                return t.rearrange("q (o e) -> q o e", o=1).to_broadcast([P, 2, EXPERTS])

            def gate(k, p, u):
                if not after_pair(p):
                    dve.wait_ge(s_late, 64)
                dve.wait_ge(r.s_lg_ps, p + 1)
                if after_pair(p):
                    dve.wait_ge(r.s_disp, p * 64)
                    dve.wait_ge(r.s_rank_ps, p)
                routed(p, dve.tensor_tensor(r.lg[:, :, :], bank[home[k, "route", u][1]][:, 0:2 * EXPERTS].rearrange("q (v e) -> q v e", v=2), each(rb), ALU.add))
                routed(p, dve.tensor_reduce(r.nmx[:, :], r.lg[:, :, :], AX.X, ALU.max, negate=True))
                routed(p, dve.tensor_tensor(r.ls[:, :, :], r.lg[:, :, :], wide(r.nmx), ALU.add))

            def largest(p, prob, best, eq, key, km, oh):
                routed(p, dve.tensor_reduce(best[:, :], prob[:, :, :], AX.X, ALU.max))
                routed(p, dve.tensor_tensor(eq[:, :, :], prob[:, :, :], wide(best), ALU.is_equal))
                routed(p, dve.tensor_tensor(key[:, :, :], eq[:, :, :], each(falling), ALU.mult))
                routed(p, dve.tensor_reduce(km[:, :], key[:, :, :], AX.X, ALU.max))
                routed(p, dve.tensor_tensor(oh[:, :, :], each(falling), wide(km), ALU.is_equal))

            def choose(k, p, u):
                dve.wait_ge(r.s_exp, p * 2 + 1)
                routed(p, dve.tensor_reduce(r.sm[:, :], r.exl[:, :, :], AX.X, ALU.add))
                routed(p, dve.reciprocal(r.rsm[:, :], r.sm[:, :]))
                routed(p, dve.tensor_tensor(r.p[:, :, :], r.exl[:, :, :], wide(r.rsm), ALU.mult))
                largest(p, r.p, r.p1, r.eq, r.key, r.km, r.oh1)

            def second(k, p, u):
                routed(p, dve.scalar_tensor_tensor(out=r.pm[:, :, :], in0=r.oh1[:, :, :], scalar=-2.0, in1=r.p[:, :, :], op0=ALU.mult, op1=ALU.add))
                largest(p, r.pm, r.p2, r.eq2, r.key2, r.km2, r.oh2)
                routed(p, dve.tensor_tensor(r.sel[:, :, :], r.oh1[:, :, :], r.oh2[:, :, :], ALU.add))
                routed(p, dve.tensor_tensor(r.acc[:, 1, :], r.acc[:, 0, :], r.sel[:, 0, :], ALU.add))
                assert done[0] == SELECTED, done[0]
                routed(p, dve.tensor_tensor(r.d[:, :], r.p2[:, :], r.p1[:, :], ALU.subtract))

            def place(k, p, u):
                dve.wait_ge(r.s_exp, p * 2 + 2)
                routed(p, dve.tensor_scalar(r.den[:, :], r.ed[:, :], 1.0, None, ALU.add))
                routed(p, dve.reciprocal(r.w1[:, :], r.den[:, :]))
                tile = lambda c, col: r.sent[:, :, c, col]
                routed(p, dve.tensor_tensor(tile(1, ROW - 1), r.ed[:, :], r.w1[:, :], ALU.mult))
                routed(p, dve.tensor_copy(tile(0, ROW - 1), r.w1[:, :]))

            def number(k, p, u):
                dve.wait_ge(r.s_rank_ps, p + 1)
                routed(p, dve.tensor_tensor(r.base[:, :, :], bank[home[k, "place", u][0]][:, 0:2 * EXPERTS].rearrange("q (v e) -> q v e", v=2), each(region), ALU.add))
                assert done[0] == SELECTED + 6, done[0]
                routed(p, dve.tensor_tensor(r.t1[:, :, :], r.base[:, :, :], r.oh1[:, :, :], ALU.mult))
                routed(p, dve.tensor_tensor(r.t2[:, :, :], r.base[:, :, :], r.oh2[:, :, :], ALU.mult))
                routed(p, dve.tensor_reduce(r.pos[:, 0, :], r.t1[:, :, :], AX.X, ALU.add))
                routed(p, dve.tensor_reduce(r.pos[:, 1, :], r.t2[:, :, :], AX.X, ALU.add))
                routed(p, dve.tensor_tensor(r.acc[:, 0, :], r.acc[:, 1, :], r.sel[:, 1, :], ALU.add))
                routed(p, dve.tensor_copy(r.row[:, :, :], r.pos[:, :, :].rearrange("q c v -> q v c")))
                routed(p, dve.tensor_copy(r.sent[:, :, :, P].bitcast(I32), rows_sb[:, bass.ds(p * 2, 2), :]))
                assert done[0] == ROUTER_OPS, done[0]

            dve.wait_ge(s_pool_ones, 2)
            dve.wait_ge(s_setup, SETUP)
            iterations({"gate": gate, "choose": choose, "second": second, "place": place, "number": number, "project": project, "spread_terms": spread_terms, "values": values, "scores": scores, "shift": shift, "restore": restore, "norm": norm})

            tables = [0]

            def listed(ins):
                tables[0] += 1
                ins.then_inc(s_table, 1)
                dve.wait_ge(s_table, tables[0])

            row0 = lambda t, a, b, inner=True: (t.rearrange("q (o n) -> q o n", o=1) if inner else t.rearrange("q (n o) -> q n o", o=1)).to_broadcast([1, a, b])
            dve.wait_ge(s_counts, 1)
            listed(dve.tensor_copy(tb.count[:, :], bank[DVE_BANK][0:1, 0:EXPERTS]))
            listed(dve.tensor_tensor(tb.full[:, :, :], row0(tb.count[:, :], EXPERTS, T_ALL // P, False), row0(tile_starts[0:1], EXPERTS, T_ALL // P), ALU.is_gt))
            listed(dve.tensor_reduce(tb.tiles[:, :], tb.full[:, :, :], AX.X, ALU.add))
            listed(dve.tensor_tensor(tb.before[:, :, :], row0(tb.tiles[:, :], E9, EXPERTS), below[0:1].rearrange("q (a b) -> q a b", a=E9), ALU.mult))
            listed(dve.tensor_reduce(tb.first[:, :], tb.before[:, :, :], AX.X, ALU.add))
            listed(dve.tensor_tensor(tb.past[:, :, :], row0(slot_no[0:1], SLOTS, EXPERTS, False), row0(tb.first[:, 1:E9], SLOTS, EXPERTS), ALU.is_ge))
            listed(dve.tensor_reduce(tb.expert[:, :], tb.past[:, :, :], AX.X, ALU.add))
            listed(dve.tensor_scalar(slot_expert_i[:, :], tb.expert[:, :], float(EXPERTS - 1), None, ALU.min))
            listed(dve.scalar_tensor_tensor(out=tb.shift[:, :], in0=tb.first[:, :], scalar=-float(P), in1=region9[0:1], op0=ALU.mult, op1=ALU.add))
            listed(dve.tensor_tensor(tb.one[:, :, :], row0(tb.expert[:, :], SLOTS, E9, False), row0(expert_no[0:1], SLOTS, E9), ALU.is_equal))
            listed(dve.tensor_tensor(tb.prod[:, :, :], tb.one[:, :, :], row0(tb.shift[:, :], SLOTS, E9), ALU.mult))
            listed(dve.tensor_reduce(tb.start[:, :], tb.prod[:, :, :], AX.X, ALU.add))
            listed(dve.tensor_tensor(slot_row_i[:, :], tb.start[:, :], slot_rows[0:1], ALU.add))
            assert tables[0] == TABLE_OPS

            dve.wait_ge(s_weights, 16 * (EXPERTS + 1))

            def turned(i, v):
                n, b = i * AHEAD + v, v % 2
                dve.wait_ge(s_xst_ps, n + 1)
                if after_pair(i) or v >= 2:
                    dve.wait_ge(s_h_ps, (n - 2) * 2 + 2)
                dve.tensor_copy(xsT[b][:, :], bank[6 + b][:, 0:P]).then_inc(s_xst, 1)

            def gated(i, v):
                n, b = i * AHEAD + v, v % 2
                expert = dve.value_load(slot_expert_i[0:1, bass.ds(n, 1)], min_val=0, max_val=EXPERTS - 1)
                dve.wait_ge(s_o_ps, n + 1)
                if after_pair(i) or v >= 2:
                    dve.wait_ge(s_ys, n - 1)
                if after_pair(i):
                    dve.wait_ge(s_scatter[v], i * 16)
                dve.tensor_tensor(yb[b][:, :], bank[4 + b][:, 0:D], b2[:, bass.ds(expert, 1), :].rearrange("q o d -> q (o d)"), ALU.add).then_inc(s_yb, 1)
                dve.wait_ge(s_yb, n + 1)
                dve.tensor_scalar(ys[v], yb[b][:, :], xs[v][:, ROW - 1:ROW], None, ALU.mult).then_inc(s_ys, 1)

            slots(dve, (turned, 2), (gated, 0))

            def add_and_measure(q):
                t = slice(TN * q, TN * q + TN)
                dve.wait_ge(s_yy[q], 32)
                dve.tensor_tensor(y3[:, t, :], yy[0][:, t, :], residual[:, t, :], ALU.add).then_inc(s_y3a, 1)
                dve.wait_ge(s_y3a, q + 1)
                dve.tensor_tensor(y3[:, t, :], y3[:, t, :], yy[1][:, t, :], ALU.add).then_inc(s_y3, 1)
                dve.wait_ge(s_y3, q + 1)
                for b in range(TN * q, TN * q + TN):
                    dve.bn_stats(bs3[:, b, :], y3[:, b, :]).then_inc(s_bs3, 1)
                for b in range(TN * q, TN * q + TN):
                    dve.wait_ge(s_bs3, b + 1)
                    dve.bn_aggr(ba3[:, b, :], bs3[:, b, :]).then_inc(s_ba3, 1)

            def offset(q):
                t = slice(TN * q, TN * q + TN)
                dve.wait_ge(s_ba3, TN * (q + 1))
                dve.wait_ge(s_rs3, q + 1)
                dve.scalar_tensor_tensor(out=off3[:, t], in0=ba3[:, t, 0], scalar=-1.0, in1=rs3[:, t], op0=ALU.mult, op1=ALU.mult).then_inc(s_off3, 1)

            def times_gamma(q):
                t = slice(TN * q, TN * q + TN)
                dve.wait_ge(s_xn3, TN * (q + 1))
                dve.tensor_tensor(y3[:, t, :], y3[:, t, :], g3[:, :].rearrange("q (o d) -> q o d", o=1).to_broadcast([P, TN, D]), ALU.mult).then_inc(s_g3, 1)

            for q in range(TAIL + 2):
                if q < TAIL:
                    add_and_measure(q)
                if 1 <= q <= TAIL:
                    offset(q - 1)
                if q >= 2:
                    times_gamma(q - 2)

        @block.gpsimd
        def _(pool):
            for k in KINDS:
                pool.memset(k.qm[:, :, :, :].bitcast(F32), 0.0).then_inc(k.s_zero, 1)
                pool.memset(k.km[:, :, :, :].bitcast(F32), 0.0).then_inc(k.s_zero, 1)
            pool.memset(half[:, :], -0.5).then_inc(s_pool_setup, 1)
            pool.wait_ge(SA.s_const, 32)
            pool.wait_ge(CA.s_const, 32)
            pool.wait_ge(s_residual, 16)
            pool.tensor_tensor(residual[:, :, :], residual[:, :, :], SA.bo[:, :].rearrange("p (o d) -> p o d", o=1).to_broadcast([P, B, D]), ALU.add).then_inc(s_pool_setup, 3)

            def weights(k, p, part):
                if not k.causal:
                    return
                u, half = divmod(part, 2)
                for g in (2 * half, 2 * half + 1):
                    n = p * 8 + 4 * u + g + 1
                    pool.wait_ge(k.s_ex, n)
                    blockg = k.pt[u][:, 512 * g:512 * g + 512]
                    pool.affine_select(out=blockg, in_=blockg, compare_op=ALU.is_ge, fill=0.0, base=0,
                                       pattern=[[0, J], [1, P]], channel_multiplier=-1).then_inc(k.s_pm, 1)

            def norm(k, p, u):
                n = p * 2 + u + 1
                pool.wait_ge(k.s_ba, n)
                if after_pair(p):
                    pool.wait_ge(k.s_x1, n - 2)
                pool.tensor_scalar(k.ve[:, u:u + 1], k.ba[:, u, 1:2], EPS, None, ALU.add).then_inc(k.s_ve, 1)
                pool.wait_ge(k.s_ve, n)
                pool.tensor_tensor(k.rs[:, u:u + 1], k.ve[:, u:u + 1], half[:, :], ALU.pow).then_inc(k.s_rs, 1)
                pool.wait_ge(k.s_x1, n)
                if k.causal:
                    pool.tensor_tensor(residual[:, bass.ds(p * 2 + u, 1), :].rearrange("q o d -> q (o d)"), k.x1[:, u, :], CA.bo[:, :], ALU.add).then_inc(k.s_xr, 1)
                else:
                    pool.tensor_copy(residual[:, bass.ds(p * 2 + u, 1), :].rearrange("q o d -> q (o d)"), k.x1[:, u, :]).then_inc(k.s_xr, 1)

            def number(k, p, u):
                pool.wait_ge(s_filled, p * 32 + 32)
                pool.wait_ge(r.s_rt, p * ROUTER_OPS + ROUTER_OPS)
                pool.wait_ge(r.s_xe1, p + 1)
                pool.wait_ge(CA.s_xr, p * 2 + 2)
                for v in range(2):
                    for c in range(TOPK):
                        pool.indirect_dma_start(out=dispatched, out_offset=bass.IndirectOffsetOnAxis(ap=r.row[:, v, c:c + 1], axis=0),
                                                in_=r.sent[:, v, c, :], in_offset=None).then_inc(r.s_disp, 16)

            iterations({"number": number, "weights": weights, "norm": norm})


            def scatter(i, v):
                pool.wait_ge(s_ys, i * AHEAD + v + 1)
                pool.indirect_dma_start(out=results, out_offset=bass.IndirectOffsetOnAxis(ap=xs[v][:, P:P + 1].bitcast(I32), axis=0),
                                        in_=ys[v], in_offset=None, bounds_check=TOPK * T_ALL - 1, oob_is_err=False).then_inc(s_scatter[v], 16)

            for i in range(ROUNDS):
                for v in range(AHEAD):
                    scatter(i, v)
            def deviation(q):
                pool.wait_ge(s_ba3, TN * (q + 1))
                t = slice(TN * q, TN * q + TN)
                pool.tensor_scalar(ve3[:, t], ba3[:, t, 1], EPS, None, ALU.add).then_inc(s_ve3, 1)
                pool.wait_ge(s_ve3, q + 1)
                pool.tensor_tensor(rs3[:, t], ve3[:, t], half[:, :].to_broadcast([P, TN]), ALU.pow).then_inc(s_rs3, 1)

            def plus_beta(q):
                t = slice(TN * q, TN * q + TN)
                pool.wait_ge(s_g3, q + 1)
                pool.tensor_tensor(o3[:, t, :], y3[:, t, :], beta3[:, :].rearrange("q (o d) -> q o d", o=1).to_broadcast([P, TN, D]), ALU.add).then_inc(s_o3, TN)

            for q in range(TAIL + 2):
                if q < TAIL:
                    deviation(q)
                if q >= 2:
                    plus_beta(q - 2)




def kernel(**inputs):
    import concourse.bacc as bacc
    from concourse.bass_utils import run_bass_kernel_spmd

    nc = bacc.Bacc("TRN2", target_bir_lowering=False, num_devices=1)
    arrays = {}

    def given(name, a):
        a = np.ascontiguousarray(a)
        arrays[f"in_{name}"] = a
        return nc.dram_tensor(f"in_{name}", a.shape, mybir.dt.from_np(a.dtype), kind="ExternalInput").ap()

    x, ctx = given("x", inputs["x"]), given("ctx", inputs["ctx_1024"])
    layer = lambda name: given(name, inputs["L0_xattn_" + name])

    def packed(a, norm):
        get = lambda n: inputs[f"L0_xattn_{n}"]
        columns = [get(f"{a}_{n}") for n in ("wq", "wk", "wv", "wo")] + [get(f"{a}_{n}")[:, None] for n in ("bq", "bk")]
        rows = [get(f"{a}_bv"), get(f"{a}_bo"), get(f"{norm}_g"), get(f"{norm}_b")]
        return {"square": given(f"{a}_square", np.concatenate(columns, axis=1)), "rows": given(f"{a}_rows", np.concatenate(rows))}

    sa, ca = (packed(a, l) for a, l in (("sa", "ln1"), ("ca", "ln2")))
    moe = dict(rw=layer("router_w"), w1=layer("e_w1"), b1=layer("e_b1"), w2=layer("e_w2"),
               rows=given("late_rows", np.concatenate([inputs["L0_xattn_" + n].ravel() for n in ("router_b", "e_b2", "ln3_g", "ln3_b")])))
    tokens = x.shape[0] * x.shape[1]
    consts = given("shape_constants", shape_constants())
    expert_consts = given("expert_constants", expert_constants(tokens, slot_count(tokens)))
    rows = given("result_rows", result_rows(x.shape[0]))
    out = nc.dram_tensor("out", x.shape, F32, kind="ExternalOutput").ap()
    build(nc, x, ctx, sa, ca, moe, out, consts, expert_consts, rows)
    return run_bass_kernel_spmd(nc, [arrays], core_ids=[0]).results[0]["out"]
```
